# Optimizing a Trainium2 kernel written in Bass

```python
import numpy as np
import jax
import jax.numpy as jnp

def _softmax(x, axis=-1):
    return jax.nn.softmax(x, axis=axis)
def _gelu(x):
    return jax.nn.gelu(x, approximate=True)
def _silu(x):
    return jax.nn.silu(x)
def _sigmoid(x):
    return jax.nn.sigmoid(x)
def _layernorm(x, axis=-1, eps=1e-5):
    m = jnp.mean(x, axis=axis, keepdims=True)
    v = jnp.var(x, axis=axis, keepdims=True)
    return (x - m) / jnp.sqrt(v + eps)
def _scatter_add(tgt, idx, src, axis=0):
    return tgt.at[idx].add(src)
def _segment_sum(src, seg, n):
    return jax.ops.segment_sum(src, seg, n)

kernel_name = 'mk_conv_seq_d4_conv_nchw64_44e166'

def setup_inputs(seed: int = 0):
    np.random.seed(seed)
    _w = jnp.asarray
    def _rec_inputs():
        import jax
        import jax.numpy as jnp
        _gk = jax.random.key(seed)
        x = -0.0005207 + 1.001 * jax.random.normal(jax.random.fold_in(_gk, 1), (8, 64, 64, 64), jnp.float32)
        return x
    x = _rec_inputs()
    def _L0_conv_setup():
        import jax, jax.numpy as jnp
        import numpy as np

        def _prelu(x, a):
            return jnp.where(x >= 0, x, a * x)

        def _conv1x1(x, w, b):
            return jnp.einsum('nchw,oc->nohw', x, w) + b[None, :, None, None]
        key = jax.random.key(seed)
        ks = jax.random.split(key, 7)
        N, C, H, W = (8, 64, 64, 64)
        red = 2
        c = C // red
        s = 1.0 / np.sqrt(C).astype(np.float32)
        x = jax.random.normal(ks[0], (N, C, H, W), dtype=jnp.float32)
        w1 = jax.random.normal(ks[1], (c, C), dtype=jnp.float32) * s
        b1 = jnp.zeros((c,), dtype=jnp.float32)
        w2 = jax.random.normal(ks[2], (c, C), dtype=jnp.float32) * s
        b2 = jnp.zeros((c,), dtype=jnp.float32)
        w3 = jax.random.normal(ks[3], (C, C), dtype=jnp.float32) * s
        b3 = jnp.zeros((C,), dtype=jnp.float32)
        a1 = jnp.full((1,), 0.25, dtype=jnp.float32)
        a2 = jnp.full((1,), 0.25, dtype=jnp.float32)
        a3 = jnp.full((1,), 0.25, dtype=jnp.float32)
        return {'x': x, 'w1': w1, 'b1': b1, 'a1': a1, 'w2': w2, 'b2': b2, 'a2': a2, 'w3': w3, 'b3': b3, 'a3': a3}
    _L0_conv_all = _L0_conv_setup()
    _L0_conv_in = {k: v for k, v in _L0_conv_all.items() if k in ('w1', 'b1', 'a1', 'w2', 'b2', 'a2', 'w3', 'b3', 'a3', )}
    del _L0_conv_all

    def _L1_conv_setup():
        import jax, jax.numpy as jnp
        import numpy as np
        key = jax.random.key(seed)
        ks = jax.random.split(key, 7)
        B, C, H, W = (4, 64, 64, 64)
        C8 = C // 8
        return {'x': jax.random.normal(ks[0], (B, C, H, W), dtype=jnp.float32), 'Wq': jax.random.normal(ks[1], (C8, C), dtype=jnp.float32) * 0.05, 'bq': jax.random.normal(ks[2], (C8,), dtype=jnp.float32) * 0.05, 'Wk': jax.random.normal(ks[3], (C8, C), dtype=jnp.float32) * 0.05, 'bk': jax.random.normal(ks[4], (C8,), dtype=jnp.float32) * 0.05, 'Wv': jax.random.normal(ks[5], (C, C), dtype=jnp.float32) * 0.05, 'bv': jax.random.normal(ks[6], (C,), dtype=jnp.float32) * 0.05}
    _L1_conv_all = _L1_conv_setup()
    _L1_conv_in = {k: v for k, v in _L1_conv_all.items() if k in ('Wq', 'bq', 'Wk', 'bk', 'Wv', 'bv', )}
    del _L1_conv_all

    def _L2_conv_setup():
        import jax, jax.numpy as jnp
        import numpy as np
        WS = 8
        SHIFT = 4
        NH = 8
        C = 64
        HD = C // NH
        SCALE = HD ** (-0.5)
        MLP_HID = int(C * 2.0)

        def _rel_pos_index():
            coords = np.stack(np.meshgrid(np.arange(WS), np.arange(WS), indexing='ij'))
            flat = coords.reshape(2, -1)
            rel = flat[:, :, None] - flat[:, None, :]
            rel = rel.transpose(1, 2, 0).copy()
            rel[..., 0] += WS - 1
            rel[..., 1] += WS - 1
            rel[..., 0] *= 2 * WS - 1
            return rel.sum(-1)
        RPI = _rel_pos_index()

        def _shift_mask(H, W):
            img = np.zeros((H, W))
            slices = (slice(0, -WS), slice(-WS, -SHIFT), slice(-SHIFT, None))
            cnt = 0
            for hs in slices:
                for ws_ in slices:
                    img[hs, ws_] = cnt
                    cnt += 1
            mw = img.reshape(H // WS, WS, W // WS, WS).transpose(0, 2, 1, 3).reshape(-1, WS * WS)
            m = mw[:, None, :] - mw[:, :, None]
            return np.where(m != 0, np.float32(-100.0), np.float32(0.0)).astype(np.float32)

        def layernorm(x, g, b, eps=1e-05):
            mu = x.mean(-1, keepdims=True)
            var = ((x - mu) ** 2).mean(-1, keepdims=True)
            return (x - mu) * jax.lax.rsqrt(var + eps) * g + b

        def _block(x, H, W, shift, mask, n1g, n1b, qw, qb, pw, pb, rpb, n2g, n2b, f1w, f1b, f2w, f2b):
            B, L, Cc = x.shape
            shortcut = x
            h = layernorm(x, n1g, n1b).reshape(B, H, W, Cc)
            if shift > 0:
                h = jnp.roll(h, (-shift, -shift), (1, 2))
            xw = h.reshape(B, H // WS, WS, W // WS, WS, Cc).transpose(0, 1, 3, 2, 4, 5).reshape(-1, WS * WS, Cc)
            B_, N, _ = xw.shape
            qkv = (xw @ qw + qb).reshape(B_, N, 3, NH, HD).transpose(2, 0, 3, 1, 4)
            q, k, v = (qkv[0] * SCALE, qkv[1], qkv[2])
            attn = jnp.einsum('bhnd,bhmd->bhnm', q, k)
            bias = rpb[RPI.reshape(-1)].reshape(N, N, NH).transpose(2, 0, 1)
            attn = attn + bias[None]
            if mask is not None:
                nW = mask.shape[0]
                attn = (attn.reshape(B_ // nW, nW, NH, N, N) + mask[None, :, None]).reshape(B_, NH, N, N)
            attn = jax.nn.softmax(attn, axis=-1)
            o = jnp.einsum('bhnm,bhmd->bhnd', attn, v).transpose(0, 2, 1, 3).reshape(B_, N, Cc)
            o = o @ pw + pb
            o = o.reshape(B, H // WS, W // WS, WS, WS, Cc).transpose(0, 1, 3, 2, 4, 5).reshape(B, H, W, Cc)
            if shift > 0:
                o = jnp.roll(o, (shift, shift), (1, 2))
            x = shortcut + o.reshape(B, L, Cc)
            h2 = layernorm(x, n2g, n2b)
            x = x + (jax.nn.gelu(h2 @ f1w + f1b, approximate=False) @ f2w + f2b)
            return x
        key = jax.random.key(seed)
        ks = jax.random.split(key, 16)
        B, H, W = (32, 64, 64)
        d = {'x': jax.random.normal(ks[0], (B, C, H, W), jnp.float32), 'pe_g': jnp.ones((C,), jnp.float32), 'pe_b': jnp.zeros((C,), jnp.float32), 'norm1_g': jnp.ones((2, C), jnp.float32), 'norm1_b': jnp.zeros((2, C), jnp.float32), 'qkv_w': jax.random.normal(ks[1], (2, C, 3 * C), jnp.float32) * 0.02, 'qkv_b': jnp.zeros((2, 3 * C), jnp.float32), 'proj_w': jax.random.normal(ks[2], (2, C, C), jnp.float32) * 0.02, 'proj_b': jnp.zeros((2, C), jnp.float32), 'rpb': jax.random.normal(ks[3], (2, (2 * WS - 1) ** 2, NH), jnp.float32) * 0.02, 'norm2_g': jnp.ones((2, C), jnp.float32), 'norm2_b': jnp.zeros((2, C), jnp.float32), 'fc1_w': jax.random.normal(ks[4], (2, C, MLP_HID), jnp.float32) * 0.02, 'fc1_b': jnp.zeros((2, MLP_HID), jnp.float32), 'fc2_w': jax.random.normal(ks[5], (2, MLP_HID, C), jnp.float32) * 0.02, 'fc2_b': jnp.zeros((2, C), jnp.float32)}
        return d
    _L2_conv_all = _L2_conv_setup()
    _L2_conv_in = {k: v for k, v in _L2_conv_all.items() if k in ('pe_g', 'pe_b', 'norm1_g', 'norm1_b', 'qkv_w', 'qkv_b', 'proj_w', 'proj_b', 'rpb', 'norm2_g', 'norm2_b', 'fc1_w', 'fc1_b', 'fc2_w', 'fc2_b', )}
    del _L2_conv_all

    def _L3_conv_setup():
        import jax, jax.numpy as jnp
        from jax import lax
        import numpy as np
        B, C, H, W = (8, 64, 256, 256)
        K = 9
        R = (K - 1) // 2
        HIDDEN = 32

        def _forward(x, gauss_kernel, w1, b1, w2, b2):
            Bx, Cx, Hx, Wx = x.shape
            Kx = gauss_kernel.shape[0]
            r = (Kx - 1) // 2
            h = jax.nn.relu(jnp.einsum('bchw,co->bohw', x, w1) + b1[None, :, None, None])
            ks = jax.nn.relu(jnp.einsum('bohw,o->bhw', h, w2[:, 0]) + b2[0]) * 20.0 + 1.0
            sigma = ks / 3.0
            logits = -gauss_kernel[None, None, None] / (2.0 * sigma[..., None, None] ** 2)
            wgt = jnp.exp(logits)
            wgt = wgt / jnp.sum(wgt, axis=(-2, -1), keepdims=True)
            wflat = wgt.reshape(Bx, Hx, Wx, Kx * Kx)
            xp = jnp.pad(x, ((0, 0), (0, 0), (r, r), (r, r)))

            def step(acc, idx):
                u = idx // Kx
                v = idx % Kx
                xs = lax.dynamic_slice(xp, (0, 0, u, v), (Bx, Cx, Hx, Wx))
                wk = lax.dynamic_slice_in_dim(wflat, idx, 1, axis=3)[..., 0]
                return (acc + xs * wk[:, None, :, :], None)
            low_freq, _ = lax.scan(step, jnp.zeros_like(x), jnp.arange(Kx * Kx))
            enhanced = x + low_freq
            mu = jnp.mean(enhanced, axis=(2, 3), keepdims=True)
            var = jnp.var(enhanced, axis=(2, 3), keepdims=True)
            return (enhanced - mu) / jnp.sqrt(var + 1e-05)
        key = jax.random.key(seed)
        k1, k2, k3, k4, k5 = jax.random.split(key, 5)
        x = jax.random.normal(k1, (B, C, H, W), dtype=jnp.float32)
        off = jnp.arange(K, dtype=jnp.float32) - R
        gauss_kernel = off[:, None] ** 2 + off[None, :] ** 2
        w1 = jax.random.normal(k2, (C, HIDDEN), dtype=jnp.float32) * (1.0 / np.sqrt(C))
        b1 = jax.random.normal(k3, (HIDDEN,), dtype=jnp.float32) * 0.01
        w2 = jax.random.normal(k4, (HIDDEN, 1), dtype=jnp.float32) * (1.0 / np.sqrt(HIDDEN))
        b2 = jax.random.normal(k5, (1,), dtype=jnp.float32) * 0.01
        return {'x': x, 'gauss_kernel': gauss_kernel, 'w1': w1, 'b1': b1, 'w2': w2, 'b2': b2}
    _L3_conv_all = _L3_conv_setup()
    _L3_conv_in = {k: v for k, v in _L3_conv_all.items() if k in ('gauss_kernel', 'w1', 'b1', 'w2', 'b2', )}
    del _L3_conv_all

    return {
        "x": x,
        "L0_conv_w1": _L0_conv_in["w1"],
        "L0_conv_b1": _L0_conv_in["b1"],
        "L0_conv_a1": _L0_conv_in["a1"],
        "L0_conv_w2": _L0_conv_in["w2"],
        "L0_conv_b2": _L0_conv_in["b2"],
        "L0_conv_a2": _L0_conv_in["a2"],
        "L0_conv_w3": _L0_conv_in["w3"],
        "L0_conv_b3": _L0_conv_in["b3"],
        "L0_conv_a3": _L0_conv_in["a3"],
        "L1_conv_Wq": _L1_conv_in["Wq"],
        "L1_conv_bq": _L1_conv_in["bq"],
        "L1_conv_Wk": _L1_conv_in["Wk"],
        "L1_conv_bk": _L1_conv_in["bk"],
        "L1_conv_Wv": _L1_conv_in["Wv"],
        "L1_conv_bv": _L1_conv_in["bv"],
        "L2_conv_pe_g": _L2_conv_in["pe_g"],
        "L2_conv_pe_b": _L2_conv_in["pe_b"],
        "L2_conv_norm1_g": _L2_conv_in["norm1_g"],
        "L2_conv_norm1_b": _L2_conv_in["norm1_b"],
        "L2_conv_qkv_w": _L2_conv_in["qkv_w"],
        "L2_conv_qkv_b": _L2_conv_in["qkv_b"],
        "L2_conv_proj_w": _L2_conv_in["proj_w"],
        "L2_conv_proj_b": _L2_conv_in["proj_b"],
        "L2_conv_rpb": _L2_conv_in["rpb"],
        "L2_conv_norm2_g": _L2_conv_in["norm2_g"],
        "L2_conv_norm2_b": _L2_conv_in["norm2_b"],
        "L2_conv_fc1_w": _L2_conv_in["fc1_w"],
        "L2_conv_fc1_b": _L2_conv_in["fc1_b"],
        "L2_conv_fc2_w": _L2_conv_in["fc2_w"],
        "L2_conv_fc2_b": _L2_conv_in["fc2_b"],
        "L3_conv_gauss_kernel": _L3_conv_in["gauss_kernel"],
        "L3_conv_w1": _L3_conv_in["w1"],
        "L3_conv_b1": _L3_conv_in["b1"],
        "L3_conv_w2": _L3_conv_in["w2"],
        "L3_conv_b2": _L3_conv_in["b2"],
    }

def reference(x, L0_conv_w1, L0_conv_b1, L0_conv_a1, L0_conv_w2, L0_conv_b2, L0_conv_a2, L0_conv_w3, L0_conv_b3, L0_conv_a3, L1_conv_Wq, L1_conv_bq, L1_conv_Wk, L1_conv_bk, L1_conv_Wv, L1_conv_bv, L2_conv_pe_g, L2_conv_pe_b, L2_conv_norm1_g, L2_conv_norm1_b, L2_conv_qkv_w, L2_conv_qkv_b, L2_conv_proj_w, L2_conv_proj_b, L2_conv_rpb, L2_conv_norm2_g, L2_conv_norm2_b, L2_conv_fc1_w, L2_conv_fc1_b, L2_conv_fc2_w, L2_conv_fc2_b, L3_conv_gauss_kernel, L3_conv_w1, L3_conv_b1, L3_conv_w2, L3_conv_b2):
    import jax
    import jax.numpy as jnp
    def _L0_conv_ref(x, w1, b1, a1, w2, b2, a2, w3, b3, a3):
        import jax, jax.numpy as jnp
        import numpy as np

        def _prelu(x, a):
            return jnp.where(x >= 0, x, a * x)

        def _conv1x1(x, w, b):
            return jnp.einsum('nchw,oc->nohw', x, w) + b[None, :, None, None]
        res_scale = 1.0
        n, C, h, w = x.shape
        e1 = _prelu(_conv1x1(x, w1, b1), a1[0])
        e2 = _prelu(_conv1x1(x, w2, b2), a2[0])
        e3 = _prelu(_conv1x1(x, w3, b3), a3[0])
        c = e1.shape[1]
        hw = h * w
        q = e1.transpose(0, 2, 3, 1).reshape(n, hw, c)
        k = e2.reshape(n, c, hw)
        score = jax.nn.softmax(jnp.matmul(q, k), axis=-1)
        v = e3.reshape(n, C, hw).transpose(0, 2, 1)
        out = jnp.matmul(score, v)
        out = out.transpose(0, 2, 1).reshape(n, C, h, w)
        return out + res_scale * x

    def _L1_conv_ref(x, Wq, bq, Wk, bk, Wv, bv):
        import jax, jax.numpy as jnp
        import numpy as np
        B, C, H, W = x.shape
        N = H * W
        xf = x.reshape(B, C, N)
        q = jnp.einsum('dc,bcn->bnd', Wq, xf) + bq
        k = jnp.einsum('dc,bcn->bdn', Wk, xf) + bk[:, None]
        v = jnp.einsum('dc,bcn->bdn', Wv, xf) + bv[:, None]
        attn = jnp.einsum('bnd,bdm->bnm', q, k)
        attn = jax.nn.softmax(attn, axis=-2)
        out = jnp.einsum('bcm,bnm->bcn', v, attn)
        return out.reshape(B, C, H, W) + x

    def _L2_conv_ref(x, pe_g, pe_b, norm1_g, norm1_b, qkv_w, qkv_b, proj_w, proj_b, rpb, norm2_g, norm2_b, fc1_w, fc1_b, fc2_w, fc2_b):
        import jax, jax.numpy as jnp
        import numpy as np
        WS = 8
        SHIFT = 4
        NH = 8
        C = 64
        HD = C // NH
        SCALE = HD ** (-0.5)
        MLP_HID = int(C * 2.0)

        def _rel_pos_index():
            coords = np.stack(np.meshgrid(np.arange(WS), np.arange(WS), indexing='ij'))
            flat = coords.reshape(2, -1)
            rel = flat[:, :, None] - flat[:, None, :]
            rel = rel.transpose(1, 2, 0).copy()
            rel[..., 0] += WS - 1
            rel[..., 1] += WS - 1
            rel[..., 0] *= 2 * WS - 1
            return rel.sum(-1)
        RPI = _rel_pos_index()

        def _shift_mask(H, W):
            img = np.zeros((H, W))
            slices = (slice(0, -WS), slice(-WS, -SHIFT), slice(-SHIFT, None))
            cnt = 0
            for hs in slices:
                for ws_ in slices:
                    img[hs, ws_] = cnt
                    cnt += 1
            mw = img.reshape(H // WS, WS, W // WS, WS).transpose(0, 2, 1, 3).reshape(-1, WS * WS)
            m = mw[:, None, :] - mw[:, :, None]
            return np.where(m != 0, np.float32(-100.0), np.float32(0.0)).astype(np.float32)

        def layernorm(x, g, b, eps=1e-05):
            mu = x.mean(-1, keepdims=True)
            var = ((x - mu) ** 2).mean(-1, keepdims=True)
            return (x - mu) * jax.lax.rsqrt(var + eps) * g + b

        def _block(x, H, W, shift, mask, n1g, n1b, qw, qb, pw, pb, rpb, n2g, n2b, f1w, f1b, f2w, f2b):
            B, L, Cc = x.shape
            shortcut = x
            h = layernorm(x, n1g, n1b).reshape(B, H, W, Cc)
            if shift > 0:
                h = jnp.roll(h, (-shift, -shift), (1, 2))
            xw = h.reshape(B, H // WS, WS, W // WS, WS, Cc).transpose(0, 1, 3, 2, 4, 5).reshape(-1, WS * WS, Cc)
            B_, N, _ = xw.shape
            qkv = (xw @ qw + qb).reshape(B_, N, 3, NH, HD).transpose(2, 0, 3, 1, 4)
            q, k, v = (qkv[0] * SCALE, qkv[1], qkv[2])
            attn = jnp.einsum('bhnd,bhmd->bhnm', q, k)
            bias = rpb[RPI.reshape(-1)].reshape(N, N, NH).transpose(2, 0, 1)
            attn = attn + bias[None]
            if mask is not None:
                nW = mask.shape[0]
                attn = (attn.reshape(B_ // nW, nW, NH, N, N) + mask[None, :, None]).reshape(B_, NH, N, N)
            attn = jax.nn.softmax(attn, axis=-1)
            o = jnp.einsum('bhnm,bhmd->bhnd', attn, v).transpose(0, 2, 1, 3).reshape(B_, N, Cc)
            o = o @ pw + pb
            o = o.reshape(B, H // WS, W // WS, WS, WS, Cc).transpose(0, 1, 3, 2, 4, 5).reshape(B, H, W, Cc)
            if shift > 0:
                o = jnp.roll(o, (shift, shift), (1, 2))
            x = shortcut + o.reshape(B, L, Cc)
            h2 = layernorm(x, n2g, n2b)
            x = x + (jax.nn.gelu(h2 @ f1w + f1b, approximate=False) @ f2w + f2b)
            return x
        B, Cc, H, W = x.shape
        t = x.reshape(B, Cc, H * W).transpose(0, 2, 1)
        t = layernorm(t, pe_g, pe_b)
        mask = jnp.asarray(_shift_mask(H, W))
        for i, shift in enumerate((0, SHIFT)):
            t = _block(t, H, W, shift, mask if shift > 0 else None, norm1_g[i], norm1_b[i], qkv_w[i], qkv_b[i], proj_w[i], proj_b[i], rpb[i], norm2_g[i], norm2_b[i], fc1_w[i], fc1_b[i], fc2_w[i], fc2_b[i])
        return t.transpose(0, 2, 1).reshape(B, Cc, H, W)

    def _L3_conv_ref(x, gauss_kernel, w1, b1, w2, b2):
        import jax, jax.numpy as jnp
        from jax import lax
        import numpy as np
        B, C, H, W = (8, 64, 256, 256)
        K = 9
        R = (K - 1) // 2
        HIDDEN = 32

        def _forward(x, gauss_kernel, w1, b1, w2, b2):
            Bx, Cx, Hx, Wx = x.shape
            Kx = gauss_kernel.shape[0]
            r = (Kx - 1) // 2
            h = jax.nn.relu(jnp.einsum('bchw,co->bohw', x, w1) + b1[None, :, None, None])
            ks = jax.nn.relu(jnp.einsum('bohw,o->bhw', h, w2[:, 0]) + b2[0]) * 20.0 + 1.0
            sigma = ks / 3.0
            logits = -gauss_kernel[None, None, None] / (2.0 * sigma[..., None, None] ** 2)
            wgt = jnp.exp(logits)
            wgt = wgt / jnp.sum(wgt, axis=(-2, -1), keepdims=True)
            wflat = wgt.reshape(Bx, Hx, Wx, Kx * Kx)
            xp = jnp.pad(x, ((0, 0), (0, 0), (r, r), (r, r)))

            def step(acc, idx):
                u = idx // Kx
                v = idx % Kx
                xs = lax.dynamic_slice(xp, (0, 0, u, v), (Bx, Cx, Hx, Wx))
                wk = lax.dynamic_slice_in_dim(wflat, idx, 1, axis=3)[..., 0]
                return (acc + xs * wk[:, None, :, :], None)
            low_freq, _ = lax.scan(step, jnp.zeros_like(x), jnp.arange(Kx * Kx))
            enhanced = x + low_freq
            mu = jnp.mean(enhanced, axis=(2, 3), keepdims=True)
            var = jnp.var(enhanced, axis=(2, 3), keepdims=True)
            return (enhanced - mu) / jnp.sqrt(var + 1e-05)
        return _forward(x, gauss_kernel, w1, b1, w2, b2)

    def _gn(v, G=32, eps=1e-5):
        B_, C_, H_, W_ = v.shape
        g = v.reshape(B_, G, C_ // G, H_, W_)
        m = jnp.mean(g, axis=(2, 3, 4), keepdims=True)
        s = jnp.var(g, axis=(2, 3, 4), keepdims=True)
        return ((g - m) / jnp.sqrt(s + eps)).reshape(v.shape)

    def _ln_c(v, eps=1e-6):
        m = jnp.mean(v, axis=1, keepdims=True)
        s = jnp.var(v, axis=1, keepdims=True)
        return (v - m) / jnp.sqrt(s + eps)

    def _ln_t(v, eps=1e-5):
        m = jnp.mean(v, axis=-1, keepdims=True)
        s = jnp.var(v, axis=-1, keepdims=True)
        return (v - m) / jnp.sqrt(s + eps)

    def _to_tokens(v):
        B_, C_, H_, W_ = v.shape
        return v.reshape(B_, C_, H_ * W_).transpose(0, 2, 1)
    def _from_tokens(t, like):
        B_, C_, H_, W_ = like.shape
        return t.transpose(0, 2, 1).reshape(B_, C_, H_, W_)

    x = _L0_conv_ref(x, L0_conv_w1, L0_conv_b1, L0_conv_a1, L0_conv_w2, L0_conv_b2, L0_conv_a2, L0_conv_w3, L0_conv_b3, L0_conv_a3)
    x = _L1_conv_ref(x, L1_conv_Wq, L1_conv_bq, L1_conv_Wk, L1_conv_bk, L1_conv_Wv, L1_conv_bv)
    x = _L2_conv_ref(x, L2_conv_pe_g, L2_conv_pe_b, L2_conv_norm1_g, L2_conv_norm1_b, L2_conv_qkv_w, L2_conv_qkv_b, L2_conv_proj_w, L2_conv_proj_b, L2_conv_rpb, L2_conv_norm2_g, L2_conv_norm2_b, L2_conv_fc1_w, L2_conv_fc1_b, L2_conv_fc2_w, L2_conv_fc2_b)
    x = _L3_conv_ref(x, L3_conv_gauss_kernel, L3_conv_w1, L3_conv_b1, L3_conv_w2, L3_conv_b2)
    return x


_drawn_inputs = setup_inputs


def setup_inputs(seed=0):
    import zlib

    import numpy as np

    out = dict(_drawn_inputs(seed))
    spreads = {'L0_conv_b1': (0.0, 0.1),
     'L0_conv_b2': (0.0, 0.301),
     'L0_conv_b3': (0.0, 0.1),
     'L2_conv_pe_g': (1.0, 0.2),
     'L2_conv_pe_b': (0.0, 0.1),
     'L2_conv_norm1_g': (1.0, 0.6),
     'L2_conv_norm1_b': (0.0, 0.8),
     'L2_conv_qkv_b': (0.0, 0.448),
     'L2_conv_proj_b': (0.0, 0.1),
     'L2_conv_norm2_g': (1.0, 0.6),
     'L2_conv_norm2_b': (0.0, 2.0),
     'L2_conv_fc1_b': (0.0, 0.631),
     'L2_conv_fc2_b': (0.0, 0.1)}
    factors = {'L1_conv_bq': 64.0,
     'L1_conv_bk': 3.801,
     'L2_conv_qkv_w': 4.747,
     'L2_conv_proj_w': 3.487,
     'L2_conv_rpb': 8.0,
     'L3_conv_b1': 6.275}
    for name, (base, spread) in spreads.items():
        noise = np.random.default_rng([zlib.crc32(name.encode()), seed]).standard_normal(out[name].shape)
        drawn = base * np.exp(spread * noise) if base else spread * noise
        out[name] = jnp.asarray(drawn.astype(out[name].dtype))
    for name, factor in factors.items():
        out[name] = (out[name] * factor).astype(out[name].dtype)
    return out
```

```python
from contextlib import ExitStack

import concourse.bass as bass
from concourse import mybir

F32 = mybir.dt.float32
F16 = mybir.dt.float16
ALU = mybir.AluOpType
ACT = mybir.ActivationFunctionType
AXX = mybir.AxisListType.X

NI, C, HH, WW = 8, 64, 64, 64
NT = HH * WW
CH = 512
NCH = NT // CH
KT = NT // 128
SHIFT = 4


def _attention0(nc, keep, x_in, w, x_out):
    UQ = 1024
    NU = NT // UQ
    QT = UQ // 128
    ASTEPS = QT * NCH
    MS = 64.0
    NP = 4
    GV = KT // 8
    with ExitStack() as ctx:
        sb = lambda n, s, d=F32: ctx.enter_context(nc.sbuf_tensor("a0_" + n, s, d))
        sem = lambda n: keep.enter_context(nc.semaphore("a0_" + n))
        xa = sb("xa", [C + 1, NT])
        xr = sb("xr", [128, NU, CH])
        wqk = sb("wqk", [C + 1, 2, 96])
        wv = sb("wv", [C + 1, C])
        al = sb("al", [128, 3])
        ident = sb("ident", [128, 128])
        ones = sb("ones", [128, C])
        raw = sb("raw", [96, 2, 2, CH])
        neg = sb("neg", [96, 2, 2, CH])
        negv = sb("negv", [128, 2, CH])
        qs = sb("qs", [97, NT], F16)
        ks = sb("ks", [97, NT], F16)
        vt = sb("vt", [128, KT, C])
        p = sb("p", [128, NP, UQ])
        sum_d = sb("sum_d", [128, UQ])
        sum_p = sb("sum_p", [128, UQ])
        mparts = sb("mparts", [128, QT, NCH])
        mneg = sb("mneg", [128, QT])
        rden = sb("rden", [128, CH])
        att = sb("att", [128, CH])
        res = sb("res", [128, CH])
        a_ps = ctx.enter_context(nc.psum_tensor("a0_a_ps", [128, 2, CH], F32))
        b_ps = ctx.enter_context(nc.psum_tensor("a0_b_ps", [128, 2, 2, CH], F32))
        acc = ctx.enter_context(nc.psum_tensor("a0_acc", [128, CH], F32))
        den = ctx.enter_context(nc.psum_tensor("a0_den", [128, CH], F32))

        w_loaded = sem("w_loaded")
        xa_loaded, xr_loaded = sem("xa_loaded"), sem("xr_loaded")
        const_done = sem("const_done")
        proj_done = sem("proj_done")
        neg_done = sem("neg_done")
        raw_done, hi_done, split_done = sem("raw_done"), sem("hi_done"), sem("split_done")
        vt_done = sem("vt_done")
        sa_done, max_done = sem("sa_done"), sem("max_done")
        mneg_done, mrow_ps, mrow_done = sem("mneg_done"), sem("mrow_ps"), sem("mrow_done")
        sb_done, exp_done, pv_done = sem("sb_done"), sem("exp_done"), sem("pv_done")
        addp_done, addd_done, den_done = sem("addp_done"), sem("addd_done"), sem("den_done")
        rden_done, att_done, res_done = sem("rden_done"), sem("att_done"), sem("res_done")
        stored = sem("stored")
        block = ctx.enter_context(nc.Block())

        PREP = NCH + GV
        HALF = KT // 2

        @block.sync
        def _(e):
            e.dma_start(wqk[:], w["wqk"]).then_inc(w_loaded, 16)
            e.dma_start(wv[:], w["wv"]).then_inc(w_loaded, 16)
            e.dma_start(al[:], w["al"]).then_inc(w_loaded, 16)
            e.dma_start(ident[:], w["ident"]).then_inc(w_loaded, 16)
            e.sem_inc(stored, 1)
            xin_v = x_in.rearrange("i c (u j n) -> j i c u n", u=NU, j=2)
            xout_v = x_out.rearrange("i c (u j n) -> j i c u n", u=NU, j=2)

            def load_xa(im):
                e.dma_start(xa[0:C, :], x_in[bass.ds(im, 1)].rearrange("a c n -> (a c) n")).then_inc(xa_loaded, 16)

            def load_xr(im):
                for j in range(2):
                    e.dma_start(xr[64 * j:64 * j + 64], xin_v[j][bass.ds(im, 1)].rearrange("i c u n -> (i c) u n"))\
                        .then_inc(xr_loaded, 16)

            def store(im, u):
                e.wait_ge(res_done, im * NU + u + 1)
                for j in range(2):
                    e.dma_start(xout_v[j][bass.ds(im, 1), :, bass.ds(u, 1)].rearrange("i c u n -> (i c) (u n)"),
                                res[64 * j:64 * j + 64]).then_inc(stored, 16)

            load_xa(0)
            load_xr(0)
            with e.Fori(0, NI - 1) as im:
                e.wait_ge(vt_done, im * GV + GV)
                load_xa(im + 1)
                for u in range(NU):
                    store(im, u)
                load_xr(im + 1)
            for u in range(NU):
                store(NI - 1, u)
            e.wait_ge(stored, NI * NU * 32 + 1)

        @block.gpsimd
        def _(e):
            e.sem_inc(addp_done, NP // 2)
            with e.Fori(0, NI) as im:
                for ch in range(NCH):
                    cs = slice(ch * CH, ch * CH + CH)
                    e.wait_ge(hi_done, im * NCH + ch + 1)
                    e.tensor_tensor(qs[64:96, cs], raw[64:96, ch % 2, 0], qs[64:96, cs], ALU.subtract)
                    e.tensor_tensor(ks[32:64, cs], raw[32:64, ch % 2, 1], ks[32:64, cs],
                                    ALU.subtract).then_inc(split_done, 1)
                with e.Fori(0, NU) as u:
                    g = e.snap(im * NU + u)
                    e.wait_ge(den_done, g + 1)
                    for i in range(1, HALF):
                        e.wait_ge(exp_done, g * KT + 2 * i + 1 + 2)
                        if i > 1:
                            e.wait_ge(addp_done, g * HALF + i + NP // 2)
                        e.tensor_tensor(sum_p[:], p[:, 0] if i == 1 else sum_p[:], p[:, (2 * i) % NP],
                                        ALU.add).then_inc(addp_done, 2 if i == 1 else 1)

        @block.scalar
        def _(e):
            e.sem_inc(exp_done, 2)
            e.sem_inc(mrow_done, 1)
            with e.Fori(0, NI) as im:
                for ch in range(NCH):
                    cs = slice(ch * CH, ch * CH + CH)
                    e.wait_ge(raw_done, im * NCH + ch + 1)
                    e.activation(qs[0:96, cs], raw[:, ch % 2, 0], ACT.Copy)
                    e.activation(ks[0:96, cs], raw[:, ch % 2, 1], ACT.Copy).then_inc(hi_done, 1)
                with e.Fori(0, NU) as u:
                    g = e.snap(im * NU + u)
                    e.wait_ge(mrow_ps, g + 1)
                    e.activation(qs[96:97, bass.ds(u * UQ, UQ)], a_ps[96:97, :, :].rearrange("p a n -> p (a n)"),
                                 ACT.Copy, scale=1.0 / MS).then_inc(mrow_done, 1)
                    for kt in range(KT):
                        e.wait_ge(sb_done, g * KT + kt + 1)
                        e.wait_ge(pv_done, g * KT + kt + 1)
                        e.wait_ge(addp_done if kt % 2 == 0 else addd_done, g * HALF + kt // 2 + 1)
                        e.activation(p[:, kt % NP], b_ps[:, kt % 2].rearrange("p a n -> p (a n)"),
                                     ACT.Exp).then_inc(exp_done, 1)

        @block.vector
        def _(e):
            e.memset(xa[C:C + 1, :], 1.0).then_inc(const_done, 1)
            e.memset(ks[96:97, :], MS).then_inc(const_done, 1)
            e.memset(ones[:], 1.0).then_inc(const_done, 1)
            e.sem_inc(addd_done, NP // 2)
            e.sem_inc(att_done, 1)
            e.wait_ge(w_loaded, 64)

            def max_steps(g, t, c):
                s = t * NCH + c
                e.wait_ge(sa_done, g * ASTEPS + s + 1)
                e.reduce_max(mparts[:, t, c:c + 1], a_ps[:, s % 2], AXX).then_inc(max_done, 1)

            def mneg_step(g):
                e.wait_ge(max_done, g * ASTEPS + ASTEPS + 2)
                e.reduce_max(mneg[:], mparts[:], AXX, negate=True).then_inc(mneg_done, 1)

            e.sem_inc(max_done, 2)
            with e.Fori(0, NI) as im:
                for ch in range(NCH):
                    t = b_ps[0:96, ch % 2]
                    e.wait_ge(proj_done, im * PREP + ch + 1)
                    for j in range(2):
                        ins = e.tensor_scalar(neg[:, ch % 2, j], t[:, j], 0.0, al[0:96, j:j + 1], ALU.min, ALU.mult)
                    ins.then_inc(neg_done, 1)
                    e.wait_ge(neg_done, im * PREP + ch + 1)
                    if ch >= 2:
                        e.wait_ge(split_done, im * NCH + ch - 1)
                    e.scalar_tensor_tensor(raw[:, ch % 2], t, 0.0, neg[:, ch % 2], ALU.max, ALU.add)\
                        .then_inc(raw_done, 1)
                for gv in range(GV):
                    t = a_ps[:, gv % 2]
                    e.wait_ge(proj_done, im * PREP + NCH + gv + 1)
                    e.tensor_scalar(negv[:, gv % 2], t, 0.0, al[:, 2:3], ALU.min, ALU.mult).then_inc(neg_done, 1)
                    e.wait_ge(neg_done, im * PREP + NCH + gv + 1)
                    e.scalar_tensor_tensor(vt[:, 8 * gv:8 * gv + 8].rearrange("p a c -> p (a c)"), t, 0.0,
                                           negv[:, gv % 2], ALU.max, ALU.add).then_inc(vt_done, 1)
                g0 = e.snap(im * NU)
                for s in range(ASTEPS):
                    max_steps(g0, s // NCH, s % NCH)
                mneg_step(g0)

                def unit(g, u, more):
                    for kt in range(KT):
                        if more:
                            for s in range(2 * kt, 2 * kt + 2):
                                max_steps(g + 1, s // NCH, s % NCH)
                        if kt % 2 and kt > 1:
                            e.wait_ge(exp_done, g * KT + kt + 1 + 2)
                            if kt > 3:
                                e.wait_ge(addd_done, g * HALF + kt // 2 + NP // 2)
                            e.tensor_tensor(sum_d[:], p[:, 1] if kt == 3 else sum_d[:], p[:, kt % NP],
                                            ALU.add).then_inc(addd_done, 2 if kt == 3 else 1)
                    if more:
                        mneg_step(g + 1)
                    e.wait_ge(den_done, g + 2)
                    e.reciprocal(rden[:], den[:]).then_inc(rden_done, 1)
                    e.wait_ge(rden_done, g + 1)
                    e.tensor_tensor(att[:], acc[:], rden[:], ALU.mult).then_inc(att_done, 1)
                    e.wait_ge(att_done, g + 2)
                    e.wait_ge(xr_loaded, im * 32 + 32)
                    e.wait_ge(stored, g * 32 + 1)
                    e.tensor_tensor(res[:], att[:], xr[:, bass.ds(u, 1)].rearrange("p a n -> p (a n)"),
                                    ALU.add).then_inc(res_done, 1)

                with e.Fori(0, NU - 1) as u:
                    unit(e.snap(im * NU + u), u, True)
                unit(e.snap(im * NU + NU - 1), NU - 1, False)

        @block.tensor
        def _(e):
            e.sem_inc(pv_done, NP)
            e.sem_inc(den_done, 1)
            e.wait_ge(w_loaded, 64)
            e.wait_ge(const_done, 3)

            def pass_a(g, u, s):
                t, c = s // NCH, s % NCH
                e.wait_ge(max_done, g * ASTEPS + s + 1)
                e.matmul(a_ps[:, s % 2], qs[0:96, bass.ds(u * UQ + t * 128, 128)],
                         ks[0:96, c * CH:c * CH + CH], start=True, stop=True).then_inc(sa_done, 1)

            def max_row(g):
                e.wait_ge(mneg_done, g + 1)
                for t in range(QT):
                    ins = e.matmul(a_ps[96:97, t // 4, (t % 4) * 128:(t % 4) * 128 + 128], mneg[:, t:t + 1],
                                   ident[:], start=True, stop=True)
                ins.then_inc(mrow_ps, 1)

            with e.Fori(0, NI) as im:
                e.wait_ge(xa_loaded, im * 16 + 16)
                e.wait_ge(exp_done, im * (NU * KT) + 2)
                for ch in range(NCH):
                    if ch >= 2:
                        e.wait_ge(raw_done, im * NCH + ch - 1)
                    for j in range(2):
                        ins = e.matmul(b_ps[0:96, ch % 2, j], wqk[:, j], xa[:, ch * CH:ch * CH + CH],
                                       start=True, stop=True)
                    ins.then_inc(proj_done, 1)
                e.wait_ge(mrow_done, im * NU + 1)
                for gv in range(GV):
                    if gv >= 2:
                        e.wait_ge(vt_done, im * GV + gv - 1)
                    for i in range(8):
                        t = gv * 8 + i
                        ins = e.matmul(a_ps[:, gv % 2, i * C:i * C + C], xa[:, t * 128:t * 128 + 128],
                                       wv[:], start=True, stop=True)
                    ins.then_inc(proj_done, 1)
                e.wait_ge(split_done, im * NCH + NCH)
                e.wait_ge(vt_done, im * GV + GV)
                g0 = e.snap(im * NU)
                for s in range(ASTEPS):
                    pass_a(g0, 0, s)
                max_row(g0)

                def pv(g, kt):
                    e.wait_ge(exp_done, g * KT + kt + 1 + 2)
                    for j in range(2):
                        ins = e.matmul(acc[64 * j:64 * j + 64, :], vt[:, kt], p[:, kt % NP, j * CH:j * CH + CH],
                                       start=kt == 0, stop=kt == KT - 1)
                    ins.then_inc(pv_done, 1)

                def unit(g, u, more):
                    e.wait_ge(mrow_done, g + 2)
                    e.wait_ge(att_done, g + 1)
                    for kt in range(KT):
                        e.wait_ge(exp_done, g * KT + kt + 1)
                        for j in range(2):
                            ins = e.matmul(b_ps[:, kt % 2, j], ks[:, kt * 128:kt * 128 + 128],
                                           qs[:, bass.ds(u * UQ + j * CH, CH)], start=True, stop=True)
                        ins.then_inc(sb_done, 1)
                        if more:
                            for s in range(2 * kt, 2 * kt + 2):
                                pass_a(g + 1, u + 1, s)
                        if kt >= 1:
                            pv(g, kt - 1)
                    pv(g, KT - 1)
                    e.wait_ge(addp_done, g * HALF + HALF + NP // 2)
                    e.wait_ge(addd_done, g * HALF + HALF + NP // 2)
                    for j in range(2):
                        for k, part in enumerate((sum_d, sum_p)):
                            ins = e.matmul(den[64 * j:64 * j + 64, :], ones[:], part[:, j * CH:j * CH + CH],
                                           start=k == 0, stop=k == 1)
                    ins.then_inc(den_done, 1)
                    if more:
                        max_row(g + 1)

                with e.Fori(0, NU - 1) as u:
                    unit(e.snap(im * NU + u), u, True)
                unit(e.snap(im * NU + NU - 1), NU - 1, False)


def _attention1(nc, keep, x_in, w, x_out):
    NPART = 4
    PW = NT // NPART
    NP = 4
    LAG = 2
    with ExitStack() as ctx:
        sb = lambda n, s, d=F32: ctx.enter_context(nc.sbuf_tensor("a1_" + n, s, d))
        sem = lambda n: keep.enter_context(nc.semaphore("a1_" + n))
        xa = sb("xa", [C + 1, NT])
        xr = sb("xr", [128, NT // 2])
        wqk = sb("wqk", [C + 1, 2, 128])
        wv = sb("wv", [C + 1, C])
        raw = sb("raw", [128, 2, 2, CH])
        qs = sb("qs", [128, NT], F16)
        ks = sb("ks", [128, NT], F16)
        v = sb("v", [128, KT, C])
        p = sb("p", [128, NP, NT])
        nm = sb("nm", [128, NP, NPART])
        nrow = sb("nrow", [128, NP])
        z = sb("z", [128, NP, NPART])
        f = sb("f", [128, NP, NPART])
        fz = sb("fz", [128, NP, NPART])
        zrow = sb("zrow", [128, NP])
        rz = sb("rz", [128, NP])
        gain = sb("gain", [128, NP, NPART])
        vs = sb("vs", [128, NP, NPART, C])
        res = sb("res", [128, NT // 2])
        acc = ctx.enter_context(nc.psum_tensor("a1_acc", [128, 4, CH], F32))
        s_ps = ctx.enter_context(nc.psum_tensor("a1_s_ps", [128, 2, 2, CH], F32))

        w_loaded = sem("w_loaded")
        xa_loaded, xr_loaded, ones_done = sem("xa_loaded"), sem("xr_loaded"), sem("ones_done")
        proj_done, raw_done, hi_done, split_done = sem("proj_done"), sem("raw_done"), sem("hi_done"), sem("split_done")
        vproj_done, v_done = sem("vproj_done"), sem("v_done")
        s_done, nm_done, exp_done = sem("s_done"), sem("nm_done"), sem("exp_done")
        nrow_done, f_done, scale_done, vs_done = sem("nrow_done"), sem("f_done"), sem("scale_done"), sem("vs_done")
        pv_done, res_done, stored = sem("pv_done"), sem("res_done"), sem("stored")
        block = ctx.enter_context(nc.Block())
        GV = KT // 8
        NSPLIT = 3 * NCH

        @block.sync
        def _(e):
            xin_v = x_in.rearrange("i c (h n) -> h i c n", h=2)
            xout_v = x_out.rearrange("i c (h n) -> h i c n", h=2)
            e.sem_inc(stored, 1)

            def load_xa(im):
                e.dma_start(xa[0:C, :], x_in[bass.ds(im, 1)].rearrange("a c n -> (a c) n")).then_inc(xa_loaded, 16)

            def load_xr(im):
                for h in range(2):
                    e.dma_start(xr[64 * h:64 * h + 64], xin_v[h][bass.ds(im, 1)].rearrange("i c n -> (i c) n"))\
                        .then_inc(xr_loaded, 16)

            def store(im):
                e.wait_ge(res_done, im * 4 + 4 + 4)
                for h in range(2):
                    e.dma_start(xout_v[h][bass.ds(im, 1)].rearrange("i c n -> (i c) n"),
                                res[64 * h:64 * h + 64]).then_inc(stored, 16)

            e.dma_start(wqk[:], w["wqk1"]).then_inc(w_loaded, 16)
            e.dma_start(wv[:], w["wv1"]).then_inc(w_loaded, 16)
            load_xa(0)
            load_xr(0)
            with e.Fori(0, NI - 1) as im:
                e.wait_ge(vproj_done, im * GV + GV)
                load_xa(im + 1)
                store(im)
                load_xr(im + 1)
            store(NI - 1)
            e.wait_ge(stored, NI * 32 + 1)

        @block.gpsimd
        def _(e):
            with e.Fori(0, NI) as im:
                for ch in range(NCH):
                    cs = slice(ch * CH, ch * CH + CH)
                    e.wait_ge(hi_done, im * NCH + ch + 1)
                    for j, (qk, r, n) in enumerate(((qs, 64, 64), (ks, 32, 32), (ks, 96, 32))):
                        e.tensor_tensor(qk[r:r + n, cs], raw[r:r + n, ch % 2, min(j, 1)], qk[r:r + n, cs],
                                        ALU.subtract).then_inc(split_done, 1)
                        e.wait_ge(split_done, im * NSPLIT + ch * 3 + j + 1)

        @block.scalar
        def _(e):
            e.sem_inc(exp_done, 2)

            def part(t, slot, c):
                e.wait_ge(nm_done, t * NPART + c + 1)
                if c == 0:
                    e.wait_ge(pv_done, t + 1)
                e.activation(p[:, slot, c * PW:c * PW + PW], s_ps[:, c % 2].rearrange("p a n -> p (a n)"),
                             ACT.Exp, bias=nm[:, slot, c:c + 1], accum_out=z[:, slot, c:c + 1])\
                    .then_inc(exp_done, 1)

            def rescale(t, slot):
                e.wait_ge(nrow_done, t + 1)
                e.activation(f[:, slot], nm[:, slot], ACT.Exp, bias=nrow[:, slot:slot + 1], scale=-1.0)\
                    .then_inc(f_done, 1)

            with e.Fori(0, NI) as im:
                for ch in range(NCH):
                    cs = slice(ch * CH, ch * CH + CH)
                    e.wait_ge(raw_done, im * NCH + ch + 1)
                    e.activation(qs[:, cs], raw[:, ch % 2, 0], ACT.Copy)
                    e.activation(ks[:, cs], raw[:, ch % 2, 1], ACT.Copy).then_inc(hi_done, 1)
                with e.Fori(0, KT // NP) as i:
                    t = e.snap(im * KT + i * NP)
                    for slot in range(NP):
                        for c in range(NPART):
                            part(t + slot, slot, c)
                        rescale(t + slot, slot)

        @block.vector
        def _(e):
            e.memset(xa[C:C + 1, :], 1.0).then_inc(ones_done, 1)
            e.sem_inc(res_done, 4)

            def scale_v(t, slot, kt, k):
                if k == 0:
                    e.wait_ge(f_done, t + 1)
                    ins = e.tensor_tensor(fz[:, slot], f[:, slot], z[:, slot], ALU.mult)
                elif k == 1:
                    ins = e.reduce_sum(zrow[:, slot:slot + 1], fz[:, slot], AXX)
                elif k == 2:
                    ins = e.reciprocal(rz[:, slot:slot + 1], zrow[:, slot:slot + 1])
                elif k == 3:
                    ins = e.tensor_scalar(gain[:, slot], f[:, slot], rz[:, slot:slot + 1], None, ALU.mult)
                else:
                    ins = e.tensor_tensor(vs[:, slot], v[:, bass.ds(kt, 1)].broadcast_to([128, NPART, C]),
                                          gain[:, slot].unsqueeze(2).broadcast_to([128, NPART, C]), ALU.mult)
                ins.then_inc(vs_done, 1)
                if k < 4:
                    e.wait_ge(vs_done, t * 5 + k + 1)

            def step(t, slot, kt, before, now):
                for c in range(NPART):
                    if before and c >= 1:
                        scale_v(t - 1, (slot - 1) % NP, kt - 1, c - 1)
                    if now:
                        e.wait_ge(s_done, t * NPART + c + 1)
                        e.reduce_max(nm[:, slot, c:c + 1], s_ps[:, c % 2].rearrange("p a n -> p (a n)"), AXX,
                                     negate=True).then_inc(nm_done, 1)
                if now:
                    e.wait_ge(nm_done, t * NPART + NPART)
                    e.tensor_reduce(nrow[:, slot:slot + 1], nm[:, slot], AXX, ALU.min).then_inc(nrow_done, 1)
                if before:
                    for k in (3, 4):
                        if k == 4:
                            e.wait_ge(pv_done, t - 1 + 1)
                        scale_v(t - 1, (slot - 1) % NP, kt - 1, k)

            with e.Fori(0, NI) as im:
                for ch in range(NCH):
                    e.wait_ge(proj_done, im * NCH + ch + 1)
                    if ch >= 2:
                        e.wait_ge(split_done, im * NSPLIT + 3 * ch - 3)
                    e.tensor_copy(raw[:, ch % 2], s_ps[:, ch % 2]).then_inc(raw_done, 1)
                for gv in range(GV):
                    e.wait_ge(vproj_done, im * GV + gv + 1)
                    e.tensor_copy(v[:, 8 * gv:8 * gv + 8].rearrange("p a c -> p (a c)"), s_ps[:, gv % 2, 0])\
                        .then_inc(v_done, 1)
                e.wait_ge(v_done, im * GV + GV)
                t = e.snap(im * KT)
                for slot in range(NP):
                    step(t + slot, slot, slot, slot > 0, True)
                with e.Fori(1, KT // NP) as i:
                    t = e.snap(im * KT + i * NP)
                    for slot in range(NP):
                        step(t + slot, slot, i * NP + slot, True, True)
                step(im * KT + KT, 0, KT, True, False)
                e.wait_ge(pv_done, im * KT + KT + NP)
                e.wait_ge(xr_loaded, im * 32 + 32)
                e.wait_ge(stored, im * 32 + 1)
                for b in range(4):
                    e.tensor_tensor(res[:, b * CH:b * CH + CH], acc[:, b], xr[:, b * CH:b * CH + CH], ALU.add)\
                        .then_inc(res_done, 1)

        @block.tensor
        def _(e):
            e.sem_inc(pv_done, NP)
            e.wait_ge(w_loaded, 32)
            e.wait_ge(ones_done, 1)

            def step(t, slot, kt, now, before, first=False, last=False):
                old = (slot - LAG) % NP
                for c in range(NPART):
                    if now:
                        e.wait_ge(exp_done, t * NPART + c + 1)
                        for j in range(2):
                            n0 = c * PW + j * CH
                            ins = e.matmul(s_ps[:, c % 2, j], ks[:, bass.ds(kt * 128, 128)], qs[:, n0:n0 + CH],
                                           start=True, stop=True)
                        ins.then_inc(s_done, 1)
                    if before:
                        if c == 0:
                            e.wait_ge(vs_done, (t - LAG) * 5 + 5)
                        for h in range(2):
                            n = h * 4 + c
                            ins = e.matmul(acc[64 * h:64 * h + 64, c], vs[:, old, n // 2],
                                           p[:, old, n * CH:n * CH + CH], start=first, stop=last)
                        if c == NPART - 1:
                            ins.then_inc(pv_done, 1)

            with e.Fori(0, NI) as im:
                e.wait_ge(xa_loaded, im * 16 + 16)
                e.wait_ge(exp_done, im * (KT * NPART) + 2)
                for ch in range(NCH):
                    if ch >= 2:
                        e.wait_ge(raw_done, im * NCH + ch - 1)
                    for j in range(2):
                        ins = e.matmul(s_ps[:, ch % 2, j], wqk[:, j], xa[:, ch * CH:ch * CH + CH],
                                       start=True, stop=True)
                    ins.then_inc(proj_done, 1)
                for gv in range(GV):
                    if gv >= 2:
                        e.wait_ge(v_done, im * GV + gv - 1)
                    else:
                        e.wait_ge(raw_done, im * NCH + NCH - 1 + gv)
                    for i in range(8):
                        t = gv * 8 + i
                        ins = e.matmul(s_ps[:, gv % 2, 0, i * C:i * C + C], xa[:, t * 128:t * 128 + 128],
                                       wv[:], start=True, stop=True)
                    ins.then_inc(vproj_done, 1)
                e.wait_ge(split_done, im * NSPLIT + NSPLIT)
                e.wait_ge(v_done, im * GV + GV)
                e.wait_ge(res_done, im * 4 + 4)
                t = e.snap(im * KT)
                for slot in range(NP):
                    step(t + slot, slot, slot, True, slot >= LAG, first=slot == LAG)
                with e.Fori(1, KT // NP) as i:
                    t = e.snap(im * KT + i * NP)
                    for slot in range(NP):
                        step(t + slot, slot, i * NP + slot, True, True)
                t = e.snap(im * KT + KT)
                for slot in range(LAG):
                    step(t + slot, slot, KT + slot, False, True, last=slot == LAG - 1)


def _swin(nc, keep, name, x_in, w, x_out, shifted):
    NC = 4
    NW = 8
    NH, HD, WT = 8, 8, 64
    SCALE = HD ** -0.5
    EPS = 1e-5
    OC = 2 * (HD + 1)
    LN = ["norm1", "norm2"] if shifted else ["pe", "norm1", "norm2"]
    L = len(LN)
    COL = {n: i for i, n in enumerate(["pe_g", "pe_b", "norm1_g", "norm1_b", "norm2_g", "norm2_b",
                                       "q_b", "k_b", "proj_b", "fc1_b", "fc2_b"])}
    NV = 4 if shifted else 1
    with ExitStack() as ctx:
        sb = lambda n, s, d=F32: ctx.enter_context(nc.sbuf_tensor(f"{name}_{n}", s, d))
        sem = lambda n: keep.enter_context(nc.semaphore(f"{name}_{n}"))
        ps = lambda n, s: ctx.enter_context(nc.psum_tensor(f"{name}_{n}", s, F32))
        x = sb("x", [128, CH])
        t = x if shifted else sb("t", [128, CH])
        cols = sb("cols", [128, len(COL)])
        wqk = sb("wqk", [128, 2, 128])
        wv = sb("wv", [128, C])
        vb = sb("vb", [128, C])
        wp = sb("wp", [C, C])
        w1 = sb("w1", [128, 128])
        w2 = sb("w2", [128, C])
        mean_w = sb("mean_w", [128, 128])
        ident = sb("ident", [128, 128])
        hmask = sb("hmask", [128, NH])
        rel = sb("rel", [128, NH, WT])
        mask = sb("mask", [128, NV, 2, WT])
        bias = sb("bias", [128, NV, 2, NH, WT])
        xc = sb("xc", [128, 2, CH])
        sq = sb("sq", [128, CH])
        rstd = sb("rstd", [128, 2, 4, 2])
        half = sb("half", [128, 2])
        var = sb("var", [128, 2, 4, 2])
        half_w = sb("half_w", [128, 2])
        xn = sb("xn", [128, CH])
        hw = sb("hw", [128, NW, WT])
        q = sb("q", [128, NW, WT])
        k = sb("k", [128, NW, WT])
        kb = sb("kb", [128, 2, NH, WT])
        v = sb("v", [128, 2, NW, 4, 2, HD + 1])
        s1 = sb("s1", [128, 2, NH, WT])
        nmx = sb("nmx", [128, 2, NH])
        s2 = sb("s2", [128, 2, NH, WT])
        p = sb("p", [128, 2, NH * WT])
        pt = sb("pt", [128, 2, 4, 128])
        rz = sb("rz", [128, 2, 32])
        o = sb("o", [128, NW, C])
        ot = sb("ot", [C, 2, NW, WT])
        yb = sb("yb", [128, CH])
        x2 = sb("x2", [128, CH])
        h2 = sb("h2", [128, CH])
        g = sb("g", [128, 2, CH])
        xo = sb("xo", [128, CH])
        lin = ps("lin", [128, 2, CH])
        s_ps = ps("s_ps", [128, 2, CH])
        pt_ps = ps("pt_ps", [128, 2, CH])
        o_ps = ps("o_ps", [128, 2, CH])

        (w_loaded, const_done, x_loaded, st_done, xc_done, sq_done, rs_done, var_done, xn_done, y_done, qk_ps, qk_done,
         v_ps, v_done, kb_done, s_done, s1_done, nmx_done, s2_done, e_done, tp_done, pt_done, pv_done, rz_done,
         o_done, ot_ps, ot_done, proj_ps, yb_done, x2_done, fc1_ps, g_done, fc2_ps, xo_done, stored, passed) = [
            sem(n) for n in ("w_loaded", "const_done", "x_loaded", "st_done", "xc_done", "sq_done", "rs_done", "var_done",
                             "xn_done", "y_done", "qk_ps", "qk_done", "v_ps", "v_done", "kb_done", "s_done",
                             "s1_done", "nmx_done", "s2_done", "e_done", "tp_done", "pt_done", "pv_done",
                             "rz_done", "o_done", "ot_ps", "ot_done", "proj_ps", "yb_done", "x2_done",
                             "fc1_ps", "g_done", "fc2_ps", "xo_done", "stored", "passed")]
        block = ctx.enter_context(nc.Block())
        NCHUNK = NI * NC

        def own_wait(e):
            e.sem_inc(passed, 1)

        col = lambda n: cols[:, COL[n]:COL[n] + 1]
        loads = [(cols, "cols"), (wqk, "wqk2"), (wv, "wv2"), (vb, "vb2"), (wp, "wp2"), (w1, "w12"), (w2, "w22"),
                 (mean_w, "mean_w"), (half_w, "half_w"), (ident, "ident"), (hmask, "hmask"), (rel, "rel"), (mask, "mask")]
        XD = 4 if shifted else 2

        @block.sync
        def _(e):
            for dst, n in loads:
                src = w[n] if n != "mask" else w[n][:, 0:NV]
                e.dma_start(dst[:], src).then_inc(w_loaded, 16)
            e.sem_inc(x2_done, 1)
            e.sem_inc(stored, 1)

            def pieces(dram, sbt, im, c):
                for h in range(2):
                    sh = sbt[64 * h:64 * h + 64, :].rearrange("p (r c) -> p r c", c=WW)
                    if not shifted:
                        rows = dram[bass.ds(im, 1), :, bass.ds(c * 8 + h * 32, 8)].rearrange("a c r w -> (a c) r w")
                        yield rows, sh
                    else:
                        rows = dram[bass.ds(im, 1), :, bass.ds(c * 8 + (h * 32 + 4), 8)]\
                            .rearrange("a c r w -> (a c) r w")
                        yield rows[:, :, 4:WW], sh[:, :, 0:WW - 4]
                        yield rows[:, :, 0:4], sh[:, :, WW - 4:WW]

            with e.Fori(0, NI) as im:
                with e.Fori(0, NC) as c:
                    it = e.snap(im * NC + c)
                    e.wait_ge(x2_done, it + 1)
                    for dram, sbt in pieces(x_in, x, im, c):
                        e.dma_start(sbt, dram).then_inc(x_loaded, 16)
                    e.wait_ge(xo_done, it + 1)
                    for dram, sbt in pieces(x_out, xo, im, c):
                        e.dma_start(dram, sbt).then_inc(stored, 16)
            e.wait_ge(stored, NCHUNK * XD * 16 + 1)

        @block.gpsimd
        def _(e):
            e.wait_ge(w_loaded, 16 * len(loads))
            e.wait_ge(const_done, 1)

            def norm(it, l):
                e.wait_ge(var_done, it * L + l + 1)
                e.tensor_tensor(rstd[:, l % 2], var[:, l % 2], half[:, 0:1].unsqueeze(2).broadcast_to([128, 4, 2]), ALU.pow)\
                    .then_inc(rs_done, 1)

            with e.Fori(0, NCHUNK) as it:
                for l in range(L - 1):
                    norm(it, l)
                for i in range(NW):
                    if i == 0:
                        e.wait_ge(qk_done, it * 2 + 2)
                    e.wait_ge(s_done, it * NW + i + 1)
                    e.tensor_tensor(kb[:, i % 2], k[:, i:i + 1].broadcast_to([128, NH, WT]),
                                    hmask[:].unsqueeze(2).broadcast_to([128, NH, WT]), ALU.mult)\
                        .then_inc(kb_done, 1)
                norm(it, L - 1)

        @block.scalar
        def _(e):
            e.sem_inc(e_done, 2)
            e.sem_inc(g_done, 1)
            e.wait_ge(w_loaded, 16 * len(loads))

            def norm(it, l):
                e.wait_ge(xc_done, it * L + l + 1)
                e.activation(sq[:], xc[:, l % 2], ACT.Square).then_inc(sq_done, 1)
                e.wait_ge(st_done, it * (3 * L) + 3 * l + 2)
                e.activation(var[:, l % 2].rearrange("p a h -> p (a h)"), lin[:, 1, 0:8], ACT.Copy, bias=EPS).then_inc(var_done, 1)
                e.wait_ge(xn_done, it * L + l + 1)
                if LN[l] == "norm1":
                    out = hw[:].rearrange("p w (r c) -> p r w c", c=8)
                    src = xn[:].rearrange("p (r w c) -> p r w c", w=NW, c=8)
                else:
                    out, src = (t if LN[l] == "pe" else h2)[:], xn[:]
                e.activation(out, src, ACT.Identity, scale=col(LN[l] + "_g"), bias=col(LN[l] + "_b"))\
                    .then_inc(y_done, 1)

            def transposed(it, i):
                e.wait_ge(tp_done, it * NW + i + 1 + 2)
                e.wait_ge(pv_done, it * NW + i + 1)
                e.activation(pt[:, i % 2].rearrange("p a n -> p (a n)"), pt_ps[:, i % 2], ACT.Copy)\
                    .then_inc(pt_done, 1)

            with e.Fori(0, NCHUNK) as it:
                for l in range(L - 1):
                    norm(it, l)
                for i in range(NW):
                    e.wait_ge(s2_done, it * NW + i + 1)
                    e.wait_ge(tp_done, it * NW + i + 1)
                    e.activation(p[:, i % 2], s2[:, i % 2].rearrange("p h m -> p (h m)"), ACT.Exp)\
                        .then_inc(e_done, 1)
                    if i:
                        transposed(it, i - 1)
                transposed(it, NW - 1)
                for b in range(2):
                    e.wait_ge(ot_ps, it * 2 + b + 1)
                    e.activation(ot[:, :, 4 * b:4 * b + 4].rearrange("p h w n -> p w h n"),
                                 s_ps[0:C, b].rearrange("p (w h n) -> p w h n", w=4, h=2), ACT.Copy)\
                        .then_inc(ot_done, 1)
                e.wait_ge(proj_ps, it + 1)
                e.activation(yb[:].rearrange("p (r w c) -> p w r c", w=NW, c=8),
                             lin[:, 0].rearrange("p (w r c) -> p w r c", w=NW, c=8), ACT.Identity,
                             bias=col("proj_b")).then_inc(yb_done, 1)
                norm(it, L - 1)
                for h in range(2):
                    e.wait_ge(fc1_ps, it * 2 + h + 1)
                    e.activation(g[:, h], lin[:, h], ACT.Gelu, bias=col("fc1_b")).then_inc(g_done, 1)

        @block.vector
        def _(e):
            e.memset(half[:], -0.5).then_inc(const_done, 1)
            e.memset(v[:], 0.0).then_inc(const_done, 1)
            e.wait_ge(const_done, 2)
            for par in range(2):
                e.memset(v[64 * par:64 * par + 64, :, :, :, par, HD:HD + 1], 1.0).then_inc(const_done, 1)
            e.wait_ge(w_loaded, 16 * len(loads))
            for a in range(NV):
                for b in range(2):
                    e.tensor_tensor(bias[:, a, b], rel[:], mask[:, a, b:b + 1].broadcast_to([128, NH, WT]), ALU.add)\
                        .then_inc(const_done, 1)
            e.wait_ge(const_done, 4 + 2 * NV)

            def norm(it, l):
                src = x if l == 0 else (t if l < L - 1 else x2)
                e.wait_ge(st_done, it * (3 * L) + 3 * l + 1)
                e.tensor_tensor(xc[:, l % 2], src[:], lin[:, 0], ALU.subtract).then_inc(xc_done, 1)
                e.wait_ge(st_done, it * (3 * L) + 3 * l + 3)
                e.tensor_tensor(xn[:], xc[:, l % 2], lin[:, 1], ALU.mult).then_inc(xn_done, 1)

            def chunk(it, c):
                e.wait_ge(x_loaded, it * (16 * XD) + 16 * XD)
                for l in range(L - 1):
                    norm(it, l)
                e.wait_ge(qk_ps, it * 2 + 1)
                e.tensor_scalar(q[:].rearrange("p w n -> p (w n)"), lin[:, 0], col("q_b"), SCALE, ALU.add, ALU.mult)\
                    .then_inc(qk_done, 1)
                e.wait_ge(qk_ps, it * 2 + 2)
                e.tensor_scalar(k[:].rearrange("p w n -> p (w n)"), lin[:, 1], col("k_b"), None, ALU.add)\
                    .then_inc(qk_done, 1)
                for h in range(2):
                    e.wait_ge(v_ps, it * 2 + h + 1)
                    for par in range(2):
                        r = slice(64 * par, 64 * par + 64)
                        e.tensor_tensor(
                            v[r, h, :, :, par, 0:HD],
                            lin[r, h].rearrange("p (w a b d) -> p w a b d", w=NW, b=2, d=HD)[:, :, :, par],
                            vb[r].rearrange("p (a b d) -> p a b d", b=2, d=HD)[:, :, par].unsqueeze(1)
                            .broadcast_to([64, NW, 4, HD]), ALU.add).then_inc(v_done, 1)
                for i in range(NW):
                    e.wait_ge(s_done, it * NW + i + 1 + 2)
                    if shifted:
                        b = bias[:, bass.ds(c, 1), i // (NW - 1)].rearrange("p a h m -> p (a h) m")
                    else:
                        b = bias[:, 0, 0]
                    e.tensor_tensor(s1[:, i % 2], s_ps[:, i % 2].rearrange("p (h m) -> p h m", h=NH), b, ALU.add)\
                        .then_inc(s1_done, 1)
                    e.wait_ge(s1_done, it * NW + i + 1)
                    e.reduce_max(nmx[:, i % 2], s1[:, i % 2], AXX, negate=True).then_inc(nmx_done, 1)
                    e.wait_ge(nmx_done, it * NW + i + 1)
                    e.wait_ge(e_done, it * NW + i + 1)
                    e.tensor_tensor(s2[:, i % 2], s1[:, i % 2], nmx[:, i % 2].unsqueeze(2)
                                    .broadcast_to([128, NH, WT]), ALU.add).then_inc(s2_done, 1)
                for b in range(2):
                    e.wait_ge(pv_done, it * NW + 4 * b + 4 + 2)
                    ob = o_ps[:, b, 0:4 * 4 * OC].rearrange("p (a b d) -> p a b d", b=2, d=HD + 1)
                    e.reciprocal(rz[:, b].rearrange("p (a b) -> p a b", b=2), ob[:, :, :, HD]).then_inc(rz_done, 1)
                    e.wait_ge(rz_done, it * 2 + b + 1)
                    e.tensor_tensor(o[:, 4 * b:4 * b + 4].rearrange("p w (a b d) -> p (w a) b d", b=2, d=HD),
                                    ob[:, :, :, 0:HD],
                                    rz[:, b].rearrange("p (a b) -> p a b", b=2).unsqueeze(3)
                                    .broadcast_to([128, 16, 2, HD]), ALU.mult).then_inc(o_done, 1)
                e.wait_ge(yb_done, it + 1)
                e.tensor_tensor(x2[:], t[:], yb[:], ALU.add).then_inc(x2_done, 1)
                norm(it, L - 1)
                e.wait_ge(fc2_ps, it + 1)
                e.wait_ge(stored, it * (16 * XD) + 1)
                e.scalar_tensor_tensor(xo[:], pt_ps[:, 0], col("fc2_b"), x2[:], ALU.add, ALU.add)\
                    .then_inc(xo_done, 1)

            with e.Fori(0, NI) as im:
                with e.Fori(0, NC) as c:
                    chunk(e.snap(im * NC + c), c)

        @block.tensor
        def _(e):
            e.sem_inc(s_done, 2)
            e.sem_inc(tp_done, 2)
            e.sem_inc(pv_done, 2)
            e.wait_ge(w_loaded, 16 * len(loads))
            e.wait_ge(const_done, 4 + 2 * NV)

            def norm(it, l):
                src = x if l == 0 else (t if l < L - 1 else x2)
                if l == 0:
                    e.wait_ge(x_loaded, it * (16 * XD) + 16 * XD)
                    e.wait_ge(g_done, it * 2 + 1)
                elif l < L - 1:
                    e.wait_ge(y_done, it * L + l)
                else:
                    e.wait_ge(x2_done, it + 1 + 1)
                e.matmul(lin[:, 0], mean_w[:], src[:], start=True, stop=True).then_inc(st_done, 1)
                e.wait_ge(sq_done, it * L + l + 1)
                for a in range(4):
                    ins = e.matmul(lin[:, 1, 2 * a:2 * a + 2], sq[:, a * 128:a * 128 + 128], half_w[:],
                                   start=True, stop=True)
                ins.then_inc(st_done, 1)
                e.wait_ge(rs_done, it * L + l + 1)
                for a in range(4):
                    for h in range(2):
                        ins = e.matmul(lin[64 * h:64 * h + 64, 1, a * 128:a * 128 + 128],
                                       rstd[:, l % 2, a, h:h + 1].broadcast_to([128, 64]), ident[:],
                                       start=True, stop=True)
                ins.then_inc(st_done, 1)

            def scores(it, i):
                e.wait_ge(kb_done, it * NW + i + 1)
                if i >= 2:
                    e.wait_ge(s1_done, it * NW + i - 1)
                own_wait(e)
                for h in range(2):
                    r = slice(64 * h, 64 * h + 64)
                    ins = e.matmul(s_ps[r, i % 2], q[r, i], kb[r, i % 2].rearrange("p h m -> p (h m)"),
                                   start=True, stop=True)
                ins.then_inc(s_done, 1)

            def transposes(it, i):
                e.wait_ge(e_done, it * NW + i + 1 + 2)
                if i >= 2:
                    e.wait_ge(pt_done, it * NW + i - 1)
                for a in range(4):
                    ins = e.transpose(pt_ps[:, i % 2, a * 128:a * 128 + 128], p[:, i % 2, a * 128:a * 128 + 128],
                                      ident[:])
                ins.then_inc(tp_done, 1)

            def products(it, i):
                e.wait_ge(pt_done, it * NW + i + 1)
                for a in range(4):
                    for h in range(2):
                        o0 = (i % 4) * 4 * OC + a * OC
                        ins = e.matmul(o_ps[64 * h:64 * h + 64, i // 4, o0:o0 + OC], pt[:, i % 2, a, 64 * h:64 * h + 64],
                                       v[:, h, i, a].rearrange("p b d -> p (b d)"), start=True, stop=True)
                ins.then_inc(pv_done, 1)

            with e.Fori(0, NCHUNK) as it:
                for l in range(L - 1):
                    norm(it, l)
                e.wait_ge(y_done, it * L + L - 1)
                for j in range(2):
                    e.matmul(lin[:, j], wqk[:, j], hw[:].rearrange("p w n -> p (w n)"), start=True, stop=True)\
                        .then_inc(qk_ps, 1)
                for h in range(2):
                    e.wait_ge(qk_done, it * 2 + h + 1)
                    own_wait(e)
                    r = slice(64 * h, 64 * h + 64)
                    for i in range(NW):
                        for par in range(2):
                            ins = e.matmul(lin[64 * par:64 * par + 64, h, i * C:i * C + C], hw[r, i], wv[r],
                                           start=True, stop=True)
                    ins.then_inc(v_ps, 1)
                for i in range(NW + 2):
                    if i < NW:
                        scores(it, i)
                    if 1 <= i <= NW:
                        transposes(it, i - 1)
                    if i >= 2:
                        if i == 2:
                            e.wait_ge(v_done, it * 4 + 4)
                        products(it, i - 2)
                for b in range(2):
                    e.wait_ge(o_done, it * 2 + b + 1)
                    own_wait(e)
                    for i in range(4 * b, 4 * b + 4):
                        ins = e.transpose(s_ps[0:C, b, (i % 4) * 128:(i % 4) * 128 + 128], o[:, i], ident[:])
                    ins.then_inc(ot_ps, 1)
                e.wait_ge(ot_done, it * 2 + 2)
                own_wait(e)
                for h in range(2):
                    ins = e.matmul(lin[64 * h:64 * h + 64, 0], wp[:], ot[:, h].rearrange("p w n -> p (w n)"),
                                   start=True, stop=True)
                ins.then_inc(proj_ps, 1)
                norm(it, L - 1)
                e.wait_ge(y_done, it * L + L)
                for h in range(2):
                    r = slice(64 * h, 64 * h + 64)
                    e.matmul(lin[:, h], w1[r], h2[r], start=True, stop=True).then_inc(fc1_ps, 1)
                for h in range(2):
                    e.wait_ge(g_done, it * 2 + h + 1 + 1)
                    ins = e.matmul(pt_ps[64 * h:64 * h + 64, 0], w2[:], g[:, h], start=True, stop=True)
                ins.then_inc(fc2_ps, 1)


def _adaptive_blur(nc, keep, x_in, w, x_out):
    TS = NT // 128
    HT = TS // 2
    ND = 5
    NB = 8
    HID = 32
    NTAP = 81
    with ExitStack() as ctx:
        sb = lambda n, s, d=F32: ctx.enter_context(nc.sbuf_tensor("bl_" + n, s, d))
        sem = lambda n: keep.enter_context(nc.semaphore("bl_" + n))
        ps = lambda n, s: ctx.enter_context(nc.psum_tensor("bl_" + n, s, F32))
        x = sb("x", [128, NT // 2])
        w1 = sb("w1", [128, HID])
        b1 = sb("b1", [HID, 1])
        w2 = sb("w2", [HID, 1])
        b2 = sb("b2", [128, 1])
        taps = sb("taps", [NTAP, 1])
        ntaps = sb("ntaps", [NTAP, 1])
        dist = sb("dist", [128, ND, 128])
        ndist = sb("ndist", [128, ND * 128])
        ident = sb("ident", [128, 128])
        fold = sb("fold", [128, 128])
        ones = sb("ones", [NTAP, 1])
        hid = sb("hid", [HID, NT])
        kc = sb("kc", [128, 4, TS])
        sc = sb("sc", [128, TS])
        s = sb("s", [128, (TS + 4) * 128])
        e81 = sb("e81", [NTAP, 2, CH])
        rzc = sb("rzc", [128, TS])
        xt = sb("xt", [128, HT, 128])
        lg = sb("lg", [128, 2, ND * 128])
        f = sb("f", [128, NB, ND * 128])
        rz = sb("rz", [128, 2, CH])
        low = sb("low", [128, 2, CH])
        enh = sb("enh", [128, NT // 2])
        cen = sb("cen", [128, NT // 2])
        sq = sb("sq", [128, NT // 2])
        out = sb("out", [128, NT // 2])
        stat = sb("stat", [128, 4])
        half = sb("half", [128, 1])
        ring = ps("ring", [128, 2, CH])
        acc = ps("acc", [128, 2, CH])
        rz_ps = ps("rz_ps", [128, 2, CH])
        small = ps("small", [128, CH])

        names = ("w_loaded", "const_done", "x_loaded", "h_ps", "h_done", "ks_ps", "kc_done", "sc_done", "sbc_ps",
                 "sbc_done", "e81_done", "z_ps", "rzc_done", "xt_ps", "xt_done", "lg_done", "f_done", "acc_done",
                 "rz_ps_done", "rz_done", "low_done", "enh_done", "sum_done", "mean_ps", "cen_done", "ssq_done",
                 "var_ps", "var_done", "rstd_done", "out_done", "stored", "passed")
        (w_loaded, const_done, x_loaded, h_ps, h_done, ks_ps, kc_done, sc_done, sbc_ps, sbc_done, e81_done, z_ps,
         rzc_done, xt_ps, xt_done, lg_done, f_done, acc_done, rz_ps_done, rz_done, low_done, enh_done, sum_done,
         mean_ps, cen_done, ssq_done, var_ps, var_done, rstd_done, out_done, stored, passed) = [sem(n) for n in names]
        block = ctx.enter_context(nc.Block())
        NG = NCH
        loads = [(w1, "b_w1"), (b1, "b_b1"), (w2, "b_w2"), (b2, "b_b2"), (taps, "b_taps"), (dist, "b_dist"),
                 (ident, "ident"), (fold, "b_fold")]
        NLOAD = 16 * len(loads)

        def at(g):
            return slice(64 * (g // 4), 64 * (g // 4) + 64), slice((g % 4) * CH, (g % 4) * CH + CH)

        def alone(e):
            e.sem_inc(passed, 1)

        @block.sync
        def _(e):
            for dst, n in loads:
                e.dma_start(dst[:], w[n]).then_inc(w_loaded, 16)
            e.sem_inc(enh_done, 1)
            e.sem_inc(stored, 1)
            with e.Fori(0, NI) as im:
                e.wait_ge(enh_done, im * NG + 1)
                for h in range(2):
                    e.dma_start(x[64 * h:64 * h + 64],
                                x_in[bass.ds(im, 1), :, h * (NT // 2):(h + 1) * (NT // 2)]
                                .rearrange("a c n -> (a c) n")).then_inc(x_loaded, 16)
                e.wait_ge(out_done, im + 1)
                for h in range(2):
                    e.dma_start(x_out[bass.ds(im, 1), :, h * (NT // 2):(h + 1) * (NT // 2)]
                                .rearrange("a c n -> (a c) n"), out[64 * h:64 * h + 64]).then_inc(stored, 16)
            e.wait_ge(stored, NI * 32 + 1)

        @block.gpsimd
        def _(e):
            e.wait_ge(const_done, 4)
            with e.Fori(0, NI) as im:
                e.wait_ge(var_done, im + 1)
                e.tensor_tensor(stat[:, 3:4], stat[:, 2:3], half[:], ALU.pow).then_inc(rstd_done, 1)

        @block.scalar
        def _(e):
            e.wait_ge(w_loaded, NLOAD)
            e.wait_ge(const_done, 6)
            with e.Fori(0, NI) as im:
                for g in range(NG):
                    e.wait_ge(h_ps, im * NG + g + 1)
                    e.activation(hid[:, g * CH:g * CH + CH], ring[0:HID, g % 2], ACT.Relu, bias=b1[:])\
                        .then_inc(h_done, 1)
                for g in range(NG):
                    e.wait_ge(sbc_ps, im * NG + g + 1)
                    if g >= 2:
                        e.wait_ge(z_ps, im * NG + g - 1)
                    e.activation(s[:, (2 * 128) + g * CH:(2 * 128) + g * CH + CH], ring[:, g % 2], ACT.Copy)\
                        .then_inc(sbc_done, 1)
                    e.activation(e81[:, g % 2], ring[0:NTAP, g % 2], ACT.Exp, scale=ntaps[:]).then_inc(e81_done, 1)

                def spread(g):
                    r, _ = at(g)
                    e.wait_ge(rz_ps_done, im * NG + g + 1)
                    if g >= 2:
                        e.wait_ge(low_done, im * NG + g - 1)
                    e.activation(rz[r, g % 2], rz_ps[r, g % 2], ACT.Copy).then_inc(rz_done, 1)

                for t in range(TS):
                    e.wait_ge(lg_done, im * TS + t + 1)
                    if t >= NB:
                        e.wait_ge(acc_done, im * TS + t - NB + 3)
                    e.activation(f[:, t % NB], lg[:, t % 2], ACT.Exp).then_inc(f_done, 1)
                    if t % 4 == 3:
                        spread(t // 4)
                e.wait_ge(cen_done, im + 1)
                e.activation(sq[:], cen[:], ACT.Square, accum_out=stat[:, 1:2]).then_inc(ssq_done, 1)

        @block.vector
        def _(e):
            e.memset(half[:], -0.5).then_inc(const_done, 1)
            e.memset(ones[:], 1.0).then_inc(const_done, 1)
            e.memset(s[:, 0:256], 0.0).then_inc(const_done, 1)
            e.memset(s[:, 256 + NT:512 + NT], 0.0).then_inc(const_done, 1)
            e.wait_ge(w_loaded, NLOAD)
            e.tensor_scalar(ntaps[:], taps[:], -1.0, None, ALU.mult).then_inc(const_done, 1)
            e.tensor_scalar(ndist[:], dist[:].rearrange("p a b -> p (a b)"), -1.0, None, ALU.mult)\
                .then_inc(const_done, 1)
            e.wait_ge(const_done, 6)
            with e.Fori(0, NI) as im:
                e.wait_ge(ks_ps, im + 1)
                steps = [
                    lambda: e.tensor_scalar(kc[:, 0], small[:, 0:TS], b2[:], 0.0, ALU.add, ALU.max),
                    lambda: e.tensor_scalar(kc[:, 1], kc[:, 0], 20.0, 1.0, ALU.mult, ALU.add),
                    lambda: e.tensor_tensor(kc[:, 2], kc[:, 1], kc[:, 1], ALU.mult),
                    lambda: e.reciprocal(kc[:, 3], kc[:, 2])]
                for n, make in enumerate(steps):
                    make().then_inc(kc_done, 1)
                    e.wait_ge(kc_done, im * 4 + n + 1)
                e.tensor_scalar(sc[:], kc[:, 3], 4.5, None, ALU.mult).then_inc(sc_done, 1)
                for g in range(4):
                    e.wait_ge(xt_ps, im * 4 + g + 1)
                    e.tensor_copy(xt[:, 4 * g:4 * g + 4].rearrange("p a b -> p (a b)"), ring[:, g % 2])\
                        .then_inc(xt_done, 1)
                e.wait_ge(z_ps, im * NG + NG)
                e.reciprocal(rzc[:], small[:, TS:2 * TS]).then_inc(rzc_done, 1)
                e.wait_ge(sbc_done, im * NG + NG)

                def enhance(g):
                    r, c = at(g)
                    e.wait_ge(rz_done, im * NG + g + 1)
                    e.wait_ge(acc_done, im * TS + 4 * g + 4)
                    e.tensor_tensor(low[r, g % 2], acc[r, g % 2], rz[r, g % 2], ALU.mult).then_inc(low_done, 1)
                    e.wait_ge(low_done, im * NG + g + 1)
                    e.tensor_tensor(enh[r, c], low[r, g % 2], x[r, c], ALU.add).then_inc(enh_done, 1)

                for t in range(TS):
                    if t >= 2:
                        e.wait_ge(f_done, im * TS + t - 1)
                    e.tensor_tensor(lg[:, t % 2], ndist[:], s[:, t * 128:t * 128 + ND * 128], ALU.mult)\
                        .then_inc(lg_done, 1)
                    if t % 4 == 3 and t > 4:
                        enhance(t // 4 - 1)
                enhance(NG - 1)
                e.wait_ge(enh_done, im * NG + NG + 1)
                e.reduce_sum(stat[:, 0:1], enh[:], AXX).then_inc(sum_done, 1)
                e.wait_ge(mean_ps, im + 1)
                e.tensor_scalar(cen[:], enh[:], small[:, 2 * TS:2 * TS + 1], None, ALU.subtract).then_inc(cen_done, 1)
                e.wait_ge(var_ps, im + 1)
                e.tensor_scalar(stat[:, 2:3], small[:, 2 * TS + 1:2 * TS + 2], 1e-5, None, ALU.add)\
                    .then_inc(var_done, 1)
                e.wait_ge(rstd_done, im + 1)
                e.wait_ge(stored, im * 32 + 1)
                e.tensor_scalar(out[:], cen[:], stat[:, 3:4], None, ALU.mult).then_inc(out_done, 1)

        @block.tensor
        def _(e):
            e.wait_ge(w_loaded, NLOAD)
            e.wait_ge(const_done, 6)
            with e.Fori(0, NI) as im:
                e.wait_ge(x_loaded, im * 32 + 32)
                alone(e)
                for g in range(NG):
                    r, c = at(g)
                    if g >= 2:
                        e.wait_ge(h_done, im * NG + g - 1)
                        alone(e)
                    e.matmul(ring[0:HID, g % 2], w1[r], x[r, c], start=True, stop=True).then_inc(h_ps, 1)
                e.wait_ge(h_done, im * NG + NG)
                alone(e)
                for t in range(TS):
                    ins = e.matmul(small[:, t:t + 1], hid[:, t * 128:t * 128 + 128], w2[:], start=True, stop=True)
                ins.then_inc(ks_ps, 1)
                for g in range(4):
                    if g >= 2:
                        e.wait_ge(xt_done, im * 4 + g - 1)
                        alone(e)
                    for t in range(4 * g, 4 * g + 4):
                        ins = e.transpose(ring[:, g % 2, (t % 4) * 128:(t % 4) * 128 + 128],
                                          x[:, t * 128:t * 128 + 128], ident[:])
                    ins.then_inc(xt_ps, 1)

                def sums(g):
                    e.wait_ge(e81_done, im * NG + g + 1)
                    alone(e)
                    for t in range(4 * g, 4 * g + 4):
                        ins = e.matmul(small[:, TS + t:TS + t + 1], e81[:, g % 2, (t % 4) * 128:(t % 4) * 128 + 128],
                                       ones[:], start=True, stop=True)
                    ins.then_inc(z_ps, 1)

                e.wait_ge(sc_done, im + 1)
                e.wait_ge(xt_done, im * 4 + 4)
                for g in range(NG):
                    if g >= 2:
                        sums(g - 2)
                    for t in range(4 * g, 4 * g + 4):
                        ins = e.matmul(ring[:, g % 2, (t % 4) * 128:(t % 4) * 128 + 128],
                                       sc[:, t:t + 1].broadcast_to([128, 128]), ident[:], start=True, stop=True)
                    ins.then_inc(sbc_ps, 1)
                sums(NG - 2)
                sums(NG - 1)
                e.wait_ge(rzc_done, im + 1)
                alone(e)

                def spread(g):
                    r, _ = at(g)
                    if g >= 2:
                        e.wait_ge(rz_done, im * NG + g - 1)
                        alone(e)
                    for t in range(4 * g, 4 * g + 4):
                        ins = e.matmul(rz_ps[r, g % 2, (t % 4) * 128:(t % 4) * 128 + 128],
                                       rzc[:, t:t + 1].broadcast_to([128, C]), ident[:], start=True, stop=True)
                    ins.then_inc(rz_ps_done, 1)

                for t in range(TS):
                    g = t // 4
                    r, _ = at(g)
                    if t % 4 == 0:
                        spread(g)
                        if g >= 2:
                            e.wait_ge(low_done, im * NG + g - 1)
                    e.wait_ge(f_done, im * TS + min(t + 3, TS))
                    alone(e)
                    reach = [q for q in range(t - 2, t + 3) if 0 <= q < TS]
                    for q in reach:
                        ins = e.matmul(acc[r, g % 2, (t % 4) * 128:(t % 4) * 128 + 128],
                                       xt[:, q % HT, 64 * (q // HT):64 * (q // HT) + 64],
                                       f[:, q % NB, (t - q + 2) * 128:(t - q + 2) * 128 + 128],
                                       start=q == reach[0], stop=q == reach[-1])
                    ins.then_inc(acc_done, 1)
                e.wait_ge(sum_done, im + 1)
                alone(e)
                e.matmul(small[:, 2 * TS:2 * TS + 1], fold[:], stat[:, 0:1], start=True, stop=True).then_inc(mean_ps, 1)
                e.wait_ge(ssq_done, im + 1)
                alone(e)
                e.matmul(small[:, 2 * TS + 1:2 * TS + 2], fold[:], stat[:, 1:2], start=True, stop=True)\
                    .then_inc(var_ps, 1)


def _copy_rows(nc, keep, name, rows_from, rows_to):
    done = keep.enter_context(nc.semaphore(name))
    with nc.Block() as block:
        @block.sync
        def _(e):
            e.dma_start(rows_to, rows_from).then_inc(done, 16)
            e.wait_ge(done, 16)


def conv_attention_swin_blur(nc, x, wt, out):
    S = SHIFT
    scratch = lambda n, shape: nc.dram_tensor(n, shape, F32, kind="Internal").ap()
    x1 = scratch("after_attention0", (NI, C, NT))
    x2 = scratch("after_attention1", (NI, C, HH, WW))
    x3 = scratch("after_swin", (NI, C, HH + S, WW))
    x4 = scratch("after_shifted_swin", (NI, C, HH + S, WW))
    pixels = lambda a: a.rearrange("i c h w -> i c (h w)")
    with ExitStack() as keep:
        _attention0(nc, keep, pixels(x), wt, x1)
        _attention1(nc, keep, x1, wt, pixels(x2))
        _swin(nc, keep, "w0", x2, {**wt, **{n: wt[n + "_0"] for n in SWIN_WEIGHTS}}, x3, False)
        _copy_rows(nc, keep, "x3_rows", x3[:, :, 0:S], x3[:, :, HH:HH + S])
        _swin(nc, keep, "w1", x3, {**wt, **{n: wt[n + "_1"] for n in SWIN_WEIGHTS}}, x4, True)
        _copy_rows(nc, keep, "x4_rows", x4[:, :, HH:HH + S], x4[:, :, 0:S])
        _adaptive_blur(nc, keep, x4[:, :, 0:HH].rearrange("i c h w -> i c (h w)"), wt, pixels(out))


SWIN_WEIGHTS = ("cols", "wqk2", "wv2", "vb2", "wp2", "w12", "w22", "rel")


def _layouts(inputs):
    import numpy as np
    f32 = np.float32
    with_bias = lambda m, b: np.concatenate([m.T, b[None]], 0)
    twice = lambda m: np.concatenate([m, m])

    def blocks(m):
        z = np.zeros_like(m)
        return np.block([[m, z], [z, m]])

    def four(m, b):
        a = np.zeros((C + 1, 4, 32), f32)
        a[:, :, 0:8] = with_bias(m, b)[:, None]
        return a.reshape(C + 1, 128)

    a = {}
    g = lambda n: np.asarray(inputs["L0_conv_" + n])
    a["wqk"] = np.stack([np.tile(with_bias(g("w" + n), g("b" + n)), (1, 3)) for n in "12"], 1)
    a["wv"] = with_bias(g("w3"), g("b3"))
    a["al"] = np.tile(np.concatenate([g("a1"), g("a2"), g("a3")])[None], (128, 1))
    g = lambda n: np.asarray(inputs["L1_conv_" + n])
    a["wqk1"] = np.stack([four(g("Wq"), g("bq")), four(g("Wk"), g("bk"))], 1)
    a["wv1"] = with_bias(g("Wv"), g("bv"))

    g = lambda n: np.asarray(inputs["L2_conv_" + n])
    at = np.stack(np.meshgrid(np.arange(8), np.arange(8), indexing="ij")).reshape(2, -1)
    dy, dx = at[:, :, None] - at[:, None, :] + 7
    for b in range(2):
        qw, qb = g("qkv_w")[b], g("qkv_b")[b]
        norms = [g("pe_g"), g("pe_b"), g("norm1_g")[b], g("norm1_b")[b], g("norm2_g")[b], g("norm2_b")[b]]
        a[f"cols_{b}"] = np.stack([twice(v) for v in norms + [qb[0:C], qb[C:2 * C], g("proj_b")[b]]]
                                  + [g("fc1_b")[b], twice(g("fc2_b")[b])], 1)
        a[f"wqk2_{b}"] = np.stack([blocks(qw[:, 0:C]), blocks(qw[:, C:2 * C])], 1)
        a[f"wv2_{b}"] = twice(qw[:, 2 * C:])
        a[f"vb2_{b}"] = np.tile(qb[2 * C:], (128, 1))
        a[f"wp2_{b}"] = g("proj_w")[b]
        a[f"w12_{b}"] = twice(g("fc1_w")[b])
        a[f"w22_{b}"] = g("fc2_w")[b]
        a[f"rel_{b}"] = np.tile(g("rpb")[b][dy * 15 + dx].transpose(0, 2, 1), (2, 1, 1))
    region = np.zeros((HH, WW))
    edges = (slice(0, -8), slice(-8, -4), slice(-4, None))
    for i, rows in enumerate(edges):
        for j, columns in enumerate(edges):
            region[rows, columns] = 3 * i + j
    region = region.reshape(8, 8, 8, 8).transpose(0, 2, 1, 3).reshape(8, 8, 64)
    mask = np.where(region[:, :, None] != region[..., None], f32(-100), f32(0))
    a["mask"] = mask.reshape(2, 4, 8, 64, 64)[:, :, [0, 7]].transpose(0, 3, 1, 2, 4).reshape(128, 4, 2, 64)
    a["mean_w"] = blocks(np.full((64, 64), 1 / 64, f32))
    a["half_w"] = a["mean_w"][:, [0, 64]]
    a["hmask"] = twice((np.arange(C)[:, None] // 8 == np.arange(8)).astype(f32))
    a["ident"] = np.eye(128, dtype=f32)

    g = lambda n: np.asarray(inputs["L3_conv_" + n])
    q, p = np.arange(128)[:, None], np.arange(128)[None]
    dist = np.full((128, 5, 128), 1e30, f32)
    for d in range(5):
        u, v = q // 64 - p // 64 - 2 * (d - 2) + 4, q % 64 - p % 64 + 4
        near = (u >= 0) & (u < 9) & (v >= 0) & (v < 9)
        dist[:, d][near] = g("gauss_kernel")[u[near], v[near]]
    a["b_dist"] = dist
    a["b_taps"] = g("gauss_kernel").reshape(81, 1)
    a["b_w1"], a["b_b1"], a["b_w2"] = twice(g("w1")), g("b1")[:, None], g("w2")
    a["b_b2"] = np.tile(g("b2")[None], (128, 1))
    a["b_fold"] = np.tile(np.eye(C, dtype=f32), (2, 2)) / f32(NT)
    return {n: np.ascontiguousarray(v, f32) for n, v in a.items()}


def kernel(**inputs):
    import numpy as np
    import concourse.bacc as bacc
    from concourse.bass_utils import run_bass_kernel_spmd

    nc = bacc.Bacc("TRN2", target_bir_lowering=False, num_devices=1)
    arrays = {"x": np.ascontiguousarray(inputs["x"]), **_layouts(inputs)}
    aps = {n: nc.dram_tensor(n, a.shape, mybir.dt.from_np(a.dtype), kind="ExternalInput").ap()
           for n, a in arrays.items()}
    out = nc.dram_tensor("out", (NI, C, HH, WW), F32, kind="ExternalOutput").ap()
    conv_attention_swin_blur(nc, aps.pop("x"), aps, out)
    r = run_bass_kernel_spmd(nc, [arrays], core_ids=[0])
    return r.results[0]["out"]
```

```python
from contextlib import ExitStack

import concourse.bass as bass
from concourse import mybir

F32 = mybir.dt.float32
F16 = mybir.dt.float16
ALU = mybir.AluOpType
ACT = mybir.ActivationFunctionType
AXX = mybir.AxisListType.X

NI, C, HH, WW = 8, 64, 64, 64
NT = HH * WW
CH = 512
NCH = NT // CH
KT = NT // 128
SHIFT = 4


def _attention0(nc, keep, x_in, w, x_out):
    UQ = 1024
    NU = NT // UQ
    QT = UQ // 128
    ASTEPS = QT * NCH
    MS = 64.0
    NP = 4
    GV = KT // 8
    with ExitStack() as ctx:
        sb = lambda n, s, d=F32: ctx.enter_context(nc.sbuf_tensor("a0_" + n, s, d))
        sem = lambda n: keep.enter_context(nc.semaphore("a0_" + n))
        xa = sb("xa", [C + 1, NT])
        xr = sb("xr", [128, NU, CH])
        wqk = sb("wqk", [C + 1, 2, 96])
        wv = sb("wv", [C + 1, C])
        al = sb("al", [128, 3])
        ident = sb("ident", [128, 128])
        ones = sb("ones", [128, C])
        raw = sb("raw", [96, 2, 2, CH])
        neg = sb("neg", [96, 2, 2, CH])
        negv = sb("negv", [128, 2, CH])
        qs = sb("qs", [97, NT], F16)
        ks = sb("ks", [97, NT], F16)
        vt = sb("vt", [128, KT, C])
        p = sb("p", [128, NP, UQ])
        sum_d = sb("sum_d", [128, UQ])
        sum_p = sb("sum_p", [128, UQ])
        mparts = sb("mparts", [128, QT, NCH])
        mneg = sb("mneg", [128, QT])
        rden = sb("rden", [128, CH])
        att = sb("att", [128, CH])
        res = sb("res", [128, CH])
        a_ps = ctx.enter_context(nc.psum_tensor("a0_a_ps", [128, 2, CH], F32))
        b_ps = ctx.enter_context(nc.psum_tensor("a0_b_ps", [128, 2, 2, CH], F32))
        acc = ctx.enter_context(nc.psum_tensor("a0_acc", [128, CH], F32))
        den = ctx.enter_context(nc.psum_tensor("a0_den", [128, CH], F32))

        w_loaded = sem("w_loaded")
        xa_loaded, xr_loaded = sem("xa_loaded"), sem("xr_loaded")
        const_done = sem("const_done")
        proj_done = sem("proj_done")
        neg_done = sem("neg_done")
        raw_done, hi_done, split_done = sem("raw_done"), sem("hi_done"), sem("split_done")
        vt_done = sem("vt_done")
        sa_done, max_done = sem("sa_done"), sem("max_done")
        mneg_done, mrow_ps, mrow_done = sem("mneg_done"), sem("mrow_ps"), sem("mrow_done")
        sb_done, exp_done, pv_done = sem("sb_done"), sem("exp_done"), sem("pv_done")
        addp_done, addd_done, den_done = sem("addp_done"), sem("addd_done"), sem("den_done")
        rden_done, att_done, res_done = sem("rden_done"), sem("att_done"), sem("res_done")
        stored = sem("stored")
        block = ctx.enter_context(nc.Block())

        PREP = NCH + GV
        HALF = KT // 2

        @block.sync
        def _(e):
            e.dma_start(wqk[:], w["wqk"]).then_inc(w_loaded, 16)
            e.dma_start(wv[:], w["wv"]).then_inc(w_loaded, 16)
            e.dma_start(al[:], w["al"]).then_inc(w_loaded, 16)
            e.dma_start(ident[:], w["ident"]).then_inc(w_loaded, 16)
            e.sem_inc(stored, 1)
            xin_v = x_in.rearrange("i c (u j n) -> j i c u n", u=NU, j=2)
            xout_v = x_out.rearrange("i c (u j n) -> j i c u n", u=NU, j=2)

            def load_xa(im):
                e.dma_start(xa[0:C, :], x_in[bass.ds(im, 1)].rearrange("a c n -> (a c) n")).then_inc(xa_loaded, 16)

            def load_xr(im):
                for j in range(2):
                    e.dma_start(xr[64 * j:64 * j + 64], xin_v[j][bass.ds(im, 1)].rearrange("i c u n -> (i c) u n"))\
                        .then_inc(xr_loaded, 16)

            def store(im, u):
                e.wait_ge(res_done, im * NU + u + 1)
                for j in range(2):
                    e.dma_start(xout_v[j][bass.ds(im, 1), :, bass.ds(u, 1)].rearrange("i c u n -> (i c) (u n)"),
                                res[64 * j:64 * j + 64]).then_inc(stored, 16)

            load_xa(0)
            load_xr(0)
            with e.Fori(0, NI - 1) as im:
                e.wait_ge(vt_done, im * GV + GV)
                load_xa(im + 1)
                for u in range(NU):
                    store(im, u)
                load_xr(im + 1)
            for u in range(NU):
                store(NI - 1, u)
            e.wait_ge(stored, NI * NU * 32 + 1)

        @block.gpsimd
        def _(e):
            e.sem_inc(addp_done, NP // 2)
            with e.Fori(0, NI) as im:
                for ch in range(NCH):
                    cs = slice(ch * CH, ch * CH + CH)
                    e.wait_ge(hi_done, im * NCH + ch + 1)
                    e.tensor_tensor(qs[64:96, cs], raw[64:96, ch % 2, 0], qs[64:96, cs], ALU.subtract)
                    e.tensor_tensor(ks[32:64, cs], raw[32:64, ch % 2, 1], ks[32:64, cs],
                                    ALU.subtract).then_inc(split_done, 1)
                with e.Fori(0, NU) as u:
                    g = e.snap(im * NU + u)
                    e.wait_ge(den_done, g + 1)
                    for i in range(1, HALF):
                        e.wait_ge(exp_done, g * KT + 2 * i + 1 + 2)
                        if i > 1:
                            e.wait_ge(addp_done, g * HALF + i + NP // 2)
                        e.tensor_tensor(sum_p[:], p[:, 0] if i == 1 else sum_p[:], p[:, (2 * i) % NP],
                                        ALU.add).then_inc(addp_done, 2 if i == 1 else 1)

        @block.scalar
        def _(e):
            e.sem_inc(exp_done, 2)
            e.sem_inc(mrow_done, 1)
            with e.Fori(0, NI) as im:
                for ch in range(NCH):
                    cs = slice(ch * CH, ch * CH + CH)
                    e.wait_ge(raw_done, im * NCH + ch + 1)
                    e.activation(qs[0:96, cs], raw[:, ch % 2, 0], ACT.Copy)
                    e.activation(ks[0:96, cs], raw[:, ch % 2, 1], ACT.Copy).then_inc(hi_done, 1)
                with e.Fori(0, NU) as u:
                    g = e.snap(im * NU + u)
                    e.wait_ge(mrow_ps, g + 1)
                    e.activation(qs[96:97, bass.ds(u * UQ, UQ)], a_ps[96:97, :, :].rearrange("p a n -> p (a n)"),
                                 ACT.Copy, scale=1.0 / MS).then_inc(mrow_done, 1)
                    for kt in range(KT):
                        e.wait_ge(sb_done, g * KT + kt + 1)
                        e.wait_ge(pv_done, g * KT + kt + 1)
                        e.wait_ge(addp_done if kt % 2 == 0 else addd_done, g * HALF + kt // 2 + 1)
                        e.activation(p[:, kt % NP], b_ps[:, kt % 2].rearrange("p a n -> p (a n)"),
                                     ACT.Exp).then_inc(exp_done, 1)

        @block.vector
        def _(e):
            e.memset(xa[C:C + 1, :], 1.0).then_inc(const_done, 1)
            e.memset(ks[96:97, :], MS).then_inc(const_done, 1)
            e.memset(ones[:], 1.0).then_inc(const_done, 1)
            e.sem_inc(addd_done, NP // 2)
            e.sem_inc(att_done, 1)
            e.wait_ge(w_loaded, 64)

            def max_steps(g, t, c):
                s = t * NCH + c
                e.wait_ge(sa_done, g * ASTEPS + s + 1)
                e.reduce_max(mparts[:, t, c:c + 1], a_ps[:, s % 2], AXX).then_inc(max_done, 1)

            def mneg_step(g):
                e.wait_ge(max_done, g * ASTEPS + ASTEPS + 2)
                e.reduce_max(mneg[:], mparts[:], AXX, negate=True).then_inc(mneg_done, 1)

            e.sem_inc(max_done, 2)
            with e.Fori(0, NI) as im:
                for ch in range(NCH):
                    t = b_ps[0:96, ch % 2]
                    e.wait_ge(proj_done, im * PREP + ch + 1)
                    for j in range(2):
                        ins = e.tensor_scalar(neg[:, ch % 2, j], t[:, j], 0.0, al[0:96, j:j + 1], ALU.min, ALU.mult)
                    ins.then_inc(neg_done, 1)
                    e.wait_ge(neg_done, im * PREP + ch + 1)
                    if ch >= 2:
                        e.wait_ge(split_done, im * NCH + ch - 1)
                    e.scalar_tensor_tensor(raw[:, ch % 2], t, 0.0, neg[:, ch % 2], ALU.max, ALU.add)\
                        .then_inc(raw_done, 1)
                for gv in range(GV):
                    t = a_ps[:, gv % 2]
                    e.wait_ge(proj_done, im * PREP + NCH + gv + 1)
                    e.tensor_scalar(negv[:, gv % 2], t, 0.0, al[:, 2:3], ALU.min, ALU.mult).then_inc(neg_done, 1)
                    e.wait_ge(neg_done, im * PREP + NCH + gv + 1)
                    e.scalar_tensor_tensor(vt[:, 8 * gv:8 * gv + 8].rearrange("p a c -> p (a c)"), t, 0.0,
                                           negv[:, gv % 2], ALU.max, ALU.add).then_inc(vt_done, 1)
                g0 = e.snap(im * NU)
                for s in range(ASTEPS):
                    max_steps(g0, s // NCH, s % NCH)
                mneg_step(g0)

                def unit(g, u, more):
                    for kt in range(KT):
                        if more:
                            for s in range(2 * kt, 2 * kt + 2):
                                max_steps(g + 1, s // NCH, s % NCH)
                        if kt % 2 and kt > 1:
                            e.wait_ge(exp_done, g * KT + kt + 1 + 2)
                            if kt > 3:
                                e.wait_ge(addd_done, g * HALF + kt // 2 + NP // 2)
                            e.tensor_tensor(sum_d[:], p[:, 1] if kt == 3 else sum_d[:], p[:, kt % NP],
                                            ALU.add).then_inc(addd_done, 2 if kt == 3 else 1)
                    if more:
                        mneg_step(g + 1)
                    e.wait_ge(den_done, g + 2)
                    e.reciprocal(rden[:], den[:]).then_inc(rden_done, 1)
                    e.wait_ge(rden_done, g + 1)
                    e.tensor_tensor(att[:], acc[:], rden[:], ALU.mult).then_inc(att_done, 1)
                    e.wait_ge(att_done, g + 2)
                    e.wait_ge(xr_loaded, im * 32 + 32)
                    e.wait_ge(stored, g * 32 + 1)
                    e.tensor_tensor(res[:], att[:], xr[:, bass.ds(u, 1)].rearrange("p a n -> p (a n)"),
                                    ALU.add).then_inc(res_done, 1)

                with e.Fori(0, NU - 1) as u:
                    unit(e.snap(im * NU + u), u, True)
                unit(e.snap(im * NU + NU - 1), NU - 1, False)

        @block.tensor
        def _(e):
            e.sem_inc(pv_done, NP)
            e.sem_inc(den_done, 1)
            e.wait_ge(w_loaded, 64)
            e.wait_ge(const_done, 3)

            def pass_a(g, u, s):
                t, c = s // NCH, s % NCH
                e.wait_ge(max_done, g * ASTEPS + s + 1)
                e.matmul(a_ps[:, s % 2], qs[0:96, bass.ds(u * UQ + t * 128, 128)],
                         ks[0:96, c * CH:c * CH + CH], start=True, stop=True).then_inc(sa_done, 1)

            def max_row(g):
                e.wait_ge(mneg_done, g + 1)
                for t in range(QT):
                    ins = e.matmul(a_ps[96:97, t // 4, (t % 4) * 128:(t % 4) * 128 + 128], mneg[:, t:t + 1],
                                   ident[:], start=True, stop=True)
                ins.then_inc(mrow_ps, 1)

            with e.Fori(0, NI) as im:
                e.wait_ge(xa_loaded, im * 16 + 16)
                e.wait_ge(exp_done, im * (NU * KT) + 2)
                for ch in range(NCH):
                    if ch >= 2:
                        e.wait_ge(raw_done, im * NCH + ch - 1)
                    for j in range(2):
                        ins = e.matmul(b_ps[0:96, ch % 2, j], wqk[:, j], xa[:, ch * CH:ch * CH + CH],
                                       start=True, stop=True)
                    ins.then_inc(proj_done, 1)
                e.wait_ge(mrow_done, im * NU + 1)
                for gv in range(GV):
                    if gv >= 2:
                        e.wait_ge(vt_done, im * GV + gv - 1)
                    for i in range(8):
                        t = gv * 8 + i
                        ins = e.matmul(a_ps[:, gv % 2, i * C:i * C + C], xa[:, t * 128:t * 128 + 128],
                                       wv[:], start=True, stop=True)
                    ins.then_inc(proj_done, 1)
                e.wait_ge(split_done, im * NCH + NCH)
                e.wait_ge(vt_done, im * GV + GV)
                g0 = e.snap(im * NU)
                for s in range(ASTEPS):
                    pass_a(g0, 0, s)
                max_row(g0)

                def pv(g, kt):
                    e.wait_ge(exp_done, g * KT + kt + 1 + 2)
                    for j in range(2):
                        ins = e.matmul(acc[64 * j:64 * j + 64, :], vt[:, kt], p[:, kt % NP, j * CH:j * CH + CH],
                                       start=kt == 0, stop=kt == KT - 1)
                    ins.then_inc(pv_done, 1)

                def unit(g, u, more):
                    e.wait_ge(mrow_done, g + 2)
                    e.wait_ge(att_done, g + 1)
                    for kt in range(KT):
                        e.wait_ge(exp_done, g * KT + kt + 1)
                        for j in range(2):
                            ins = e.matmul(b_ps[:, kt % 2, j], ks[:, kt * 128:kt * 128 + 128],
                                           qs[:, bass.ds(u * UQ + j * CH, CH)], start=True, stop=True)
                        ins.then_inc(sb_done, 1)
                        if more:
                            for s in range(2 * kt, 2 * kt + 2):
                                pass_a(g + 1, u + 1, s)
                        if kt >= 1:
                            pv(g, kt - 1)
                    pv(g, KT - 1)
                    e.wait_ge(addp_done, g * HALF + HALF + NP // 2)
                    e.wait_ge(addd_done, g * HALF + HALF + NP // 2)
                    for j in range(2):
                        for k, part in enumerate((sum_d, sum_p)):
                            ins = e.matmul(den[64 * j:64 * j + 64, :], ones[:], part[:, j * CH:j * CH + CH],
                                           start=k == 0, stop=k == 1)
                    ins.then_inc(den_done, 1)
                    if more:
                        max_row(g + 1)

                with e.Fori(0, NU - 1) as u:
                    unit(e.snap(im * NU + u), u, True)
                unit(e.snap(im * NU + NU - 1), NU - 1, False)


def _attention1(nc, keep, x_in, w, x_out):
    NPART = 4
    PW = NT // NPART
    NP = 4
    LAG = 2
    with ExitStack() as ctx:
        sb = lambda n, s, d=F32: ctx.enter_context(nc.sbuf_tensor("a1_" + n, s, d))
        sem = lambda n: keep.enter_context(nc.semaphore("a1_" + n))
        xa = sb("xa", [C + 1, NT])
        xr = sb("xr", [128, NT // 2])
        wqk = sb("wqk", [C + 1, 2, 128])
        wv = sb("wv", [C + 1, C])
        raw = sb("raw", [128, 2, 2, CH])
        qs = sb("qs", [128, NT], F16)
        ks = sb("ks", [128, NT], F16)
        v = sb("v", [128, KT, C])
        p = sb("p", [128, NP, NT])
        nm = sb("nm", [128, NP, NPART])
        nrow = sb("nrow", [128, NP])
        z = sb("z", [128, NP, NPART])
        f = sb("f", [128, NP, NPART])
        fz = sb("fz", [128, NP, NPART])
        zrow = sb("zrow", [128, NP])
        rz = sb("rz", [128, NP])
        gain = sb("gain", [128, NP, NPART])
        vs = sb("vs", [128, NP, NPART, C])
        res = sb("res", [128, NT // 2])
        acc = ctx.enter_context(nc.psum_tensor("a1_acc", [128, 4, CH], F32))
        s_ps = ctx.enter_context(nc.psum_tensor("a1_s_ps", [128, 2, 2, CH], F32))

        w_loaded = sem("w_loaded")
        xa_loaded, xr_loaded, ones_done = sem("xa_loaded"), sem("xr_loaded"), sem("ones_done")
        proj_done, raw_done, hi_done, split_done = sem("proj_done"), sem("raw_done"), sem("hi_done"), sem("split_done")
        vproj_done, v_done = sem("vproj_done"), sem("v_done")
        s_done, nm_done, exp_done = sem("s_done"), sem("nm_done"), sem("exp_done")
        nrow_done, f_done, scale_done, vs_done = sem("nrow_done"), sem("f_done"), sem("scale_done"), sem("vs_done")
        pv_done, res_done, stored = sem("pv_done"), sem("res_done"), sem("stored")
        block = ctx.enter_context(nc.Block())
        GV = KT // 8
        NSPLIT = 3 * NCH

        @block.sync
        def _(e):
            xin_v = x_in.rearrange("i c (h n) -> h i c n", h=2)
            xout_v = x_out.rearrange("i c (h n) -> h i c n", h=2)
            e.sem_inc(stored, 1)

            def load_xa(im):
                e.dma_start(xa[0:C, :], x_in[bass.ds(im, 1)].rearrange("a c n -> (a c) n")).then_inc(xa_loaded, 16)

            def load_xr(im):
                for h in range(2):
                    e.dma_start(xr[64 * h:64 * h + 64], xin_v[h][bass.ds(im, 1)].rearrange("i c n -> (i c) n"))\
                        .then_inc(xr_loaded, 16)

            def store(im):
                e.wait_ge(res_done, im * 4 + 4 + 4)
                for h in range(2):
                    e.dma_start(xout_v[h][bass.ds(im, 1)].rearrange("i c n -> (i c) n"),
                                res[64 * h:64 * h + 64]).then_inc(stored, 16)

            e.dma_start(wqk[:], w["wqk1"]).then_inc(w_loaded, 16)
            e.dma_start(wv[:], w["wv1"]).then_inc(w_loaded, 16)
            load_xa(0)
            load_xr(0)
            with e.Fori(0, NI - 1) as im:
                e.wait_ge(vproj_done, im * GV + GV)
                load_xa(im + 1)
                store(im)
                load_xr(im + 1)
            store(NI - 1)
            e.wait_ge(stored, NI * 32 + 1)

        @block.gpsimd
        def _(e):
            with e.Fori(0, NI) as im:
                for ch in range(NCH):
                    cs = slice(ch * CH, ch * CH + CH)
                    e.wait_ge(hi_done, im * NCH + ch + 1)
                    for j, (qk, r, n) in enumerate(((qs, 64, 64), (ks, 32, 32), (ks, 96, 32))):
                        e.tensor_tensor(qk[r:r + n, cs], raw[r:r + n, ch % 2, min(j, 1)], qk[r:r + n, cs],
                                        ALU.subtract).then_inc(split_done, 1)
                        e.wait_ge(split_done, im * NSPLIT + ch * 3 + j + 1)

        @block.scalar
        def _(e):
            e.sem_inc(exp_done, 2)

            def part(t, slot, c):
                e.wait_ge(nm_done, t * NPART + c + 1)
                if c == 0:
                    e.wait_ge(pv_done, t + 1)
                e.activation(p[:, slot, c * PW:c * PW + PW], s_ps[:, c % 2].rearrange("p a n -> p (a n)"),
                             ACT.Exp, bias=nm[:, slot, c:c + 1], accum_out=z[:, slot, c:c + 1])\
                    .then_inc(exp_done, 1)

            def rescale(t, slot):
                e.wait_ge(nrow_done, t + 1)
                e.activation(f[:, slot], nm[:, slot], ACT.Exp, bias=nrow[:, slot:slot + 1], scale=-1.0)\
                    .then_inc(f_done, 1)

            with e.Fori(0, NI) as im:
                for ch in range(NCH):
                    cs = slice(ch * CH, ch * CH + CH)
                    e.wait_ge(raw_done, im * NCH + ch + 1)
                    e.activation(qs[:, cs], raw[:, ch % 2, 0], ACT.Copy)
                    e.activation(ks[:, cs], raw[:, ch % 2, 1], ACT.Copy).then_inc(hi_done, 1)
                with e.Fori(0, KT // NP) as i:
                    t = e.snap(im * KT + i * NP)
                    for slot in range(NP):
                        for c in range(NPART):
                            part(t + slot, slot, c)
                        rescale(t + slot, slot)

        @block.vector
        def _(e):
            e.memset(xa[C:C + 1, :], 1.0).then_inc(ones_done, 1)
            e.sem_inc(res_done, 4)

            def scale_v(t, slot, kt, k):
                if k == 0:
                    e.wait_ge(f_done, t + 1)
                    ins = e.tensor_tensor(fz[:, slot], f[:, slot], z[:, slot], ALU.mult)
                elif k == 1:
                    ins = e.reduce_sum(zrow[:, slot:slot + 1], fz[:, slot], AXX)
                elif k == 2:
                    ins = e.reciprocal(rz[:, slot:slot + 1], zrow[:, slot:slot + 1])
                elif k == 3:
                    ins = e.tensor_scalar(gain[:, slot], f[:, slot], rz[:, slot:slot + 1], None, ALU.mult)
                else:
                    ins = e.tensor_tensor(vs[:, slot], v[:, bass.ds(kt, 1)].broadcast_to([128, NPART, C]),
                                          gain[:, slot].unsqueeze(2).broadcast_to([128, NPART, C]), ALU.mult)
                ins.then_inc(vs_done, 1)
                if k < 4:
                    e.wait_ge(vs_done, t * 5 + k + 1)

            def step(t, slot, kt, before, now):
                for c in range(NPART):
                    if before and c >= 1:
                        scale_v(t - 1, (slot - 1) % NP, kt - 1, c - 1)
                    if now:
                        e.wait_ge(s_done, t * NPART + c + 1)
                        e.reduce_max(nm[:, slot, c:c + 1], s_ps[:, c % 2].rearrange("p a n -> p (a n)"), AXX,
                                     negate=True).then_inc(nm_done, 1)
                if now:
                    e.wait_ge(nm_done, t * NPART + NPART)
                    e.tensor_reduce(nrow[:, slot:slot + 1], nm[:, slot], AXX, ALU.min).then_inc(nrow_done, 1)
                if before:
                    for k in (3, 4):
                        if k == 4:
                            e.wait_ge(pv_done, t - 1 + 1)
                        scale_v(t - 1, (slot - 1) % NP, kt - 1, k)

            with e.Fori(0, NI) as im:
                for ch in range(NCH):
                    e.wait_ge(proj_done, im * NCH + ch + 1)
                    if ch >= 2:
                        e.wait_ge(split_done, im * NSPLIT + 3 * ch - 3)
                    e.tensor_copy(raw[:, ch % 2], s_ps[:, ch % 2]).then_inc(raw_done, 1)
                for gv in range(GV):
                    e.wait_ge(vproj_done, im * GV + gv + 1)
                    e.tensor_copy(v[:, 8 * gv:8 * gv + 8].rearrange("p a c -> p (a c)"), s_ps[:, gv % 2, 0])\
                        .then_inc(v_done, 1)
                e.wait_ge(v_done, im * GV + GV)
                t = e.snap(im * KT)
                for slot in range(NP):
                    step(t + slot, slot, slot, slot > 0, True)
                with e.Fori(1, KT // NP) as i:
                    t = e.snap(im * KT + i * NP)
                    for slot in range(NP):
                        step(t + slot, slot, i * NP + slot, True, True)
                step(im * KT + KT, 0, KT, True, False)
                e.wait_ge(pv_done, im * KT + KT + NP)
                e.wait_ge(xr_loaded, im * 32 + 32)
                e.wait_ge(stored, im * 32 + 1)
                for b in range(4):
                    e.tensor_tensor(res[:, b * CH:b * CH + CH], acc[:, b], xr[:, b * CH:b * CH + CH], ALU.add)\
                        .then_inc(res_done, 1)

        @block.tensor
        def _(e):
            e.sem_inc(pv_done, NP)
            e.wait_ge(w_loaded, 32)
            e.wait_ge(ones_done, 1)

            def step(t, slot, kt, now, before, first=False, last=False):
                old = (slot - LAG) % NP
                for c in range(NPART):
                    if now:
                        e.wait_ge(exp_done, t * NPART + c + 1)
                        for j in range(2):
                            n0 = c * PW + j * CH
                            ins = e.matmul(s_ps[:, c % 2, j], ks[:, bass.ds(kt * 128, 128)], qs[:, n0:n0 + CH],
                                           start=True, stop=True)
                        ins.then_inc(s_done, 1)
                    if before:
                        if c == 0:
                            e.wait_ge(vs_done, (t - LAG) * 5 + 5)
                        for h in range(2):
                            n = h * 4 + c
                            ins = e.matmul(acc[64 * h:64 * h + 64, c], vs[:, old, n // 2],
                                           p[:, old, n * CH:n * CH + CH], start=first, stop=last)
                        if c == NPART - 1:
                            ins.then_inc(pv_done, 1)

            with e.Fori(0, NI) as im:
                e.wait_ge(xa_loaded, im * 16 + 16)
                e.wait_ge(exp_done, im * (KT * NPART) + 2)
                for ch in range(NCH):
                    if ch >= 2:
                        e.wait_ge(raw_done, im * NCH + ch - 1)
                    for j in range(2):
                        ins = e.matmul(s_ps[:, ch % 2, j], wqk[:, j], xa[:, ch * CH:ch * CH + CH],
                                       start=True, stop=True)
                    ins.then_inc(proj_done, 1)
                for gv in range(GV):
                    if gv >= 2:
                        e.wait_ge(v_done, im * GV + gv - 1)
                    else:
                        e.wait_ge(raw_done, im * NCH + NCH - 1 + gv)
                    for i in range(8):
                        t = gv * 8 + i
                        ins = e.matmul(s_ps[:, gv % 2, 0, i * C:i * C + C], xa[:, t * 128:t * 128 + 128],
                                       wv[:], start=True, stop=True)
                    ins.then_inc(vproj_done, 1)
                e.wait_ge(split_done, im * NSPLIT + NSPLIT)
                e.wait_ge(v_done, im * GV + GV)
                e.wait_ge(res_done, im * 4 + 4)
                t = e.snap(im * KT)
                for slot in range(NP):
                    step(t + slot, slot, slot, True, slot >= LAG, first=slot == LAG)
                with e.Fori(1, KT // NP) as i:
                    t = e.snap(im * KT + i * NP)
                    for slot in range(NP):
                        step(t + slot, slot, i * NP + slot, True, True)
                t = e.snap(im * KT + KT)
                for slot in range(LAG):
                    step(t + slot, slot, KT + slot, False, True, last=slot == LAG - 1)


def _swin(nc, keep, name, x_in, w, x_out, shifted):
    NC = 4
    NW = 8
    NH, HD, WT = 8, 8, 64
    SCALE = HD ** -0.5
    EPS = 1e-5
    OC = 2 * (HD + 1)
    LN = ["norm1"] if shifted else ["pe", "norm1"]
    LA = len(LN)
    COL = {n: i for i, n in enumerate(["pe_g", "pe_b", "norm1_g", "norm1_b", "norm2_g", "norm2_b",
                                       "q_b", "k_b", "proj_b", "fc1_b", "fc2_b"])}
    NV = 4 if shifted else 1
    NCHUNK = NI * NC
    with ExitStack() as ctx:
        sb = lambda n, s, d=F32: ctx.enter_context(nc.sbuf_tensor(f"{name}_{n}", s, d))
        sem = lambda n: keep.enter_context(nc.semaphore(f"{name}_{n}"))
        ps = lambda n, s: ctx.enter_context(nc.psum_tensor(f"{name}_{n}", s, F32))
        x = sb("x", [128, NC, CH])
        t = x if shifted else sb("t", [128, NC, CH])
        cols = sb("cols", [128, len(COL)])
        wqk = sb("wqk", [128, 2, 128])
        wv = sb("wv", [128, C])
        vb = sb("vb", [128, C])
        wp = sb("wp", [128, 2, C])
        w1 = sb("w1", [128, 128])
        w2 = sb("w2", [128, C])
        mean_w = sb("mean_w", [128, 128])
        half_w = sb("half_w", [128, 2])
        ident = sb("ident", [128, 128])
        hmask = sb("hmask", [128, NH])
        rel = sb("rel", [128, NH, WT])
        mask = sb("mask", [128, NV, 2, WT])
        bias = sb("bias", [128, NV, 2, NH, WT])
        minus_half = sb("minus_half", [128, 2])
        xc = sb("xc", [128, 2, CH])
        sq = sb("sq", [128, 2, CH])
        var = sb("var", [128, 2, 4, 2])
        rstd = sb("rstd", [128, 2, 4, 2])
        xn = sb("xn", [128, 2, CH])
        hw = sb("hw", [128, NW, WT])
        q = sb("q", [128, 2, NW, WT])
        k = sb("k", [128, 2, NW, WT])
        v = sb("v", [128, 2, 2, NW, 4, 2, HD + 1])
        kb = sb("kb", [128, 2, NH, WT])
        s1 = sb("s1", [128, 2, NH, WT])
        nmx = sb("nmx", [128, 2, NH])
        s2 = sb("s2", [128, 2, NH, WT])
        p = sb("p", [128, 2, NH * WT])
        pt = sb("pt", [128, 2, 4, 128])
        rz = sb("rz", [128, 2, 16])
        o = sb("o", [128, NW, C])
        ot = sb("ot", [128, 2, 8, 4, 8])
        x2 = sb("x2", [128, CH])
        h2 = sb("h2", [128, CH])
        g = sb("g", [128, 2, CH])
        xo = sb("xo", [128, 2, CH])
        lin_a = ps("lin_a", [128, 2, CH])
        lin_c = ps("lin_c", [128, CH])
        s_ps = ps("s_ps", [128, 2, CH])
        pt_ps = ps("pt_ps", [128, 2, CH])
        o_ps = ps("o_ps", [128, CH])

        w_loaded, const_done, passed = [sem(n) for n in ("w_loaded", "const_done", "passed")]
        x_loaded = [sem(f"x_loaded{c}") for c in range(NC)]
        stored = [sem(f"stored{b}") for b in range(2)]
        norm_ps, normv_done, norms_done, rs_done = [
            [sem(n + s) for s in ("_a", "_c")] for n in ("norm_ps", "normv_done", "norms_done", "rs_done")]
        qk_ps, qk_done, v_ps, v_done = [sem(n) for n in ("qk_ps", "qk_done", "v_ps", "v_done")]
        kb_done, s_done, soft_done, e_done, tp_done, pt_done, pv_done, out_done = [
            sem(n) for n in ("kb_done", "s_done", "soft_done", "e_done", "tp_done", "pt_done", "pv_done", "out_done")]
        ot_ps, ot_done, proj_ps, x2_done, fc1_ps, g_done, fc2_ps, xo_done = [
            sem(n) for n in ("ot_ps", "ot_done", "proj_ps", "x2_done", "fc1_ps", "g_done", "fc2_ps", "xo_done")]
        block = ctx.enter_context(nc.Block())

        def own_wait(e):
            e.sem_inc(passed, 1)

        col = lambda n: cols[:, COL[n]:COL[n] + 1]
        loads = [(cols, "cols"), (wqk, "wqk2"), (wv, "wv2"), (vb, "vb2"), (wp, "wp2"), (w1, "w12"), (w2, "w22"),
                 (mean_w, "mean_w"), (half_w, "half_w"), (ident, "ident"), (hmask, "hmask"), (rel, "rel"), (mask, "mask")]
        NLOAD = 16 * len(loads)
        XD = 4 if shifted else 2
        CONSTS = 4 + 2 * NV

        def iterations(e, iteration):
            iteration(-1, -1, NC - 1, "A")
            iteration(0, -1, 0, "AB")
            iteration(1, -1, 1, "ABC")
            with e.Fori(0, NI - 1) as im:
                for f in range(NC):
                    iteration(e.snap(im * NC + (f + 2)), im, (f + 2) % NC, "ABCF")
            for f, stages in enumerate(("ABCF", "BCF", "CF", "F")):
                iteration(NCHUNK - 2 + f, NI - 1, (f + 2) % NC, stages)

        def loaded(e, im, c):
            e.wait_ge(x_loaded[(c + 1) % NC], im * (16 * XD) + (((c - 2) % NC + 3) // NC + 1) * 16 * XD)

        def has_pair(stages, i):
            return ("C" if i < 0 else "A" if i == NW else "B") in stages

        @block.sync
        def _(e):
            for dst, n in loads:
                src = w[n] if n != "mask" else w[n][:, 0:NV]
                e.dma_start(dst[:], src).then_inc(w_loaded, 16)
            for b in range(2):
                e.sem_inc(stored[b], 1)

            def pieces(dram, sbt, im, c):
                for h in range(2):
                    sh = sbt[64 * h:64 * h + 64].rearrange("p (r c) -> p r c", c=WW)
                    r0 = c * 8 + h * 32 + (SHIFT if shifted else 0)
                    rows = dram[bass.ds(im, 1), :, r0:r0 + 8].rearrange("a c r w -> (a c) r w")
                    if not shifted:
                        yield rows, sh
                    else:
                        yield rows[:, :, SHIFT:WW], sh[:, :, 0:WW - SHIFT]
                        yield rows[:, :, 0:SHIFT], sh[:, :, WW - SHIFT:WW]

            def load(im, c):
                for dram, sbt in pieces(x_in, x[:, c], im, c):
                    e.dma_start(sbt, dram).then_inc(x_loaded[c], 16)

            def store(im, c):
                e.wait_ge(xo_done, im * NC + (c + 1))
                for dram, sbt in pieces(x_out, xo[:, c % 2], im, c):
                    e.dma_start(dram, sbt).then_inc(stored[c % 2], 16)

            for c in range(NC):
                load(0, c)
            with e.Fori(0, NI - 1) as im:
                for c in range(NC):
                    e.wait_ge(x2_done, im * NC + (c + 1))
                    load(im + 1, c)
                    store(im, c)
            for c in range(NC):
                store(NI - 1, c)
            for b in range(2):
                e.wait_ge(stored[b], NCHUNK // 2 * (16 * XD) + 1)

        @block.gpsimd
        def _(e):
            e.wait_ge(w_loaded, NLOAD)
            e.wait_ge(const_done, CONSTS)

            def power(st, n):
                e.wait_ge(norms_done[st], n * 3 + 2)
                e.tensor_tensor(rstd[:, st], var[:, st], minus_half[:].unsqueeze(1).broadcast_to([128, 4, 2]), ALU.pow)\
                    .then_inc(rs_done[st], 1)

            def iteration(it, im, c, stages):
                for i in range(NW):
                    if has_pair(stages, i + 1):
                        b = (c + (i + 1) // NW) % 2
                        if i + 1 == NW:
                            e.wait_ge(qk_done, it * 2 + 4)
                        e.wait_ge(s_done, it * NW + (i + 2))
                        e.tensor_tensor(kb[:, (i + 1) % 2], k[:, b, (i + 1) % NW].unsqueeze(1).broadcast_to([128, NH, WT]),
                                        hmask[:].unsqueeze(2).broadcast_to([128, NH, WT]), ALU.mult)\
                            .then_inc(kb_done, 1)
                    if "A" in stages and i in (0, 3)[2 - LA:]:
                        power(0, (it + 1) * LA + (i // 3 - (2 - LA)))
                    if "C" in stages and i == 4:
                        power(1, it - 1)

            iterations(e, iteration)

        @block.scalar
        def _(e):
            e.sem_inc(e_done, 2)
            e.wait_ge(w_loaded, NLOAD)

            def squares(st, n):
                e.wait_ge(normv_done[st], n * 2 + 1)
                e.activation(sq[:, st], xc[:, st], ACT.Square).then_inc(norms_done[st], 1)

            def variance(st, n):
                e.wait_ge(norm_ps[st], n * 3 + 2)
                e.activation(var[:, st].rearrange("p a h -> p (a h)"), (lin_c[:] if st else lin_a[:, 0])[:, 0:8],
                             ACT.Copy, bias=EPS).then_inc(norms_done[st], 1)

            def scaled(st, n, which, c):
                e.wait_ge(normv_done[st], n * 2 + 2)
                out, src = h2[:], xn[:, st]
                if which == "norm1":
                    out = hw[:].rearrange("p w (r c) -> p r w c", c=8)
                    src = src.rearrange("p (r w c) -> p r w c", w=NW, c=8)
                elif which == "pe":
                    out = t[:, c]
                e.activation(out, src, ACT.Identity, scale=col(which + "_g"), bias=col(which + "_b"))\
                    .then_inc(norms_done[st], 1)

            def iteration(it, im, c, stages):
                ca = (c + 1) % NC
                for i in range(NW):
                    if has_pair(stages, i - 1):
                        e.wait_ge(tp_done, it * NW + (i - 1 + 1 + 2))
                        e.wait_ge(pv_done, it * NW + (i - 1 + 1))
                        e.activation(pt[:, (i - 1) % 2].rearrange("p a n -> p (a n)"), pt_ps[:, (i - 1) % 2], ACT.Copy)\
                            .then_inc(pt_done, 1)
                    if has_pair(stages, i):
                        e.wait_ge(soft_done, it * (3 * NW) + (3 * i + 3))
                        e.wait_ge(tp_done, it * NW + (i + 1))
                        e.activation(p[:, i % 2], s2[:, i % 2].rearrange("p h m -> p (h m)"), ACT.Exp)\
                            .then_inc(e_done, 1)
                    if "C" in stages:
                        j = it - 1
                        if i == 1:
                            e.wait_ge(ot_ps, j + 2)
                            e.activation(ot[:].rearrange("p h r w c -> p w (h r) c"),
                                         lin_c[:].rearrange("p (w a c) -> p w a c", w=4, c=8), ACT.Copy)\
                                .then_inc(ot_done, 1)
                        elif i == 3:
                            squares(1, j)
                        elif i == 4:
                            variance(1, j)
                        elif i == 5:
                            scaled(1, j, "norm2", None)
                        elif i == 7:
                            for h in range(2):
                                e.wait_ge(fc1_ps, it * 2 + (h - 1))
                                e.activation(g[:, h], lin_a[:, 1] if h else lin_c[:], ACT.Gelu, bias=col("fc1_b"))\
                                    .then_inc(g_done, 1)
                    if "A" in stages:
                        for l, i0 in enumerate((0, 2)[2 - LA:]):
                            n = (it + 1) * LA + l
                            if i == i0:
                                squares(0, n)
                            if i == i0 + (1 if i0 else 0):
                                variance(0, n)
                            if i == i0 + (2 if i0 else 1):
                                scaled(0, n, LN[l], ca)

            iterations(e, iteration)

        @block.vector
        def _(e):
            e.memset(minus_half[:], -0.5).then_inc(const_done, 1)
            e.memset(v[:], 0.0).then_inc(const_done, 1)
            e.wait_ge(const_done, 2)
            for par in range(2):
                e.memset(v[64 * par:64 * par + 64].rearrange("p u h w a b d -> p (u h w a) b d")[:, :, par, HD:HD + 1],
                         1.0).then_inc(const_done, 1)
            e.wait_ge(w_loaded, NLOAD)
            for a in range(NV):
                for b in range(2):
                    e.tensor_tensor(bias[:, a, b], rel[:], mask[:, a, b:b + 1].broadcast_to([128, NH, WT]), ALU.add)\
                        .then_inc(const_done, 1)
            e.wait_ge(const_done, CONSTS)

            def centre(st, n, src):
                e.wait_ge(norm_ps[st], n * 3 + 1)
                e.tensor_tensor(xc[:, st], src, lin_c[:] if st else lin_a[:, 0], ALU.subtract).then_inc(normv_done[st], 1)

            def normal(st, n):
                e.wait_ge(norm_ps[st], n * 3 + 3)
                e.tensor_tensor(xn[:, st], xc[:, st], lin_c[:] if st else lin_a[:, 0], ALU.mult).then_inc(normv_done[st], 1)

            def outputs(it, group):
                n, b = it * 4 + group, group % 4
                e.wait_ge(pv_done, n * 2 + 4)
                if group == 0:
                    e.wait_ge(ot_ps, it + 1)
                ob = o_ps[:, (b % 2) * 8 * OC:(b % 2) * 8 * OC + 8 * OC].rearrange("p (a b d) -> p a b d", b=2, d=HD + 1)
                r = rz[:, b % 2].rearrange("p (a b) -> p a b", b=2)
                e.reciprocal(r, ob[:, :, :, HD]).then_inc(out_done, 1)
                e.wait_ge(out_done, n * 2 + 1)
                e.tensor_tensor(o[:, 2 * b:2 * b + 2].rearrange("p w (a b d) -> p (w a) b d", b=2, d=HD),
                                ob[:, :, :, 0:HD], r.unsqueeze(3).broadcast_to([128, 8, 2, HD]), ALU.mult)\
                    .then_inc(out_done, 1)

            def iteration(it, im, c, stages):
                ca = (c + 1) % NC
                src_a = [x, t][2 - LA:]
                for i in range(NW):
                    if has_pair(stages, i):
                        n = it * NW + i
                        e.wait_ge(s_done, n + 3)
                        b = bias[:, c if shifted else 0, i // (NW - 1) if shifted else 0]
                        e.tensor_tensor(s1[:, i % 2], s_ps[:, i % 2].rearrange("p (h m) -> p h m", h=NH), b, ALU.add)\
                            .then_inc(soft_done, 1)
                        e.wait_ge(soft_done, n * 3 + 1)
                        e.reduce_max(nmx[:, i % 2], s1[:, i % 2], AXX, negate=True).then_inc(soft_done, 1)
                        e.wait_ge(soft_done, n * 3 + 2)
                        e.wait_ge(e_done, n + 1)
                        e.tensor_tensor(s2[:, i % 2], s1[:, i % 2], nmx[:, i % 2].unsqueeze(2)
                                        .broadcast_to([128, NH, WT]), ALU.add).then_inc(soft_done, 1)
                    if "F" in stages and i == 0:
                        e.wait_ge(fc2_ps, it - 1)
                        e.wait_ge(stored[c % 2], im * (2 * 16 * XD) + ((c - 2) % NC // 2 * (16 * XD) + 1))
                        e.scalar_tensor_tensor(xo[:, c % 2], lin_c[:], col("fc2_b"), x2[:], ALU.add, ALU.add)\
                            .then_inc(xo_done, 1)
                    if "C" in stages:
                        j = it - 1
                        if i == 2:
                            e.wait_ge(proj_ps, it)
                            e.scalar_tensor_tensor(x2[:], lin_c[:], col("proj_b"), t[:, (c - 1) % NC], ALU.add, ALU.add)\
                                .then_inc(x2_done, 1)
                        elif i == 3:
                            centre(1, j, x2[:])
                        elif i == 5:
                            normal(1, j)
                    if "A" in stages:
                        if i == 0:
                            loaded(e, im, c)
                        for l, i0 in enumerate((0, 2)[2 - LA:]):
                            if i == i0:
                                centre(0, (it + 1) * LA + l, src_a[l][:, ca])
                            if i == i0 + (2 if i0 else 1):
                                normal(0, (it + 1) * LA + l)
                        if i == 5:
                            e.wait_ge(qk_ps, it * 2 + 3)
                            e.tensor_scalar(q[:, ca % 2].rearrange("p w n -> p (w n)"), lin_a[:, 1], col("q_b"), SCALE,
                                            ALU.add, ALU.mult).then_inc(qk_done, 1)
                            e.wait_ge(qk_ps, it * 2 + 4)
                            e.tensor_scalar(k[:, ca % 2].rearrange("p w n -> p (w n)"), lin_a[:, 0], col("k_b"), None,
                                            ALU.add).then_inc(qk_done, 1)
                        if i == 6:
                            for h in range(2):
                                e.wait_ge(v_ps, it * 2 + (h + 3))
                                for par in range(2):
                                    r = slice(64 * par, 64 * par + 64)
                                    e.tensor_tensor(
                                        v[r, ca % 2, h, :, :, par, 0:HD],
                                        lin_a[r, 1 - h].rearrange("p (w a b d) -> p w a b d", w=NW, b=2, d=HD)[:, :, :, par],
                                        vb[r].rearrange("p (a b d) -> p a b d", b=2, d=HD)[:, :, par].unsqueeze(1)
                                        .broadcast_to([64, NW, 4, HD]), ALU.add).then_inc(v_done, 1)
                    if i % 2 == 0 and has_pair(stages, i - 1):
                        outputs(it, i // 2 - 1)

            iterations(e, iteration)

        @block.tensor
        def _(e):
            e.sem_inc(s_done, 2)
            e.sem_inc(tp_done, 2)
            e.sem_inc(pv_done, 2)
            e.sem_inc(ot_ps, 1)
            e.wait_ge(w_loaded, NLOAD)
            e.wait_ge(const_done, CONSTS)

            def mean(st, src):
                e.matmul(lin_c[:] if st else lin_a[:, 0], mean_w[:], src, start=True, stop=True).then_inc(norm_ps[st], 1)

            def square_sums(st, n):
                e.wait_ge(norms_done[st], n * 3 + 1)
                bank = lin_c[:] if st else lin_a[:, 0]
                for a in range(4):
                    ins = e.matmul(bank[:, 2 * a:2 * a + 2], sq[:, st, a * 128:a * 128 + 128], half_w[:],
                                   start=True, stop=True)
                ins.then_inc(norm_ps[st], 1)

            def spread(st, n):
                e.wait_ge(rs_done[st], n + 1)
                for a in range(4):
                    for h in range(2):
                        r = slice(64 * h, 64 * h + 64)
                        bank = lin_c[r] if st else lin_a[r, 0]
                        ins = e.matmul(bank[:, a * 128:a * 128 + 128], rstd[:, st, a, h:h + 1].broadcast_to([128, 64]),
                                       ident[:], start=True, stop=True)
                ins.then_inc(norm_ps[st], 1)

            def third(it, i):
                return not isinstance(it, int) or it * NW + i >= 2

            def scores(it, i, b):
                e.wait_ge(kb_done, it * NW + (i + 1))
                if third(it, i):
                    e.wait_ge(soft_done, it * (3 * NW) + (3 * i - 5))
                own_wait(e)
                for h in range(2):
                    r = slice(64 * h, 64 * h + 64)
                    ins = e.matmul(s_ps[r, i % 2], q[r, b, i % NW], kb[r, i % 2].rearrange("p h m -> p (h m)"),
                                   start=True, stop=True)
                ins.then_inc(s_done, 1)

            def transposes(it, i):
                e.wait_ge(e_done, it * NW + (i + 1 + 2))
                if third(it, i):
                    e.wait_ge(pt_done, it * NW + (i - 1))
                for a in range(4):
                    ins = e.transpose(pt_ps[:, i % 2, a * 128:a * 128 + 128], p[:, i % 2, a * 128:a * 128 + 128],
                                      ident[:])
                ins.then_inc(tp_done, 1)

            def products(it, i, b):
                w = i % NW
                if w == 0:
                    e.wait_ge(v_done, it * 4 + 4)
                if w % 2 == 0 and (i >= 4 or not isinstance(it, int) or it > 0):
                    e.wait_ge(out_done, it * 8 + (i // 2 * 2 - 2))
                e.wait_ge(pt_done, it * NW + (i + 1))
                for a in range(4):
                    for h in range(2):
                        o0 = (w % 4) * 4 * OC + a * OC
                        ins = e.matmul(o_ps[64 * h:64 * h + 64, o0:o0 + OC], pt[:, w % 2, a, 64 * h:64 * h + 64],
                                       v[:, b, h, w, a].rearrange("p b d -> p (b d)"), start=True, stop=True)
                ins.then_inc(pv_done, 1)

            def visit_a(it, im, c, i, before):
                n, ca = (it + 1) * LA, (c + 1) % NC
                if not before:
                    if LA == 2 and i == 0:
                        square_sums(0, n)
                    return
                l = LA - 1
                if i == (0 if LA == 2 else 2):
                    loaded(e, im, c)
                    if not isinstance(it, int) or it >= 0:
                        e.wait_ge(v_done, it * 4 + 4)
                    mean(0, x[:, ca])
                elif i == 1 and LA == 2:
                    spread(0, n)
                elif i == 2:
                    e.wait_ge(norms_done[0], n * 3 + 3)
                    mean(0, t[:, ca])
                elif i == 3:
                    square_sums(0, n + l)
                elif i == 4:
                    spread(0, n + l)
                elif i == 5:
                    e.wait_ge(norms_done[0], n * 3 + 3 * LA)
                    if not isinstance(it, int) or it >= 2:
                        e.wait_ge(g_done, it * 2 - 2)
                    for j in range(2):
                        e.matmul(lin_a[:, 1 - j], wqk[:, j], hw[:].rearrange("p w n -> p (w n)"), start=True, stop=True)\
                            .then_inc(qk_ps, 1)
                elif i == 6:
                    for h in range(2):
                        e.wait_ge(qk_done, it * 2 + (h + 3))
                        own_wait(e)
                        r = slice(64 * h, 64 * h + 64)
                        for w in range(NW):
                            for par in range(2):
                                ins = e.matmul(lin_a[64 * par:64 * par + 64, 1 - h, w * C:w * C + C], hw[r, w], wv[r],
                                               start=True, stop=True)
                        ins.then_inc(v_ps, 1)

            def visit_c(it, i, last):
                j = it - 1
                if i == 1:
                    e.wait_ge(out_done, it * 8)
                    if not isinstance(it, int) or it > 1:
                        e.wait_ge(xo_done, it - 1)
                    own_wait(e)
                    for a in range(NW // 2):
                        ins = e.transpose(lin_c[:, a * 128:a * 128 + 128],
                                          o[:, 2 * a:2 * a + 2].rearrange("p w c -> p (w c)"), ident[:])
                    ins.then_inc(ot_ps, 1)
                elif i == 2:
                    e.wait_ge(ot_done, it)
                    own_wait(e)
                    for b in range(2):
                        for h in range(2):
                            ins = e.matmul(
                                lin_c[64 * h:64 * h + 64].rearrange("p (r a b c) -> p r a b c", r=8, b=2, c=8)[:, :, :, b],
                                wp[:, b], ot[:, h],
                                start=True, stop=True)
                    ins.then_inc(proj_ps, 1)
                elif i == 3:
                    e.wait_ge(x2_done, it)
                    mean(1, x2[:])
                elif i == 4:
                    square_sums(1, j)
                elif i == 5:
                    spread(1, j)
                elif i == 7:
                    e.wait_ge(norms_done[1], it * 3)
                    e.wait_ge(v_done, it * 4 + 8 if not last else NCHUNK * 4)
                    own_wait(e)
                    for h in range(2):
                        r = slice(64 * h, 64 * h + 64)
                        e.matmul(lin_a[:, 1] if h else lin_c[:], w1[r], h2[r], start=True, stop=True).then_inc(fc1_ps, 1)

            def iteration(it, im, c, stages):
                for i in range(NW):
                    if "F" in stages and i == 0:
                        for h in range(2):
                            e.wait_ge(g_done, it * 2 + (h - 3))
                            ins = e.matmul(lin_c[64 * h:64 * h + 64], w2[:], g[:, h], start=True, stop=True)
                        ins.then_inc(fc2_ps, 1)
                    if "C" in stages:
                        visit_c(it, i, "A" not in stages)
                    if has_pair(stages, i + 1):
                        scores(it, i + 1, (c + (i + 1) // NW) % 2)
                    if "A" in stages:
                        visit_a(it, im, c, i, True)
                    if has_pair(stages, i):
                        transposes(it, i)
                    if has_pair(stages, i - 1):
                        products(it, i - 1, (c - (i == 0)) % 2)
                    if "A" in stages:
                        visit_a(it, im, c, i, False)

            iterations(e, iteration)


def _adaptive_blur(nc, keep, x_in, w, x_out):
    TS = NT // 128
    HT = TS // 2
    ND = 5
    NB = 8
    HID = 32
    NTAP = 81
    with ExitStack() as ctx:
        sb = lambda n, s, d=F32: ctx.enter_context(nc.sbuf_tensor("bl_" + n, s, d))
        sem = lambda n: keep.enter_context(nc.semaphore("bl_" + n))
        ps = lambda n, s: ctx.enter_context(nc.psum_tensor("bl_" + n, s, F32))
        x = sb("x", [128, NT // 2])
        w1 = sb("w1", [128, HID])
        b1 = sb("b1", [HID, 1])
        w2 = sb("w2", [HID, 1])
        b2 = sb("b2", [128, 1])
        taps = sb("taps", [NTAP, 1])
        ntaps = sb("ntaps", [NTAP, 1])
        dist = sb("dist", [128, ND, 128])
        ndist = sb("ndist", [128, ND * 128])
        ident = sb("ident", [128, 128])
        fold = sb("fold", [128, 128])
        ones = sb("ones", [NTAP, 1])
        hid = sb("hid", [HID, NT])
        kc = sb("kc", [128, 4, TS])
        sc = sb("sc", [128, TS])
        s = sb("s", [128, (TS + 4) * 128])
        e81 = sb("e81", [NTAP, 2, CH])
        rzc = sb("rzc", [128, TS])
        xt = sb("xt", [128, HT, 128])
        lg = sb("lg", [128, 2, ND * 128])
        f = sb("f", [128, NB, ND * 128])
        rz = sb("rz", [128, 2, CH])
        low = sb("low", [128, 2, CH])
        enh = sb("enh", [128, NT // 2])
        cen = sb("cen", [128, NT // 2])
        sq = sb("sq", [128, NT // 2])
        out = sb("out", [128, NT // 2])
        stat = sb("stat", [128, 4])
        half = sb("half", [128, 1])
        ring = ps("ring", [128, 2, CH])
        acc = ps("acc", [128, 2, CH])
        rz_ps = ps("rz_ps", [128, 2, CH])
        small = ps("small", [128, CH])

        names = ("w_loaded", "const_done", "x_loaded", "h_ps", "h_done", "ks_ps", "kc_done", "sc_done", "sbc_ps",
                 "sbc_done", "e81_done", "z_ps", "rzc_done", "xt_ps", "xt_done", "lg_done", "f_done", "acc_done",
                 "rz_ps_done", "rz_done", "low_done", "enh_done", "sum_done", "mean_ps", "cen_done", "ssq_done",
                 "var_ps", "var_done", "rstd_done", "out_done", "stored", "passed")
        (w_loaded, const_done, x_loaded, h_ps, h_done, ks_ps, kc_done, sc_done, sbc_ps, sbc_done, e81_done, z_ps,
         rzc_done, xt_ps, xt_done, lg_done, f_done, acc_done, rz_ps_done, rz_done, low_done, enh_done, sum_done,
         mean_ps, cen_done, ssq_done, var_ps, var_done, rstd_done, out_done, stored, passed) = [sem(n) for n in names]
        block = ctx.enter_context(nc.Block())
        NG = NCH
        loads = [(w1, "b_w1"), (b1, "b_b1"), (w2, "b_w2"), (b2, "b_b2"), (taps, "b_taps"), (dist, "b_dist"),
                 (ident, "ident"), (fold, "b_fold")]
        NLOAD = 16 * len(loads)

        def at(g):
            return slice(64 * (g // 4), 64 * (g // 4) + 64), slice((g % 4) * CH, (g % 4) * CH + CH)

        def alone(e):
            e.sem_inc(passed, 1)

        @block.sync
        def _(e):
            for dst, n in loads:
                e.dma_start(dst[:], w[n]).then_inc(w_loaded, 16)
            e.sem_inc(enh_done, 1)
            e.sem_inc(stored, 1)
            with e.Fori(0, NI) as im:
                e.wait_ge(enh_done, im * NG + 1)
                for h in range(2):
                    e.dma_start(x[64 * h:64 * h + 64],
                                x_in[bass.ds(im, 1), :, h * (NT // 2):(h + 1) * (NT // 2)]
                                .rearrange("a c n -> (a c) n")).then_inc(x_loaded, 16)
                e.wait_ge(out_done, im + 1)
                for h in range(2):
                    e.dma_start(x_out[bass.ds(im, 1), :, h * (NT // 2):(h + 1) * (NT // 2)]
                                .rearrange("a c n -> (a c) n"), out[64 * h:64 * h + 64]).then_inc(stored, 16)
            e.wait_ge(stored, NI * 32 + 1)

        @block.gpsimd
        def _(e):
            e.wait_ge(const_done, 4)
            with e.Fori(0, NI) as im:
                e.wait_ge(var_done, im + 1)
                e.tensor_tensor(stat[:, 3:4], stat[:, 2:3], half[:], ALU.pow).then_inc(rstd_done, 1)

        @block.scalar
        def _(e):
            e.wait_ge(w_loaded, NLOAD)
            e.wait_ge(const_done, 6)
            with e.Fori(0, NI) as im:
                for g in range(NG):
                    e.wait_ge(h_ps, im * NG + g + 1)
                    e.activation(hid[:, g * CH:g * CH + CH], ring[0:HID, g % 2], ACT.Relu, bias=b1[:])\
                        .then_inc(h_done, 1)
                for g in range(NG):
                    e.wait_ge(sbc_ps, im * NG + g + 1)
                    if g >= 2:
                        e.wait_ge(z_ps, im * NG + g - 1)
                    e.activation(s[:, (2 * 128) + g * CH:(2 * 128) + g * CH + CH], ring[:, g % 2], ACT.Copy)\
                        .then_inc(sbc_done, 1)
                    e.activation(e81[:, g % 2], ring[0:NTAP, g % 2], ACT.Exp, scale=ntaps[:]).then_inc(e81_done, 1)

                def spread(g):
                    r, _ = at(g)
                    e.wait_ge(rz_ps_done, im * NG + g + 1)
                    if g >= 2:
                        e.wait_ge(low_done, im * NG + g - 1)
                    e.activation(rz[r, g % 2], rz_ps[r, g % 2], ACT.Copy).then_inc(rz_done, 1)

                for t in range(TS):
                    e.wait_ge(lg_done, im * TS + t + 1)
                    if t >= NB:
                        e.wait_ge(acc_done, im * TS + t - NB + 3)
                    e.activation(f[:, t % NB], lg[:, t % 2], ACT.Exp).then_inc(f_done, 1)
                    if t % 4 == 3:
                        spread(t // 4)
                e.wait_ge(cen_done, im + 1)
                e.activation(sq[:], cen[:], ACT.Square, accum_out=stat[:, 1:2]).then_inc(ssq_done, 1)

        @block.vector
        def _(e):
            e.memset(half[:], -0.5).then_inc(const_done, 1)
            e.memset(ones[:], 1.0).then_inc(const_done, 1)
            e.memset(s[:, 0:256], 0.0).then_inc(const_done, 1)
            e.memset(s[:, 256 + NT:512 + NT], 0.0).then_inc(const_done, 1)
            e.wait_ge(w_loaded, NLOAD)
            e.tensor_scalar(ntaps[:], taps[:], -1.0, None, ALU.mult).then_inc(const_done, 1)
            e.tensor_scalar(ndist[:], dist[:].rearrange("p a b -> p (a b)"), -1.0, None, ALU.mult)\
                .then_inc(const_done, 1)
            e.wait_ge(const_done, 6)
            with e.Fori(0, NI) as im:
                e.wait_ge(ks_ps, im + 1)
                steps = [
                    lambda: e.tensor_scalar(kc[:, 0], small[:, 0:TS], b2[:], 0.0, ALU.add, ALU.max),
                    lambda: e.tensor_scalar(kc[:, 1], kc[:, 0], 20.0, 1.0, ALU.mult, ALU.add),
                    lambda: e.tensor_tensor(kc[:, 2], kc[:, 1], kc[:, 1], ALU.mult),
                    lambda: e.reciprocal(kc[:, 3], kc[:, 2])]
                for n, make in enumerate(steps):
                    make().then_inc(kc_done, 1)
                    e.wait_ge(kc_done, im * 4 + n + 1)
                e.tensor_scalar(sc[:], kc[:, 3], 4.5, None, ALU.mult).then_inc(sc_done, 1)
                for g in range(4):
                    e.wait_ge(xt_ps, im * 4 + g + 1)
                    e.tensor_copy(xt[:, 4 * g:4 * g + 4].rearrange("p a b -> p (a b)"), ring[:, g % 2])\
                        .then_inc(xt_done, 1)
                e.wait_ge(z_ps, im * NG + NG)
                e.reciprocal(rzc[:], small[:, TS:2 * TS]).then_inc(rzc_done, 1)
                e.wait_ge(sbc_done, im * NG + NG)

                def enhance(g):
                    r, c = at(g)
                    e.wait_ge(rz_done, im * NG + g + 1)
                    e.wait_ge(acc_done, im * TS + 4 * g + 4)
                    e.tensor_tensor(low[r, g % 2], acc[r, g % 2], rz[r, g % 2], ALU.mult).then_inc(low_done, 1)
                    e.wait_ge(low_done, im * NG + g + 1)
                    e.tensor_tensor(enh[r, c], low[r, g % 2], x[r, c], ALU.add).then_inc(enh_done, 1)

                for t in range(TS):
                    if t >= 2:
                        e.wait_ge(f_done, im * TS + t - 1)
                    e.tensor_tensor(lg[:, t % 2], ndist[:], s[:, t * 128:t * 128 + ND * 128], ALU.mult)\
                        .then_inc(lg_done, 1)
                    if t % 4 == 3 and t > 4:
                        enhance(t // 4 - 1)
                enhance(NG - 1)
                e.wait_ge(enh_done, im * NG + NG + 1)
                e.reduce_sum(stat[:, 0:1], enh[:], AXX).then_inc(sum_done, 1)
                e.wait_ge(mean_ps, im + 1)
                e.tensor_scalar(cen[:], enh[:], small[:, 2 * TS:2 * TS + 1], None, ALU.subtract).then_inc(cen_done, 1)
                e.wait_ge(var_ps, im + 1)
                e.tensor_scalar(stat[:, 2:3], small[:, 2 * TS + 1:2 * TS + 2], 1e-5, None, ALU.add)\
                    .then_inc(var_done, 1)
                e.wait_ge(rstd_done, im + 1)
                e.wait_ge(stored, im * 32 + 1)
                e.tensor_scalar(out[:], cen[:], stat[:, 3:4], None, ALU.mult).then_inc(out_done, 1)

        @block.tensor
        def _(e):
            e.wait_ge(w_loaded, NLOAD)
            e.wait_ge(const_done, 6)
            with e.Fori(0, NI) as im:
                e.wait_ge(x_loaded, im * 32 + 32)
                alone(e)
                for g in range(NG):
                    r, c = at(g)
                    if g >= 2:
                        e.wait_ge(h_done, im * NG + g - 1)
                        alone(e)
                    e.matmul(ring[0:HID, g % 2], w1[r], x[r, c], start=True, stop=True).then_inc(h_ps, 1)
                e.wait_ge(h_done, im * NG + NG)
                alone(e)
                for t in range(TS):
                    ins = e.matmul(small[:, t:t + 1], hid[:, t * 128:t * 128 + 128], w2[:], start=True, stop=True)
                ins.then_inc(ks_ps, 1)
                for g in range(4):
                    if g >= 2:
                        e.wait_ge(xt_done, im * 4 + g - 1)
                        alone(e)
                    for t in range(4 * g, 4 * g + 4):
                        ins = e.transpose(ring[:, g % 2, (t % 4) * 128:(t % 4) * 128 + 128],
                                          x[:, t * 128:t * 128 + 128], ident[:])
                    ins.then_inc(xt_ps, 1)

                def sums(g):
                    e.wait_ge(e81_done, im * NG + g + 1)
                    alone(e)
                    for t in range(4 * g, 4 * g + 4):
                        ins = e.matmul(small[:, TS + t:TS + t + 1], e81[:, g % 2, (t % 4) * 128:(t % 4) * 128 + 128],
                                       ones[:], start=True, stop=True)
                    ins.then_inc(z_ps, 1)

                e.wait_ge(sc_done, im + 1)
                e.wait_ge(xt_done, im * 4 + 4)
                for g in range(NG):
                    if g >= 2:
                        sums(g - 2)
                    for t in range(4 * g, 4 * g + 4):
                        ins = e.matmul(ring[:, g % 2, (t % 4) * 128:(t % 4) * 128 + 128],
                                       sc[:, t:t + 1].broadcast_to([128, 128]), ident[:], start=True, stop=True)
                    ins.then_inc(sbc_ps, 1)
                sums(NG - 2)
                sums(NG - 1)
                e.wait_ge(rzc_done, im + 1)
                alone(e)

                def spread(g):
                    r, _ = at(g)
                    if g >= 2:
                        e.wait_ge(rz_done, im * NG + g - 1)
                        alone(e)
                    for t in range(4 * g, 4 * g + 4):
                        ins = e.matmul(rz_ps[r, g % 2, (t % 4) * 128:(t % 4) * 128 + 128],
                                       rzc[:, t:t + 1].broadcast_to([128, C]), ident[:], start=True, stop=True)
                    ins.then_inc(rz_ps_done, 1)

                for t in range(TS):
                    g = t // 4
                    r, _ = at(g)
                    if t % 4 == 0:
                        spread(g)
                        if g >= 2:
                            e.wait_ge(low_done, im * NG + g - 1)
                    e.wait_ge(f_done, im * TS + min(t + 3, TS))
                    alone(e)
                    reach = [q for q in range(t - 2, t + 3) if 0 <= q < TS]
                    for q in reach:
                        ins = e.matmul(acc[r, g % 2, (t % 4) * 128:(t % 4) * 128 + 128],
                                       xt[:, q % HT, 64 * (q // HT):64 * (q // HT) + 64],
                                       f[:, q % NB, (t - q + 2) * 128:(t - q + 2) * 128 + 128],
                                       start=q == reach[0], stop=q == reach[-1])
                    ins.then_inc(acc_done, 1)
                e.wait_ge(sum_done, im + 1)
                alone(e)
                e.matmul(small[:, 2 * TS:2 * TS + 1], fold[:], stat[:, 0:1], start=True, stop=True).then_inc(mean_ps, 1)
                e.wait_ge(ssq_done, im + 1)
                alone(e)
                e.matmul(small[:, 2 * TS + 1:2 * TS + 2], fold[:], stat[:, 1:2], start=True, stop=True)\
                    .then_inc(var_ps, 1)


def _copy_rows(nc, keep, name, rows_from, rows_to):
    done = keep.enter_context(nc.semaphore(name))
    with nc.Block() as block:
        @block.sync
        def _(e):
            e.dma_start(rows_to, rows_from).then_inc(done, 16)
            e.wait_ge(done, 16)


def conv_attention_swin_blur(nc, x, wt, out):
    S = SHIFT
    scratch = lambda n, shape: nc.dram_tensor(n, shape, F32, kind="Internal").ap()
    x1 = scratch("after_attention0", (NI, C, NT))
    x2 = scratch("after_attention1", (NI, C, HH, WW))
    x3 = scratch("after_swin", (NI, C, HH + S, WW))
    x4 = scratch("after_shifted_swin", (NI, C, HH + S, WW))
    pixels = lambda a: a.rearrange("i c h w -> i c (h w)")
    with ExitStack() as keep:
        _attention0(nc, keep, pixels(x), wt, x1)
        _attention1(nc, keep, x1, wt, pixels(x2))
        _swin(nc, keep, "w0", x2, {**wt, **{n: wt[n + "_0"] for n in SWIN_WEIGHTS}}, x3, False)
        _copy_rows(nc, keep, "x3_rows", x3[:, :, 0:S], x3[:, :, HH:HH + S])
        _swin(nc, keep, "w1", x3, {**wt, **{n: wt[n + "_1"] for n in SWIN_WEIGHTS}}, x4, True)
        _copy_rows(nc, keep, "x4_rows", x4[:, :, HH:HH + S], x4[:, :, 0:S])
        _adaptive_blur(nc, keep, x4[:, :, 0:HH].rearrange("i c h w -> i c (h w)"), wt, pixels(out))


SWIN_WEIGHTS = ("cols", "wqk2", "wv2", "vb2", "wp2", "w12", "w22", "rel")


def _layouts(inputs):
    import numpy as np
    f32 = np.float32
    with_bias = lambda m, b: np.concatenate([m.T, b[None]], 0)
    twice = lambda m: np.concatenate([m, m])

    def blocks(m):
        z = np.zeros_like(m)
        return np.block([[m, z], [z, m]])

    def four(m, b):
        a = np.zeros((C + 1, 4, 32), f32)
        a[:, :, 0:8] = with_bias(m, b)[:, None]
        return a.reshape(C + 1, 128)

    a = {}
    g = lambda n: np.asarray(inputs["L0_conv_" + n])
    a["wqk"] = np.stack([np.tile(with_bias(g("w" + n), g("b" + n)), (1, 3)) for n in "12"], 1)
    a["wv"] = with_bias(g("w3"), g("b3"))
    a["al"] = np.tile(np.concatenate([g("a1"), g("a2"), g("a3")])[None], (128, 1))
    g = lambda n: np.asarray(inputs["L1_conv_" + n])
    a["wqk1"] = np.stack([four(g("Wq"), g("bq")), four(g("Wk"), g("bk"))], 1)
    a["wv1"] = with_bias(g("Wv"), g("bv"))

    g = lambda n: np.asarray(inputs["L2_conv_" + n])
    at = np.stack(np.meshgrid(np.arange(8), np.arange(8), indexing="ij")).reshape(2, -1)
    dy, dx = at[:, :, None] - at[:, None, :] + 7
    for b in range(2):
        qw, qb = g("qkv_w")[b], g("qkv_b")[b]
        norms = [g("pe_g"), g("pe_b"), g("norm1_g")[b], g("norm1_b")[b], g("norm2_g")[b], g("norm2_b")[b]]
        a[f"cols_{b}"] = np.stack([twice(v) for v in norms + [qb[0:C], qb[C:2 * C], g("proj_b")[b]]]
                                  + [g("fc1_b")[b], twice(g("fc2_b")[b])], 1)
        a[f"wqk2_{b}"] = np.stack([blocks(qw[:, 0:C]), blocks(qw[:, C:2 * C])], 1)
        a[f"wv2_{b}"] = twice(qw[:, 2 * C:])
        a[f"vb2_{b}"] = np.tile(qb[2 * C:], (128, 1))
        a[f"wp2_{b}"] = blocks(g("proj_w")[b]).reshape(128, 2, C)
        a[f"w12_{b}"] = twice(g("fc1_w")[b])
        a[f"w22_{b}"] = g("fc2_w")[b]
        a[f"rel_{b}"] = np.tile(g("rpb")[b][dy * 15 + dx].transpose(0, 2, 1), (2, 1, 1))
    region = np.zeros((HH, WW))
    edges = (slice(0, -8), slice(-8, -4), slice(-4, None))
    for i, rows in enumerate(edges):
        for j, columns in enumerate(edges):
            region[rows, columns] = 3 * i + j
    region = region.reshape(8, 8, 8, 8).transpose(0, 2, 1, 3).reshape(8, 8, 64)
    mask = np.where(region[:, :, None] != region[..., None], f32(-100), f32(0))
    a["mask"] = mask.reshape(2, 4, 8, 64, 64)[:, :, [0, 7]].transpose(0, 3, 1, 2, 4).reshape(128, 4, 2, 64)
    a["mean_w"] = blocks(np.full((64, 64), 1 / 64, f32))
    a["half_w"] = a["mean_w"][:, [0, 64]]
    a["hmask"] = twice((np.arange(C)[:, None] // 8 == np.arange(8)).astype(f32))
    a["ident"] = np.eye(128, dtype=f32)

    g = lambda n: np.asarray(inputs["L3_conv_" + n])
    q, p = np.arange(128)[:, None], np.arange(128)[None]
    dist = np.full((128, 5, 128), 1e30, f32)
    for d in range(5):
        u, v = q // 64 - p // 64 - 2 * (d - 2) + 4, q % 64 - p % 64 + 4
        near = (u >= 0) & (u < 9) & (v >= 0) & (v < 9)
        dist[:, d][near] = g("gauss_kernel")[u[near], v[near]]
    a["b_dist"] = dist
    a["b_taps"] = g("gauss_kernel").reshape(81, 1)
    a["b_w1"], a["b_b1"], a["b_w2"] = twice(g("w1")), g("b1")[:, None], g("w2")
    a["b_b2"] = np.tile(g("b2")[None], (128, 1))
    a["b_fold"] = np.tile(np.eye(C, dtype=f32), (2, 2)) / f32(NT)
    return {n: np.ascontiguousarray(v, f32) for n, v in a.items()}


def kernel(**inputs):
    import numpy as np
    import concourse.bacc as bacc
    from concourse.bass_utils import run_bass_kernel_spmd

    nc = bacc.Bacc("TRN2", target_bir_lowering=False, num_devices=1)
    arrays = {"x": np.ascontiguousarray(inputs["x"]), **_layouts(inputs)}
    aps = {n: nc.dram_tensor(n, a.shape, mybir.dt.from_np(a.dtype), kind="ExternalInput").ap()
           for n, a in arrays.items()}
    out = nc.dram_tensor("out", (NI, C, HH, WW), F32, kind="ExternalOutput").ap()
    conv_attention_swin_blur(nc, aps.pop("x"), aps, out)
    r = run_bass_kernel_spmd(nc, [arrays], core_ids=[0])
    return r.results[0]["out"]
```

```python
from contextlib import ExitStack

import concourse.bass as bass
from concourse import mybir

F32 = mybir.dt.float32
F16 = mybir.dt.float16
ALU = mybir.AluOpType
ACT = mybir.ActivationFunctionType
AXX = mybir.AxisListType.X

NI, C, HH, WW = 8, 64, 64, 64
NT = HH * WW
CH = 512
NCH = NT // CH
KT = NT // 128
SHIFT = 4


def _attention0(nc, keep, x_in, w, x_out):
    UQ = 1024
    NU = NT // UQ
    QT = UQ // 128
    ASTEPS = QT * NCH
    MS = 64.0
    NP = 4
    GV = KT // 8
    with ExitStack() as ctx:
        sb = lambda n, s, d=F32: ctx.enter_context(nc.sbuf_tensor("a0_" + n, s, d))
        sem = lambda n: keep.enter_context(nc.semaphore("a0_" + n))
        xa = sb("xa", [128, NT])
        xr = sb("xr", [128, NU, CH])
        wqk = sb("wqk", [128, 2, 96])
        wv = sb("wv", [128, C])
        al = sb("al", [128, 3])
        rest = sb("rest", [128, 3])
        ident = sb("ident", [128, 128])
        ones = sb("ones", [128, C])
        raw = sb("raw", [96, 2, 2, CH])
        neg = sb("neg", [96, 2, 2, CH])
        negv = sb("negv", [128, 2, CH])
        qs = sb("qs", [97, NT], F16)
        ks = sb("ks", [97, NT], F16)
        vt = sb("vt", [128, KT, C])
        p = sb("p", [128, NP, UQ])
        sum_d = sb("sum_d", [128, UQ])
        sum_p = sb("sum_p", [128, UQ])
        mparts = sb("mparts", [128, QT, NCH])
        mneg = sb("mneg", [128, QT])
        rden = sb("rden", [128, QT])
        accs = sb("accs", [128, CH])
        att = sb("att", [128, CH])
        res = sb("res", [128, CH])
        a_ps = ctx.enter_context(nc.psum_tensor("a0_a_ps", [128, 2, CH], F32))
        b_ps = ctx.enter_context(nc.psum_tensor("a0_b_ps", [128, 2, 2, CH], F32))
        acc = ctx.enter_context(nc.psum_tensor("a0_acc", [128, CH], F32))
        den = ctx.enter_context(nc.psum_tensor("a0_den", [128, CH], F32))

        w_loaded = sem("w_loaded")
        xa_loaded, xr_loaded = sem("xa_loaded"), sem("xr_loaded")
        const_done = sem("const_done")
        proj_done = sem("proj_done")
        neg_done = sem("neg_done")
        raw_done, hi_done, split_done = sem("raw_done"), sem("hi_done"), sem("split_done")
        vt_done = sem("vt_done")
        sa_done, max_done = sem("sa_done"), sem("max_done")
        mneg_done, mrow_ps, mrow_done = sem("mneg_done"), sem("mrow_ps"), sem("mrow_done")
        sb_done, exp_done, pv_done = sem("sb_done"), sem("exp_done"), sem("pv_done")
        addp_done, addd_done, den_done = sem("addp_done"), sem("addd_done"), sem("den_done")
        rden_done, spread_done, accs_done = sem("rden_done"), sem("spread_done"), sem("accs_done")
        att_done, res_done = sem("att_done"), sem("res_done")
        stored = sem("stored")
        block = ctx.enter_context(nc.Block())

        PREP = NCH + GV
        AHEAD = PREP - NCH
        HALF = KT // 2

        @block.sync
        def _(e):
            e.dma_start(wqk[:], w["wqk"]).then_inc(w_loaded, 16)
            e.dma_start(wv[:], w["wv"]).then_inc(w_loaded, 16)
            e.dma_start(al[:], w["al"]).then_inc(w_loaded, 16)
            e.dma_start(ident[:], w["ident"]).then_inc(w_loaded, 16)
            e.sem_inc(stored, 1)
            xin_v = x_in.rearrange("i c (u j n) -> j i c u n", u=NU, j=2)
            xout_v = x_out.rearrange("i c (u j n) -> j i c u n", u=NU, j=2)

            def load_xa(im):
                e.dma_start(xa[0:C, :], x_in[bass.ds(im, 1)].rearrange("a c n -> (a c) n")).then_inc(xa_loaded, 16)

            def load_xr(im):
                for j in range(2):
                    e.dma_start(xr[64 * j:64 * j + 64], xin_v[j][bass.ds(im, 1)].rearrange("i c u n -> (i c) u n"))\
                        .then_inc(xr_loaded, 16)

            def store(im, u):
                e.wait_ge(res_done, im * NU + u + 1)
                for j in range(2):
                    e.dma_start(xout_v[j][bass.ds(im, 1), :, bass.ds(u, 1)].rearrange("i c u n -> (i c) (u n)"),
                                res[64 * j:64 * j + 64]).then_inc(stored, 16)

            load_xa(0)
            load_xr(0)
            with e.Fori(0, NI - 1) as im:
                e.wait_ge(vt_done, im * GV + GV)
                load_xa(im + 1)
                for u in range(NU):
                    store(im, u)
                load_xr(im + 1)
            for u in range(NU):
                store(NI - 1, u)
            e.wait_ge(stored, NI * NU * 32 + 1)

        @block.gpsimd
        def _(e):
            e.sem_inc(addp_done, NP // 2)
            with e.Fori(0, NI) as im:
                for ch in range(NCH):
                    cs = slice(ch * CH, ch * CH + CH)
                    e.wait_ge(hi_done, im * NCH + ch + 1)
                    e.tensor_tensor(qs[64:96, cs], raw[64:96, ch % 2, 0], qs[64:96, cs], ALU.subtract)
                    e.tensor_tensor(ks[32:64, cs], raw[32:64, ch % 2, 1], ks[32:64, cs],
                                    ALU.subtract).then_inc(split_done, 1)
                with e.Fori(0, NU) as u:
                    g = e.snap(im * NU + u)
                    e.wait_ge(den_done, g + 1)
                    for i in range(1, HALF):
                        e.wait_ge(exp_done, g * KT + 2 * i + 1 + 2)
                        if i > 1:
                            e.wait_ge(addp_done, g * HALF + i + NP // 2)
                        e.tensor_tensor(sum_p[:], p[:, 0] if i == 1 else sum_p[:], p[:, (2 * i) % NP],
                                        ALU.add).then_inc(addp_done, 2 if i == 1 else 1)

        @block.scalar
        def _(e):
            e.sem_inc(exp_done, 2)
            e.sem_inc(mrow_done, 1)
            with e.Fori(0, NI) as im:
                def negative(ch):
                    e.wait_ge(proj_done, im * PREP + ch + 1)
                    e.activation(neg[:, ch % 2], b_ps[0:96, ch % 2], ACT.Relu, scale=-1.0).then_inc(neg_done, 1)

                negative(0)
                for ch in range(NCH):
                    if ch + 1 < NCH:
                        negative(ch + 1)
                    cs = slice(ch * CH, ch * CH + CH)
                    e.wait_ge(raw_done, im * NCH + ch + 1)
                    e.activation(qs[0:96, cs], raw[:, ch % 2, 0], ACT.Copy)
                    e.activation(ks[0:96, cs], raw[:, ch % 2, 1], ACT.Copy).then_inc(hi_done, 1)
                for gv in range(GV):
                    e.wait_ge(proj_done, im * PREP + NCH + gv + 1)
                    if gv >= 2:
                        e.wait_ge(vt_done, im * GV + gv - 1)
                    e.activation(negv[:, gv % 2], b_ps[:, gv % 2, 0], ACT.Relu, scale=-1.0).then_inc(neg_done, 1)
                def copy_out(g):
                    e.wait_ge(pv_done, g * KT + KT + NP)
                    e.wait_ge(att_done, g + 1)
                    e.activation(accs[:], acc[:], ACT.Copy).then_inc(accs_done, 1)

                def unit(g, u, pending):
                    e.wait_ge(mrow_ps, g + 1)
                    e.activation(qs[96:97, bass.ds(u * UQ, UQ)], a_ps[96:97, :, :].rearrange("p a n -> p (a n)"),
                                 ACT.Copy, scale=1.0 / MS).then_inc(mrow_done, 1)
                    if pending:
                        copy_out(g - 1)
                    for kt in range(KT):
                        e.wait_ge(sb_done, g * KT + kt + 1)
                        e.wait_ge(pv_done, g * KT + kt + 1)
                        e.wait_ge(addp_done if kt % 2 == 0 else addd_done, g * HALF + kt // 2 + 1)
                        e.activation(p[:, kt % NP], b_ps[:, kt % 2].rearrange("p a n -> p (a n)"),
                                     ACT.Exp).then_inc(exp_done, 1)

                unit(e.snap(im * NU), 0, False)
                with e.Fori(1, NU) as u:
                    unit(e.snap(im * NU + u), u, True)
                copy_out(e.snap(im * NU + NU - 1))

        @block.vector
        def _(e):
            e.memset(xa[C:128, :], 0.0).then_inc(const_done, 1)
            e.wait_ge(const_done, 1)
            e.memset(xa[C:C + 1, :], 1.0).then_inc(const_done, 1)
            e.memset(ks[96:97, :], MS).then_inc(const_done, 1)
            e.memset(ones[:], 1.0).then_inc(const_done, 1)
            e.sem_inc(addd_done, NP // 2)
            e.sem_inc(att_done, 1)
            e.wait_ge(w_loaded, 64)
            e.tensor_scalar(rest[:], al[:], -1.0, 1.0, ALU.mult, ALU.add).then_inc(const_done, 1)
            e.wait_ge(const_done, 5)

            def maximum(g, s):
                t, c = s % QT, s // QT
                e.wait_ge(sa_done, g * ASTEPS + s + 1)
                e.reduce_max(mparts[:, t, c:c + 1], a_ps[:, s % 2], AXX).then_inc(max_done, 1)

            def mneg_step(g):
                e.wait_ge(max_done, g * ASTEPS + ASTEPS + 2)
                e.reduce_max(mneg[:], mparts[:], AXX, negate=True).then_inc(mneg_done, 1)

            e.sem_inc(max_done, 2)
            with e.Fori(0, NI) as im:
                g0 = e.snap(im * NU)

                def prelu_qk(ch):
                    e.wait_ge(neg_done, im * PREP + ch + 1)
                    if ch >= 2:
                        e.wait_ge(split_done, im * NCH + ch - 1)
                    for j in range(2):
                        ins = e.scalar_tensor_tensor(raw[:, ch % 2, j], neg[:, ch % 2, j], rest[0:96, j:j + 1],
                                                     b_ps[0:96, ch % 2, j], ALU.mult, ALU.add)
                    ins.then_inc(raw_done, 1)

                def prelu_v(gv):
                    e.wait_ge(neg_done, im * PREP + NCH + gv + 1)
                    e.scalar_tensor_tensor(vt[:, 8 * gv:8 * gv + 8].rearrange("p a c -> p (a c)"), negv[:, gv % 2],
                                           rest[:, 2:3], b_ps[:, gv % 2, 0], ALU.mult, ALU.add).then_inc(vt_done, 1)

                for n in range(PREP):
                    if n >= AHEAD:
                        for s in range((n - AHEAD) * QT, (n - AHEAD + 1) * QT):
                            maximum(g0, s)
                    if n < NCH:
                        prelu_qk(n)
                    else:
                        prelu_v(n - NCH)
                mneg_step(g0)

                def reciprocals(g):
                    e.wait_ge(den_done, g + 2)
                    e.reciprocal(rden[:], den[:, 0:QT]).then_inc(rden_done, 1)

                def divide(g, u):
                    e.wait_ge(spread_done, g + 1)
                    e.wait_ge(accs_done, g + 2)
                    e.tensor_tensor(att[:], accs[:], den[:], ALU.mult).then_inc(att_done, 1)
                    e.wait_ge(att_done, g + 2)
                    e.wait_ge(xr_loaded, im * 32 + 32)
                    e.wait_ge(stored, g * 32 + 1)
                    e.tensor_tensor(res[:], att[:], xr[:, bass.ds(u, 1)].rearrange("p a n -> p (a n)"),
                                    ALU.add).then_inc(res_done, 1)

                def unit(g, u, more, pending):
                    for kt in range(KT):
                        if more:
                            for s in range(2 * kt, 2 * kt + 2):
                                maximum(g + 1, s)
                            if kt == KT - 1:
                                mneg_step(g + 1)
                        if pending and kt == 2:
                            reciprocals(g - 1)
                        if pending and kt == 4:
                            divide(g - 1, u - 1)
                        if kt % 2 and kt > 1:
                            e.wait_ge(exp_done, g * KT + kt + 1 + 2)
                            if kt > 3:
                                e.wait_ge(addd_done, g * HALF + kt // 2 + NP // 2)
                            e.tensor_tensor(sum_d[:], p[:, 1] if kt == 3 else sum_d[:], p[:, kt % NP],
                                            ALU.add).then_inc(addd_done, 2 if kt == 3 else 1)

                unit(g0, 0, True, False)
                with e.Fori(1, NU - 1) as u:
                    unit(e.snap(im * NU + u), u, True, True)
                last = e.snap(im * NU + NU - 1)
                unit(last, NU - 1, False, True)
                reciprocals(last)
                divide(last, NU - 1)

        @block.tensor
        def _(e):
            e.sem_inc(pv_done, NP)
            e.sem_inc(den_done, 1)
            e.sem_inc(accs_done, 1)
            e.wait_ge(w_loaded, 64)
            e.wait_ge(const_done, 4)

            def pass_a(g, u, s):
                t, c = s % QT, s // QT
                e.wait_ge(max_done, g * ASTEPS + s + 1)
                e.matmul(a_ps[:, s % 2], qs[0:96, bass.ds(u * UQ + t * 128, 128)],
                         ks[0:96, c * CH:c * CH + CH], start=True, stop=True).then_inc(sa_done, 1)

            def max_row(g):
                e.wait_ge(mneg_done, g + 1)
                for t in range(QT):
                    ins = e.matmul(a_ps[96:97, t // 4, (t % 4) * 128:(t % 4) * 128 + 128], mneg[:, t:t + 1],
                                   ident[:], start=True, stop=True)
                ins.then_inc(mrow_ps, 1)

            with e.Fori(0, NI) as im:
                e.wait_ge(xa_loaded, im * 16 + 16)
                e.wait_ge(exp_done, im * (NU * KT) + 2)
                g0 = e.snap(im * NU)

                def project_qk(ch):
                    if ch >= 2:
                        e.wait_ge(raw_done, im * NCH + ch - 1)
                    for j in range(2):
                        ins = e.matmul(b_ps[0:96, ch % 2, j], wqk[:, j], xa[:, ch * CH:ch * CH + CH],
                                       start=True, stop=True)
                    ins.then_inc(proj_done, 1)

                def project_v(gv):
                    if gv >= 2:
                        e.wait_ge(vt_done, im * GV + gv - 1)
                    else:
                        e.wait_ge(raw_done, im * NCH + NCH - 1 + gv)
                    for i in range(8):
                        t = gv * 8 + i
                        ins = e.matmul(b_ps[:, gv % 2, 0, i * C:i * C + C], xa[:, t * 128:t * 128 + 128],
                                       wv[:], start=True, stop=True)
                    ins.then_inc(proj_done, 1)

                for n in range(PREP):
                    if n < NCH:
                        project_qk(n)
                    else:
                        project_v(n - NCH)
                    if n >= AHEAD:
                        e.wait_ge(split_done, im * NCH + max(n - AHEAD, 1) + 1)
                        for s in range((n - AHEAD) * QT, (n - AHEAD + 1) * QT):
                            pass_a(g0, 0, s)
                e.wait_ge(vt_done, im * GV + GV)
                max_row(g0)

                def pv(g, kt):
                    e.wait_ge(exp_done, g * KT + kt + 1 + 2)
                    for j in range(2):
                        ins = e.matmul(acc[64 * j:64 * j + 64, :], vt[:, kt], p[:, kt % NP, j * CH:j * CH + CH],
                                       start=kt == 0, stop=kt == KT - 1)
                    ins.then_inc(pv_done, 1)

                def sums(g):
                    e.wait_ge(addp_done, g * HALF + HALF + NP // 2)
                    e.wait_ge(addd_done, g * HALF + HALF + NP // 2)
                    e.wait_ge(att_done, g + 1)
                    for t in range(QT):
                        for k, part in enumerate((sum_d, sum_p)):
                            ins = e.matmul(den[:, t:t + 1], part[:, t * 128:t * 128 + 128], ones[:, 0:1],
                                           start=k == 0, stop=k == 1)
                    ins.then_inc(den_done, 1)

                def spread(g):
                    e.wait_ge(rden_done, g + 1)
                    for t in range(QT):
                        j = t // (QT // 2)
                        ins = e.matmul(den[64 * j:64 * j + 64, (t % 4) * 128:(t % 4) * 128 + 128],
                                       rden[:, t:t + 1].broadcast_to([128, 64]), ident[:], start=True, stop=True)
                    ins.then_inc(spread_done, 1)

                def unit(g, u, more, pending):
                    e.wait_ge(mrow_done, g + 2)
                    for kt in range(KT):
                        e.wait_ge(exp_done, g * KT + kt + 1)
                        for j in range(2):
                            ins = e.matmul(b_ps[:, kt % 2, j], ks[:, kt * 128:kt * 128 + 128],
                                           qs[:, bass.ds(u * UQ + j * CH, CH)], start=True, stop=True)
                        ins.then_inc(sb_done, 1)
                        if more:
                            for s in range(2 * kt, 2 * kt + 2):
                                pass_a(g + 1, u + 1, s)
                        if pending and kt == 2:
                            sums(g - 1)
                        if pending and kt == 4:
                            spread(g - 1)
                        if kt == 1:
                            e.wait_ge(accs_done, g + 1)
                        if kt >= 1:
                            pv(g, kt - 1)
                    if more:
                        max_row(g + 1)
                    pv(g, KT - 1)

                unit(g0, 0, True, False)
                with e.Fori(1, NU - 1) as u:
                    unit(e.snap(im * NU + u), u, True, True)
                last = e.snap(im * NU + NU - 1)
                unit(last, NU - 1, False, True)
                sums(last)
                spread(last)


def _attention1(nc, keep, x_in, w, x_out):
    NPART = 8
    NS = 4
    PW = NT // NPART
    NP = 4
    LAG = 2
    with ExitStack() as ctx:
        sb = lambda n, s, d=F32: ctx.enter_context(nc.sbuf_tensor("a1_" + n, s, d))
        sem = lambda n: keep.enter_context(nc.semaphore("a1_" + n))
        xa = sb("xa", [128, NT])
        xr = sb("xr", [128, NT // 2])
        wqk = sb("wqk", [128, 2, 128])
        wv = sb("wv", [128, C])
        raw = sb("raw", [128, 2, 2, CH])
        qs = sb("qs", [128, NT], F16)
        ks = sb("ks", [128, NT], F16)
        v = sb("v", [128, KT, C])
        p = sb("p", [128, NP, NT])
        nm = sb("nm", [128, NP, NPART])
        nrow = sb("nrow", [128, NP])
        z = sb("z", [128, NP, NPART])
        f = sb("f", [128, NP, NPART])
        fz = sb("fz", [128, NP, NPART])
        fz4 = sb("fz4", [128, NP, NPART // 2])
        fz2 = sb("fz2", [128, NP, NPART // 4])
        zrow = sb("zrow", [128, NP])
        rz = sb("rz", [128, NP])
        minus_one = sb("minus_one", [128, 1])
        gain = sb("gain", [128, NP, NPART])
        vs = sb("vs", [128, NP, NPART, C])
        res = sb("res", [128, NT // 2])
        acc = ctx.enter_context(nc.psum_tensor("a1_acc", [128, 4, CH], F32))
        s_ps = ctx.enter_context(nc.psum_tensor("a1_s_ps", [128, 2, 2, CH], F32))

        w_loaded = sem("w_loaded")
        xa_loaded, xr_loaded, ones_done = sem("xa_loaded"), sem("xr_loaded"), sem("ones_done")
        proj_done, raw_done, hi_done, split_done = sem("proj_done"), sem("raw_done"), sem("hi_done"), sem("split_done")
        vproj_done, v_done = sem("vproj_done"), sem("v_done")
        s_done, nm_done, exp_done = sem("s_done"), sem("nm_done"), sem("exp_done")
        nrow_done, f_done, vs_done = sem("nrow_done"), sem("f_done"), sem("vs_done")
        pv_done, res_done, stored = sem("pv_done"), sem("res_done"), sem("stored")
        lowq_done = sem("lowq_done")
        passed = sem("passed")
        block = ctx.enter_context(nc.Block())
        GV = KT // 8
        NSPLIT = 2 * NCH
        VSTEPS = 7

        @block.sync
        def _(e):
            xin_v = x_in.rearrange("i c (h n) -> h i c n", h=2)
            xout_v = x_out.rearrange("i c (h n) -> h i c n", h=2)
            e.sem_inc(stored, 1)

            def load_xa(im):
                e.dma_start(xa[0:C, :], x_in[bass.ds(im, 1)].rearrange("a c n -> (a c) n")).then_inc(xa_loaded, 16)

            def load_xr(im):
                for h in range(2):
                    e.dma_start(xr[64 * h:64 * h + 64], xin_v[h][bass.ds(im, 1)].rearrange("i c n -> (i c) n"))\
                        .then_inc(xr_loaded, 16)

            def store(im):
                e.wait_ge(res_done, im * 4 + 4 + 4)
                for h in range(2):
                    e.dma_start(xout_v[h][bass.ds(im, 1)].rearrange("i c n -> (i c) n"),
                                res[64 * h:64 * h + 64]).then_inc(stored, 16)

            e.dma_start(wqk[:], w["wqk1"]).then_inc(w_loaded, 16)
            e.dma_start(wv[:], w["wv1"]).then_inc(w_loaded, 16)
            load_xa(0)
            load_xr(0)
            with e.Fori(0, NI - 1) as im:
                e.wait_ge(vproj_done, im * GV + GV)
                load_xa(im + 1)
                store(im)
                load_xr(im + 1)
            store(NI - 1)
            e.wait_ge(stored, NI * 32 + 1)

        @block.gpsimd
        def _(e):
            e.wait_ge(ones_done, 3)

            def scale_v(t, slot, kt):
                def made(k, ins):
                    ins.then_inc(vs_done, 1)
                    e.wait_ge(vs_done, t * VSTEPS + k)

                e.wait_ge(f_done, t + 1)
                made(1, e.tensor_tensor(fz[:, slot], f[:, slot], z[:, slot], ALU.mult))
                made(2, e.tensor_tensor(fz4[:, slot], fz[:, slot, 0:4], fz[:, slot, 4:8], ALU.add))
                made(3, e.tensor_tensor(fz2[:, slot], fz4[:, slot, 0:2], fz4[:, slot, 2:4], ALU.add))
                made(4, e.tensor_tensor(zrow[:, slot:slot + 1], fz2[:, slot, 0:1], fz2[:, slot, 1:2], ALU.add))
                made(5, e.tensor_tensor(rz[:, slot:slot + 1], zrow[:, slot:slot + 1], minus_one[:], ALU.pow))
                made(6, e.tensor_tensor(gain[:, slot], f[:, slot], rz[:, slot:slot + 1].broadcast_to([128, NPART]),
                                        ALU.mult))
                e.wait_ge(pv_done, t + 1)
                e.tensor_tensor(vs[:, slot], v[:, bass.ds(kt, 1)].broadcast_to([128, NPART, C]),
                                gain[:, slot].unsqueeze(2).broadcast_to([128, NPART, C]), ALU.mult).then_inc(vs_done, 1)

            with e.Fori(0, NI) as im:
                for ch in range(NCH):
                    cs = slice(ch * CH, ch * CH + CH)
                    e.wait_ge(hi_done, im * NCH + ch + 1)
                    for j, r in enumerate((32, 96)):
                        e.tensor_tensor(ks[r:r + 32, cs], raw[r:r + 32, ch % 2, 1], ks[r:r + 32, cs],
                                        ALU.subtract).then_inc(split_done, 1)
                        e.wait_ge(split_done, im * NSPLIT + ch * 2 + j + 1)
                e.wait_ge(v_done, im * GV + GV)
                e.sem_inc(passed, 1)
                with e.Fori(0, KT // NP) as i:
                    t = e.snap(im * KT + i * NP)
                    for slot in range(NP):
                        scale_v(t + slot, slot, i * NP + slot)

        @block.scalar
        def _(e):
            e.sem_inc(exp_done, NS)

            def part(t, slot, c):
                e.wait_ge(nm_done, t * NPART + c + 1)
                if c == 0:
                    e.wait_ge(pv_done, t + 1)
                e.activation(p[:, slot, c * PW:c * PW + PW], s_ps[:, c % NS // 2, c % 2],
                             ACT.Exp, bias=nm[:, slot, c:c + 1], accum_out=z[:, slot, c:c + 1])\
                    .then_inc(exp_done, 1)

            def rescale(t, slot):
                e.wait_ge(nrow_done, t + 1)
                e.activation(f[:, slot], nm[:, slot], ACT.Exp, bias=nrow[:, slot:slot + 1], scale=-1.0)\
                    .then_inc(f_done, 1)

            with e.Fori(0, NI) as im:
                for ch in range(NCH):
                    cs = slice(ch * CH, ch * CH + CH)
                    e.wait_ge(raw_done, im * NCH + ch + 1)
                    e.activation(qs[:, cs], raw[:, ch % 2, 0], ACT.Copy)
                    e.activation(ks[:, cs], raw[:, ch % 2, 1], ACT.Copy).then_inc(hi_done, 1)
                with e.Fori(0, KT // NP) as i:
                    t = e.snap(im * KT + i * NP)
                    for slot in range(NP):
                        for c in range(NPART):
                            part(t + slot, slot, c)
                        rescale(t + slot, slot)

        @block.vector
        def _(e):
            e.memset(xa[C:128, :], 0.0).then_inc(ones_done, 1)
            e.wait_ge(ones_done, 1)
            e.memset(xa[C:C + 1, :], 1.0).then_inc(ones_done, 1)
            e.memset(minus_one[:], -1.0).then_inc(ones_done, 1)
            e.sem_inc(res_done, 4)

            def maxima(t, slot):
                for c in range(NPART):
                    e.wait_ge(s_done, t * NPART + c + 1)
                    e.reduce_max(nm[:, slot, c:c + 1], s_ps[:, c % NS // 2, c % 2], AXX,
                                 negate=True).then_inc(nm_done, 1)
                e.wait_ge(nm_done, t * NPART + NPART)
                e.tensor_reduce(nrow[:, slot:slot + 1], nm[:, slot], AXX, ALU.min).then_inc(nrow_done, 1)

            with e.Fori(0, NI) as im:
                def low_q(ch):
                    cs = slice(ch * CH, ch * CH + CH)
                    e.wait_ge(hi_done, im * NCH + ch + 1)
                    e.tensor_tensor(qs[64:128, cs], raw[64:128, ch % 2, 0], qs[64:128, cs], ALU.subtract)\
                        .then_inc(lowq_done, 1)

                for ch in range(NCH):
                    e.wait_ge(proj_done, im * NCH + ch + 1)
                    if ch >= 2:
                        e.wait_ge(split_done, im * NSPLIT + 2 * ch - 2)
                        e.wait_ge(lowq_done, im * NCH + ch - 1)
                    e.tensor_copy(raw[:, ch % 2], s_ps[:, ch % 2]).then_inc(raw_done, 1)
                    if ch:
                        low_q(ch - 1)
                low_q(NCH - 1)
                for gv in range(GV):
                    e.wait_ge(vproj_done, im * GV + gv + 1)
                    e.tensor_copy(v[:, 8 * gv:8 * gv + 8].rearrange("p a c -> p (a c)"), s_ps[:, gv % 2, 0])\
                        .then_inc(v_done, 1)
                with e.Fori(0, KT // NP) as i:
                    t = e.snap(im * KT + i * NP)
                    for slot in range(NP):
                        maxima(t + slot, slot)
                e.wait_ge(pv_done, im * KT + KT + NP)
                e.wait_ge(xr_loaded, im * 32 + 32)
                e.wait_ge(stored, im * 32 + 1)
                for b in range(4):
                    e.tensor_tensor(res[:, b * CH:b * CH + CH], acc[:, b], xr[:, b * CH:b * CH + CH], ALU.add)\
                        .then_inc(res_done, 1)

        @block.tensor
        def _(e):
            e.sem_inc(pv_done, NP)
            e.wait_ge(w_loaded, 32)
            e.wait_ge(ones_done, 3)

            def step(t, slot, kt, now, before, first=False, last=False):
                old = (slot - LAG) % NP
                for c in range(NPART):
                    if now:
                        e.wait_ge(exp_done, t * NPART + c + 1)
                        e.matmul(s_ps[:, c % NS // 2, c % 2], ks[:, bass.ds(kt * 128, 128)],
                                 qs[:, c * PW:c * PW + PW], start=True, stop=True).then_inc(s_done, 1)
                    if before and c % 2:
                        if c == 1:
                            e.wait_ge(vs_done, (t - LAG) * VSTEPS + VSTEPS)
                        for h in range(2):
                            n = h * 4 + c // 2
                            ins = e.matmul(acc[64 * h:64 * h + 64, c // 2], vs[:, old, n],
                                           p[:, old, n * PW:n * PW + PW], start=first, stop=last)
                        if c == NPART - 1:
                            ins.then_inc(pv_done, 1)

            with e.Fori(0, NI) as im:
                e.wait_ge(xa_loaded, im * 16 + 16)
                e.wait_ge(exp_done, im * (KT * NPART) + NS)
                for ch in range(NCH):
                    if ch >= 2:
                        e.wait_ge(raw_done, im * NCH + ch - 1)
                    for j in range(2):
                        ins = e.matmul(s_ps[:, ch % 2, j], wqk[:, j], xa[:, ch * CH:ch * CH + CH],
                                       start=True, stop=True)
                    ins.then_inc(proj_done, 1)
                for gv in range(GV):
                    if gv >= 2:
                        e.wait_ge(v_done, im * GV + gv - 1)
                    else:
                        e.wait_ge(raw_done, im * NCH + NCH - 1 + gv)
                    for i in range(8):
                        t = gv * 8 + i
                        ins = e.matmul(s_ps[:, gv % 2, 0, i * C:i * C + C], xa[:, t * 128:t * 128 + 128],
                                       wv[:], start=True, stop=True)
                    ins.then_inc(vproj_done, 1)
                e.wait_ge(split_done, im * NSPLIT + NSPLIT)
                e.wait_ge(lowq_done, im * NCH + NCH)
                e.wait_ge(v_done, im * GV + GV)
                e.wait_ge(res_done, im * 4 + 4)
                t = e.snap(im * KT)
                for slot in range(NP):
                    step(t + slot, slot, slot, True, slot >= LAG, first=slot == LAG)
                with e.Fori(1, KT // NP) as i:
                    t = e.snap(im * KT + i * NP)
                    for slot in range(NP):
                        step(t + slot, slot, i * NP + slot, True, True)
                t = e.snap(im * KT + KT)
                for slot in range(LAG):
                    step(t + slot, slot, KT + slot, False, True, last=slot == LAG - 1)


def _swin(nc, keep, name, x_in, w, x_out, shifted):
    NC = 4
    NW = 8
    NH, HD, WT = 8, 8, 64
    SCALE = HD ** -0.5
    EPS = 1e-5
    OC = 2 * (HD + 1)
    LN = ["norm1"] if shifted else ["pe", "norm1"]
    LA = len(LN)
    COL = {n: i for i, n in enumerate(["pe_g", "pe_b", "norm1_g", "norm1_b", "norm2_g", "norm2_b",
                                       "q_b", "k_b", "proj_b", "fc1_b", "fc2_b"])}
    NV = 4 if shifted else 1
    NCHUNK = NI * NC
    LATE_A, LATE_C = (3, 4) if shifted else (1,), (1,)
    with ExitStack() as ctx:
        sb = lambda n, s, d=F32: ctx.enter_context(nc.sbuf_tensor(f"{name}_{n}", s, d))
        sem = lambda n: keep.enter_context(nc.semaphore(f"{name}_{n}"))
        ps = lambda n, s: ctx.enter_context(nc.psum_tensor(f"{name}_{n}", s, F32))
        x = sb("x", [128, NC, CH])
        t = x if shifted else sb("t", [128, NC, CH])
        cols = sb("cols", [128, len(COL)])
        wqk = sb("wqk", [128, 2, 128])
        wv = sb("wv", [128, C])
        vb = sb("vb", [128, C])
        wp = sb("wp", [128, 2, C])
        w1 = sb("w1", [128, 128])
        w2 = sb("w2", [128, C])
        mean_w = sb("mean_w", [128, 128])
        half_w = sb("half_w", [128, 2])
        ident = sb("ident", [128, 128])
        hmask = sb("hmask", [128, NH])
        rel = sb("rel", [128, NH, WT])
        mask = sb("mask", [128, NV, 2, WT])
        bias = sb("bias", [128, NV, 2, NH, WT])
        minus_half = sb("minus_half", [128, 2])
        xc = sb("xc", [128, 2, CH])
        sq = sb("sq", [128, 2, CH])
        var = sb("var", [128, 2, 4, 2])
        rstd = sb("rstd", [128, 2, 4, 2])
        xn = sb("xn", [128, 2, CH])
        hw = sb("hw", [128, NW, WT])
        q = sb("q", [128, 2, NW, WT])
        k = sb("k", [128, 2, NW, WT])
        v = sb("v", [128, 2, 2, NW, 4, 2, HD + 1])
        kb = sb("kb", [128, 4, NH, WT])
        s1 = sb("s1", [128, 2, NH, WT])
        nmx = sb("nmx", [128, 2, NH])
        s2 = sb("s2", [128, 2, NH, WT])
        p = sb("p", [128, 2, NH * WT])
        pt = sb("pt", [128, 2, 4, 128])
        rz = sb("rz", [128, 2, 16])
        o = sb("o", [128, NW, C])
        ot = sb("ot", [128, 2, 8, 4, 8])
        x2 = sb("x2", [128, CH])
        h2 = sb("h2", [128, CH])
        g = sb("g", [128, 2, CH])
        xo = sb("xo", [128, 2, CH])
        lin_a = ps("lin_a", [128, 2, CH])
        lin_c = ps("lin_c", [128, CH])
        s_ps = ps("s_ps", [128, 2, CH])
        pt_ps = ps("pt_ps", [128, 2, CH])
        o_ps = ps("o_ps", [128, CH])

        w_loaded, const_done, passed = [sem(n) for n in ("w_loaded", "const_done", "passed")]
        x_loaded = [sem(f"x_loaded{c}") for c in range(NC)]
        stored = [sem(f"stored{b}") for b in range(2)]
        norm_ps, normv_done, norms_done, rs_done = [
            [sem(n + s) for s in ("_a", "_c")] for n in ("norm_ps", "normv_done", "norms_done", "rs_done")]
        qk_ps, qk_done, v_ps, v_done = [sem(n) for n in ("qk_ps", "qk_done", "v_ps", "v_done")]
        kb_done, s_done, soft_done, e_done, tp_done, pt_done, pv_done, out_done = [
            sem(n) for n in ("kb_done", "s_done", "soft_done", "e_done", "tp_done", "pt_done", "pv_done", "out_done")]
        ot_ps, ot_done, proj_ps, x2_done, fc1_ps, g_done, fc2_ps, xo_done = [
            sem(n) for n in ("ot_ps", "ot_done", "proj_ps", "x2_done", "fc1_ps", "g_done", "fc2_ps", "xo_done")]
        block = ctx.enter_context(nc.Block())

        def own_wait(e):
            e.sem_inc(passed, 1)

        col = lambda n: cols[:, COL[n]:COL[n] + 1]
        loads = [(cols, "cols"), (wqk, "wqk2"), (wv, "wv2"), (vb, "vb2"), (wp, "wp2"), (w1, "w12"), (w2, "w22"),
                 (mean_w, "mean_w"), (half_w, "half_w"), (ident, "ident"), (hmask, "hmask"), (rel, "rel"), (mask, "mask")]
        NLOAD = 16 * len(loads)
        XD = 4 if shifted else 2
        CONSTS = 4 + 2 * NV

        def iterations(e, iteration):
            iteration(-1, -1, NC - 1, "A")
            iteration(0, -1, 0, "AB")
            iteration(1, -1, 1, "ABC")
            with e.Fori(0, NI - 1) as im:
                for f in range(NC):
                    iteration(e.snap(im * NC + (f + 2)), im, (f + 2) % NC, "ABCF")
            for f, stages in enumerate(("ABCF", "BCF", "CF", "F")):
                iteration(NCHUNK - 2 + f, NI - 1, (f + 2) % NC, stages)

        def loaded(e, im, c):
            e.wait_ge(x_loaded[(c + 1) % NC], im * (16 * XD) + (((c - 2) % NC + 3) // NC + 1) * 16 * XD)

        def has_pair(stages, i):
            return ("C" if i < 0 else "A" if i >= NW else "B") in stages

        @block.sync
        def _(e):
            for dst, n in loads:
                src = w[n] if n != "mask" else w[n][:, 0:NV]
                e.dma_start(dst[:], src).then_inc(w_loaded, 16)
            for b in range(2):
                e.sem_inc(stored[b], 1)

            def pieces(dram, sbt, im, c):
                for h in range(2):
                    sh = sbt[64 * h:64 * h + 64].rearrange("p (r c) -> p r c", c=WW)
                    r0 = c * 8 + h * 32 + (SHIFT if shifted else 0)
                    rows = dram[bass.ds(im, 1), :, r0:r0 + 8].rearrange("a c r w -> (a c) r w")
                    if not shifted:
                        yield rows, sh
                    else:
                        yield rows[:, :, SHIFT:WW], sh[:, :, 0:WW - SHIFT]
                        yield rows[:, :, 0:SHIFT], sh[:, :, WW - SHIFT:WW]

            def load(im, c):
                for dram, sbt in pieces(x_in, x[:, c], im, c):
                    e.dma_start(sbt, dram).then_inc(x_loaded[c], 16)

            def store(im, c):
                e.wait_ge(xo_done, im * NC + (c + 1))
                for dram, sbt in pieces(x_out, xo[:, c % 2], im, c):
                    e.dma_start(dram, sbt).then_inc(stored[c % 2], 16)

            for c in range(NC):
                load(0, c)
            with e.Fori(0, NI - 1) as im:
                for c in range(NC):
                    e.wait_ge(x2_done, im * NC + (c + 1))
                    load(im + 1, c)
                    store(im, c)
            for c in range(NC):
                store(NI - 1, c)
            for b in range(2):
                e.wait_ge(stored[b], NCHUNK // 2 * (16 * XD) + 1)

        @block.gpsimd
        def _(e):
            e.wait_ge(w_loaded, NLOAD)
            e.wait_ge(const_done, CONSTS)

            def power(st, n):
                e.wait_ge(norms_done[st], n * 3 + 2)
                e.tensor_tensor(rstd[:, st], var[:, st], minus_half[:].unsqueeze(1).broadcast_to([128, 4, 2]), ALU.pow)\
                    .then_inc(rs_done[st], 1)

            def iteration(it, im, c, stages):
                for i in range(NW):
                    if has_pair(stages, i + 2):
                        b = (c + (i + 2) // NW) % 2
                        if i + 2 == NW:
                            e.wait_ge(qk_done, it * 2 + 4)
                        if not isinstance(it, int) or it * NW + i + 2 >= 4:
                            e.wait_ge(s_done, it * NW + (i + 1))
                        e.tensor_tensor(kb[:, (i + 2) % 4], k[:, b, (i + 2) % NW].unsqueeze(1).broadcast_to([128, NH, WT]),
                                        hmask[:].unsqueeze(2).broadcast_to([128, NH, WT]), ALU.mult)\
                            .then_inc(kb_done, 1)
                    if "A" in stages and i in (0, 3)[2 - LA:]:
                        power(0, (it + 1) * LA + (i // 3 - (2 - LA)))
                    if "C" in stages and i == 4:
                        power(1, it - 1)

            iterations(e, iteration)

        @block.scalar
        def _(e):
            e.sem_inc(e_done, 2)
            e.wait_ge(w_loaded, NLOAD)

            def squares(st, n):
                e.wait_ge(normv_done[st], n * 2 + 1)
                e.activation(sq[:, st], xc[:, st], ACT.Square).then_inc(norms_done[st], 1)

            def variance(st, n):
                e.wait_ge(norm_ps[st], n * 3 + 2)
                e.activation(var[:, st].rearrange("p a h -> p (a h)"), (lin_c[:] if st else lin_a[:, 0])[:, 0:8],
                             ACT.Copy, bias=EPS).then_inc(norms_done[st], 1)

            def scaled(st, n, which, c):
                e.wait_ge(normv_done[st], n * 2 + 2)
                out, src = h2[:], xn[:, st]
                if which == "norm1":
                    out = hw[:].rearrange("p w (r c) -> p r w c", c=8)
                    src = src.rearrange("p (r w c) -> p r w c", w=NW, c=8)
                elif which == "pe":
                    out = t[:, c]
                e.activation(out, src, ACT.Identity, scale=col(which + "_g"), bias=col(which + "_b"))\
                    .then_inc(norms_done[st], 1)

            def exponentials(it, i):
                e.wait_ge(soft_done, it * (3 * NW) + (3 * i + 3))
                e.wait_ge(tp_done, it * NW + (i + 1))
                e.activation(p[:, i % 2], s2[:, i % 2].rearrange("p h m -> p (h m)"), ACT.Exp).then_inc(e_done, 1)

            def transposed(it, i):
                e.wait_ge(tp_done, it * NW + (i + 1 + 2))
                e.wait_ge(pv_done, it * NW + (i + 1))
                e.activation(pt[:, i % 2].rearrange("p a n -> p (a n)"), pt_ps[:, i % 2], ACT.Copy).then_inc(pt_done, 1)

            def iteration(it, im, c, stages):
                ca = (c + 1) % NC
                for i in range(NW):
                    if "C" in stages:
                        j = it - 1
                        if i == 1:
                            e.wait_ge(ot_ps, j + 2)
                            e.activation(ot[:].rearrange("p h r w c -> p w (h r) c"),
                                         lin_c[:].rearrange("p (w a c) -> p w a c", w=4, c=8), ACT.Copy)\
                                .then_inc(ot_done, 1)
                        elif i == 3:
                            squares(1, j)
                        elif i == 4:
                            variance(1, j)
                        elif i == 5:
                            scaled(1, j, "norm2", None)
                        elif i == 7:
                            for h in range(2):
                                e.wait_ge(fc1_ps, it * 2 + (h - 1))
                                e.activation(g[:, h], lin_a[:, 1] if h else lin_c[:], ACT.Gelu, bias=col("fc1_b"))\
                                    .then_inc(g_done, 1)
                    if "A" in stages:
                        for l, i0 in enumerate((0, 2)[2 - LA:]):
                            n = (it + 1) * LA + l
                            if i == i0:
                                squares(0, n)
                            if i == i0 + (1 if i0 else 0):
                                variance(0, n)
                            if i == i0 + (2 if i0 else 1):
                                scaled(0, n, LN[l], ca)
                    if has_pair(stages, i + 1):
                        exponentials(it, i + 1)
                    if has_pair(stages, i):
                        transposed(it, i)

            iterations(e, iteration)

        @block.vector
        def _(e):
            e.memset(minus_half[:], -0.5).then_inc(const_done, 1)
            e.memset(v[:], 0.0).then_inc(const_done, 1)
            e.wait_ge(const_done, 2)
            for par in range(2):
                e.memset(v[64 * par:64 * par + 64].rearrange("p u h w a b d -> p (u h w a) b d")[:, :, par, HD:HD + 1],
                         1.0).then_inc(const_done, 1)
            e.wait_ge(w_loaded, NLOAD)
            for a in range(NV):
                for b in range(2):
                    e.tensor_tensor(bias[:, a, b], rel[:], mask[:, a, b:b + 1].broadcast_to([128, NH, WT]), ALU.add)\
                        .then_inc(const_done, 1)
            e.wait_ge(const_done, CONSTS)

            def centre(st, n, src):
                e.wait_ge(norm_ps[st], n * 3 + 1)
                e.tensor_tensor(xc[:, st], src, lin_c[:] if st else lin_a[:, 0], ALU.subtract).then_inc(normv_done[st], 1)

            def normal(st, n):
                e.wait_ge(norm_ps[st], n * 3 + 3)
                e.tensor_tensor(xn[:, st], xc[:, st], lin_c[:] if st else lin_a[:, 0], ALU.mult).then_inc(normv_done[st], 1)

            def softmax(it, i, c):
                n, b = it * NW + i, i % 2
                e.wait_ge(s_done, n + 3)
                e.tensor_tensor(s1[:, b], s_ps[:, b].rearrange("p (h m) -> p h m", h=NH),
                                bias[:, c if shifted else 0, i % NW // (NW - 1) if shifted else 0], ALU.add)\
                    .then_inc(soft_done, 1)
                e.wait_ge(soft_done, n * 3 + 1)
                e.reduce_max(nmx[:, b], s1[:, b], AXX, negate=True).then_inc(soft_done, 1)
                e.wait_ge(soft_done, n * 3 + 2)
                e.wait_ge(e_done, n + 1)
                e.tensor_tensor(s2[:, b], s1[:, b], nmx[:, b].unsqueeze(2).broadcast_to([128, NH, WT]), ALU.add)\
                    .then_inc(soft_done, 1)

            def outputs(it, group):
                n, b = it * 4 + group, group % 4
                e.wait_ge(pv_done, n * 2 + 4)
                if group == 0:
                    e.wait_ge(ot_ps, it + 1)
                ob = o_ps[:, (b % 2) * 8 * OC:(b % 2) * 8 * OC + 8 * OC].rearrange("p (a b d) -> p a b d", b=2, d=HD + 1)
                r = rz[:, b % 2].rearrange("p (a b) -> p a b", b=2)
                e.reciprocal(r, ob[:, :, :, HD]).then_inc(out_done, 1)
                e.wait_ge(out_done, n * 2 + 1)
                e.tensor_tensor(o[:, 2 * b:2 * b + 2].rearrange("p w (a b d) -> p (w a) b d", b=2, d=HD),
                                ob[:, :, :, 0:HD], r.unsqueeze(3).broadcast_to([128, 8, 2, HD]), ALU.mult)\
                    .then_inc(out_done, 1)

            def iteration(it, im, c, stages):
                ca = (c + 1) % NC
                src_a = [x, t][2 - LA:]
                for i in range(NW):
                    if "F" in stages and i == 0:
                        e.wait_ge(fc2_ps, it - 1)
                        e.wait_ge(stored[c % 2], im * (2 * 16 * XD) + ((c - 2) % NC // 2 * (16 * XD) + 1))
                        e.scalar_tensor_tensor(xo[:, c % 2], lin_c[:], col("fc2_b"), x2[:], ALU.add, ALU.add)\
                            .then_inc(xo_done, 1)
                    if "C" in stages:
                        j = it - 1
                        if i == 2:
                            e.wait_ge(proj_ps, it)
                            e.scalar_tensor_tensor(x2[:], lin_c[:], col("proj_b"), t[:, (c - 1) % NC], ALU.add, ALU.add)\
                                .then_inc(x2_done, 1)
                        elif i == 3:
                            centre(1, j, x2[:])
                        elif i == 5:
                            normal(1, j)
                    if "A" in stages:
                        if i == 0:
                            loaded(e, im, c)
                        for l, i0 in enumerate((0, 2)[2 - LA:]):
                            if i == i0:
                                centre(0, (it + 1) * LA + l, src_a[l][:, ca])
                            if i == i0 + (2 if i0 else 1):
                                normal(0, (it + 1) * LA + l)
                        if i == 5:
                            e.wait_ge(qk_ps, it * 2 + 3)
                            e.tensor_scalar(q[:, ca % 2].rearrange("p w n -> p (w n)"), lin_a[:, 1], col("q_b"), SCALE,
                                            ALU.add, ALU.mult).then_inc(qk_done, 1)
                            e.wait_ge(qk_ps, it * 2 + 4)
                            e.tensor_scalar(k[:, ca % 2].rearrange("p w n -> p (w n)"), lin_a[:, 0], col("k_b"), None,
                                            ALU.add).then_inc(qk_done, 1)
                        if i == 6:
                            for h in range(2):
                                e.wait_ge(v_ps, it * 2 + (h + 3))
                                for par in range(2):
                                    r = slice(64 * par, 64 * par + 64)
                                    e.tensor_tensor(
                                        v[r, ca % 2, h, :, :, par, 0:HD],
                                        lin_a[r, 1 - h].rearrange("p (w a b d) -> p w a b d", w=NW, b=2, d=HD)[:, :, :, par],
                                        vb[r].rearrange("p (a b d) -> p a b d", b=2, d=HD)[:, :, par].unsqueeze(1)
                                        .broadcast_to([64, NW, 4, HD]), ALU.add).then_inc(v_done, 1)
                    if has_pair(stages, i + 1):
                        softmax(it, i + 1, (c + (i + 1) // NW) % NC)
                    if i % 2 == 0 and has_pair(stages, i - 1):
                        outputs(it, i // 2 - 1)

            iterations(e, iteration)

        @block.tensor
        def _(e):
            e.sem_inc(s_done, 2)
            e.sem_inc(tp_done, 2)
            e.sem_inc(pv_done, 2)
            e.sem_inc(ot_ps, 1)
            e.wait_ge(w_loaded, NLOAD)
            e.wait_ge(const_done, CONSTS)

            def mean(st, src):
                e.matmul(lin_c[:] if st else lin_a[:, 0], mean_w[:], src, start=True, stop=True).then_inc(norm_ps[st], 1)

            def square_sums(st, n):
                e.wait_ge(norms_done[st], n * 3 + 1)
                bank = lin_c[:] if st else lin_a[:, 0]
                for a in range(4):
                    ins = e.matmul(bank[:, 2 * a:2 * a + 2], sq[:, st, a * 128:a * 128 + 128], half_w[:],
                                   start=True, stop=True)
                ins.then_inc(norm_ps[st], 1)

            def spread(st, n):
                e.wait_ge(rs_done[st], n + 1)
                for a in range(4):
                    for h in range(2):
                        r = slice(64 * h, 64 * h + 64)
                        bank = lin_c[r] if st else lin_a[r, 0]
                        ins = e.matmul(bank[:, a * 128:a * 128 + 128], rstd[:, st, a, h:h + 1].broadcast_to([128, 64]),
                                       ident[:], start=True, stop=True)
                ins.then_inc(norm_ps[st], 1)

            def third(it, i):
                return not isinstance(it, int) or it * NW + i >= 2

            def scores(it, i, b):
                e.wait_ge(kb_done, it * NW + (i + 1))
                if third(it, i):
                    e.wait_ge(soft_done, it * (3 * NW) + (3 * i - 5))
                own_wait(e)
                for h in range(2):
                    r = slice(64 * h, 64 * h + 64)
                    ins = e.matmul(s_ps[r, i % 2], q[r, b, i % NW], kb[r, i % 4].rearrange("p h m -> p (h m)"),
                                   start=True, stop=True)
                ins.then_inc(s_done, 1)

            def transposes(it, i):
                e.wait_ge(e_done, it * NW + (i + 1 + 2))
                if third(it, i):
                    e.wait_ge(pt_done, it * NW + (i - 1))
                for a in range(4):
                    ins = e.transpose(pt_ps[:, i % 2, a * 128:a * 128 + 128], p[:, i % 2, a * 128:a * 128 + 128],
                                      ident[:])
                ins.then_inc(tp_done, 1)

            def products(it, i, b):
                w = i % NW
                if w == 0:
                    e.wait_ge(v_done, it * 4 + 4)
                if w % 2 == 0 and (i >= 2 or not isinstance(it, int) or it > 0):
                    e.wait_ge(out_done, it * 8 + i)
                e.wait_ge(pt_done, it * NW + (i + 1))
                for a in range(4):
                    for h in range(2):
                        o0 = (w % 4) * 4 * OC + a * OC
                        ins = e.matmul(o_ps[64 * h:64 * h + 64, o0:o0 + OC], pt[:, w % 2, a, 64 * h:64 * h + 64],
                                       v[:, b, h, w, a].rearrange("p b d -> p (b d)"), start=True, stop=True)
                ins.then_inc(pv_done, 1)

            def visit_a(it, im, c, i, before):
                n, ca = (it + 1) * LA, (c + 1) % NC
                if not before:
                    if LA == 2 and i == 0:
                        square_sums(0, n)
                    return
                l = LA - 1
                if i == (0 if LA == 2 else 2):
                    loaded(e, im, c)
                    if not isinstance(it, int) or it >= 0:
                        e.wait_ge(v_done, it * 4 + 4)
                    mean(0, x[:, ca])
                elif i == 1 and LA == 2:
                    spread(0, n)
                elif i == 2:
                    e.wait_ge(norms_done[0], n * 3 + 3)
                    mean(0, t[:, ca])
                elif i == 3:
                    square_sums(0, n + l)
                elif i == 4:
                    spread(0, n + l)
                elif i == 5:
                    e.wait_ge(norms_done[0], n * 3 + 3 * LA)
                    if not isinstance(it, int) or it >= 2:
                        e.wait_ge(g_done, it * 2 - 2)
                    for j in range(2):
                        e.matmul(lin_a[:, 1 - j], wqk[:, j], hw[:].rearrange("p w n -> p (w n)"), start=True, stop=True)\
                            .then_inc(qk_ps, 1)
                elif i == 6:
                    for h in range(2):
                        e.wait_ge(qk_done, it * 2 + (h + 3))
                        own_wait(e)
                        r = slice(64 * h, 64 * h + 64)
                        for w in range(NW):
                            for par in range(2):
                                ins = e.matmul(lin_a[64 * par:64 * par + 64, 1 - h, w * C:w * C + C], hw[r, w], wv[r],
                                               start=True, stop=True)
                        ins.then_inc(v_ps, 1)

            def visit_c(it, i, last):
                j = it - 1
                if i == 1:
                    e.wait_ge(out_done, it * 8)
                    if not isinstance(it, int) or it > 1:
                        e.wait_ge(xo_done, it - 1)
                    own_wait(e)
                    for a in range(NW // 2):
                        ins = e.transpose(lin_c[:, a * 128:a * 128 + 128],
                                          o[:, 2 * a:2 * a + 2].rearrange("p w c -> p (w c)"), ident[:])
                    ins.then_inc(ot_ps, 1)
                elif i == 2:
                    e.wait_ge(ot_done, it)
                    own_wait(e)
                    for b in range(2):
                        for h in range(2):
                            ins = e.matmul(
                                lin_c[64 * h:64 * h + 64].rearrange("p (r a b c) -> p r a b c", r=8, b=2, c=8)[:, :, :, b],
                                wp[:, b], ot[:, h],
                                start=True, stop=True)
                    ins.then_inc(proj_ps, 1)
                elif i == 3:
                    e.wait_ge(x2_done, it)
                    mean(1, x2[:])
                elif i == 4:
                    square_sums(1, j)
                elif i == 5:
                    spread(1, j)
                elif i == 7:
                    e.wait_ge(norms_done[1], it * 3)
                    e.wait_ge(v_done, it * 4 + 8 if not last else NCHUNK * 4)
                    own_wait(e)
                    for h in range(2):
                        r = slice(64 * h, 64 * h + 64)
                        e.matmul(lin_a[:, 1] if h else lin_c[:], w1[r], h2[r], start=True, stop=True).then_inc(fc1_ps, 1)

            def iteration(it, im, c, stages):
                for i in range(NW):
                    if "F" in stages and i == 0:
                        for h in range(2):
                            e.wait_ge(g_done, it * 2 + (h - 3))
                            ins = e.matmul(lin_c[64 * h:64 * h + 64], w2[:], g[:, h], start=True, stop=True)
                        ins.then_inc(fc2_ps, 1)
                    if "C" in stages and i not in LATE_C:
                        visit_c(it, i, "A" not in stages)
                    if "A" in stages and i not in LATE_A:
                        visit_a(it, im, c, i, True)
                    if has_pair(stages, i + 1):
                        scores(it, i + 1, (c + (i + 1) // NW) % 2)
                    if "C" in stages and i in LATE_C:
                        visit_c(it, i, "A" not in stages)
                    if "A" in stages and i in LATE_A:
                        visit_a(it, im, c, i, True)
                    if has_pair(stages, i):
                        transposes(it, i)
                    if has_pair(stages, i - 1):
                        products(it, i - 1, (c - (i == 0)) % 2)
                    if "A" in stages:
                        visit_a(it, im, c, i, False)

            iterations(e, iteration)


def _adaptive_blur(nc, keep, x_in, w, x_out):
    TS = NT // 128
    HT = TS // 2
    ND = 5
    NB = 8
    HID = 32
    NTAP = 81
    with ExitStack() as ctx:
        sb = lambda n, s, d=F32: ctx.enter_context(nc.sbuf_tensor("bl_" + n, s, d))
        sem = lambda n: keep.enter_context(nc.semaphore("bl_" + n))
        ps = lambda n, s: ctx.enter_context(nc.psum_tensor("bl_" + n, s, F32))
        x = sb("x", [128, NT // 2])
        w1 = sb("w1", [128, HID])
        b1 = sb("b1", [HID, 1])
        w2 = sb("w2", [HID, 1])
        b2 = sb("b2", [128, 1])
        taps = sb("taps", [NTAP, 1])
        ntaps = sb("ntaps", [NTAP, 1])
        dist = sb("dist", [128, ND, 128])
        ndist = sb("ndist", [128, ND * 128])
        ident = sb("ident", [128, 128])
        fold = sb("fold", [128, 128])
        ones = sb("ones", [NTAP, 1])
        hid = sb("hid", [HID, NT])
        kc = sb("kc", [128, 4, TS])
        sc = sb("sc", [128, TS])
        s = sb("s", [128, (TS + 4) * 128])
        e81 = sb("e81", [NTAP, 2, CH])
        rzc = sb("rzc", [128, TS])
        xt = sb("xt", [128, HT, 128])
        lg = sb("lg", [128, 2, ND * 128])
        f = sb("f", [128, NB, ND * 128])
        rz = sb("rz", [128, 2, CH])
        low = sb("low", [128, 2, CH])
        enh = sb("enh", [128, NT // 2])
        cen = sb("cen", [128, NT // 2])
        sq = sb("sq", [128, NT // 2])
        out = sb("out", [128, NT // 2])
        stat = sb("stat", [128, 4])
        half = sb("half", [128, 1])
        ring = ps("ring", [128, 2, CH])
        acc = ps("acc", [128, 2, CH])
        rz_ps = ps("rz_ps", [128, 2, CH])
        small = ps("small", [128, CH])

        names = ("w_loaded", "const_done", "x_loaded", "h_ps", "h_done", "ks_ps", "kc_done", "sc_done", "sbc_ps",
                 "sbc_done", "e81_done", "z_ps", "rzc_done", "xt_ps", "xt_done", "lg_done", "f_done", "acc_done",
                 "rz_ps_done", "rz_done", "low_done", "enh_done", "sum_done", "mean_ps", "cen_done", "ssq_done",
                 "var_ps", "var_done", "rstd_done", "out_done", "stored", "passed")
        (w_loaded, const_done, x_loaded, h_ps, h_done, ks_ps, kc_done, sc_done, sbc_ps, sbc_done, e81_done, z_ps,
         rzc_done, xt_ps, xt_done, lg_done, f_done, acc_done, rz_ps_done, rz_done, low_done, enh_done, sum_done,
         mean_ps, cen_done, ssq_done, var_ps, var_done, rstd_done, out_done, stored, passed) = [sem(n) for n in names]
        block = ctx.enter_context(nc.Block())
        NG = NCH
        loads = [(w1, "b_w1"), (b1, "b_b1"), (w2, "b_w2"), (b2, "b_b2"), (taps, "b_taps"), (dist, "b_dist"),
                 (ident, "ident"), (fold, "b_fold")]
        NLOAD = 16 * len(loads)

        def at(g):
            return slice(64 * (g // 4), 64 * (g // 4) + 64), slice((g % 4) * CH, (g % 4) * CH + CH)

        def alone(e):
            e.sem_inc(passed, 1)

        @block.sync
        def _(e):
            for dst, n in loads:
                e.dma_start(dst[:], w[n]).then_inc(w_loaded, 16)
            e.sem_inc(enh_done, 1)
            e.sem_inc(stored, 1)
            with e.Fori(0, NI) as im:
                e.wait_ge(enh_done, im * NG + 1)
                for h in range(2):
                    e.dma_start(x[64 * h:64 * h + 64],
                                x_in[bass.ds(im, 1), :, h * (NT // 2):(h + 1) * (NT // 2)]
                                .rearrange("a c n -> (a c) n")).then_inc(x_loaded, 16)
                e.wait_ge(out_done, im + 1)
                for h in range(2):
                    e.dma_start(x_out[bass.ds(im, 1), :, h * (NT // 2):(h + 1) * (NT // 2)]
                                .rearrange("a c n -> (a c) n"), out[64 * h:64 * h + 64]).then_inc(stored, 16)
            e.wait_ge(stored, NI * 32 + 1)

        @block.gpsimd
        def _(e):
            e.wait_ge(const_done, 4)
            with e.Fori(0, NI) as im:
                e.wait_ge(var_done, im + 1)
                e.tensor_tensor(stat[:, 3:4], stat[:, 2:3], half[:], ALU.pow).then_inc(rstd_done, 1)

        @block.scalar
        def _(e):
            e.wait_ge(w_loaded, NLOAD)
            e.wait_ge(const_done, 6)
            with e.Fori(0, NI) as im:
                for g in range(NG):
                    e.wait_ge(h_ps, im * NG + g + 1)
                    e.activation(hid[:, g * CH:g * CH + CH], ring[0:HID, g % 2], ACT.Relu, bias=b1[:])\
                        .then_inc(h_done, 1)
                for g in range(NG):
                    e.wait_ge(sbc_ps, im * NG + g + 1)
                    if g >= 2:
                        e.wait_ge(z_ps, im * NG + g - 1)
                    e.activation(s[:, (2 * 128) + g * CH:(2 * 128) + g * CH + CH], ring[:, g % 2], ACT.Copy)\
                        .then_inc(sbc_done, 1)
                    e.activation(e81[:, g % 2], ring[0:NTAP, g % 2], ACT.Exp, scale=ntaps[:]).then_inc(e81_done, 1)

                def spread(g):
                    r, _ = at(g)
                    e.wait_ge(rz_ps_done, im * NG + g + 1)
                    if g >= 2:
                        e.wait_ge(low_done, im * NG + g - 1)
                    e.activation(rz[r, g % 2], rz_ps[r, g % 2], ACT.Copy).then_inc(rz_done, 1)

                for t in range(TS):
                    e.wait_ge(lg_done, im * TS + t + 1)
                    if t >= NB:
                        e.wait_ge(acc_done, im * TS + t - NB + 3)
                    e.activation(f[:, t % NB], lg[:, t % 2], ACT.Exp).then_inc(f_done, 1)
                    if t % 4 == 3:
                        spread(t // 4)
                e.wait_ge(cen_done, im + 1)
                e.activation(sq[:], cen[:], ACT.Square, accum_out=stat[:, 1:2]).then_inc(ssq_done, 1)

        @block.vector
        def _(e):
            e.memset(half[:], -0.5).then_inc(const_done, 1)
            e.memset(ones[:], 1.0).then_inc(const_done, 1)
            e.memset(s[:, 0:256], 0.0).then_inc(const_done, 1)
            e.memset(s[:, 256 + NT:512 + NT], 0.0).then_inc(const_done, 1)
            e.wait_ge(w_loaded, NLOAD)
            e.tensor_scalar(ntaps[:], taps[:], -1.0, None, ALU.mult).then_inc(const_done, 1)
            e.tensor_scalar(ndist[:], dist[:].rearrange("p a b -> p (a b)"), -1.0, None, ALU.mult)\
                .then_inc(const_done, 1)
            e.wait_ge(const_done, 6)
            with e.Fori(0, NI) as im:
                e.wait_ge(ks_ps, im + 1)
                steps = [
                    lambda: e.tensor_scalar(kc[:, 0], small[:, 0:TS], b2[:], 0.0, ALU.add, ALU.max),
                    lambda: e.tensor_scalar(kc[:, 1], kc[:, 0], 20.0, 1.0, ALU.mult, ALU.add),
                    lambda: e.tensor_tensor(kc[:, 2], kc[:, 1], kc[:, 1], ALU.mult),
                    lambda: e.reciprocal(kc[:, 3], kc[:, 2])]
                for n, make in enumerate(steps):
                    make().then_inc(kc_done, 1)
                    e.wait_ge(kc_done, im * 4 + n + 1)
                e.tensor_scalar(sc[:], kc[:, 3], 4.5, None, ALU.mult).then_inc(sc_done, 1)
                for g in range(4):
                    e.wait_ge(xt_ps, im * 4 + g + 1)
                    e.tensor_copy(xt[:, 4 * g:4 * g + 4].rearrange("p a b -> p (a b)"), ring[:, g % 2])\
                        .then_inc(xt_done, 1)
                e.wait_ge(z_ps, im * NG + NG)
                e.reciprocal(rzc[:], small[:, TS:2 * TS]).then_inc(rzc_done, 1)
                e.wait_ge(sbc_done, im * NG + NG)

                def enhance(g):
                    r, c = at(g)
                    e.wait_ge(rz_done, im * NG + g + 1)
                    e.wait_ge(acc_done, im * TS + 4 * g + 4)
                    e.tensor_tensor(low[r, g % 2], acc[r, g % 2], rz[r, g % 2], ALU.mult).then_inc(low_done, 1)
                    e.wait_ge(low_done, im * NG + g + 1)
                    e.tensor_tensor(enh[r, c], low[r, g % 2], x[r, c], ALU.add).then_inc(enh_done, 1)

                for t in range(TS):
                    if t >= 2:
                        e.wait_ge(f_done, im * TS + t - 1)
                    e.tensor_tensor(lg[:, t % 2], ndist[:], s[:, t * 128:t * 128 + ND * 128], ALU.mult)\
                        .then_inc(lg_done, 1)
                    if t % 4 == 3 and t > 4:
                        enhance(t // 4 - 1)
                enhance(NG - 1)
                e.wait_ge(enh_done, im * NG + NG + 1)
                e.reduce_sum(stat[:, 0:1], enh[:], AXX).then_inc(sum_done, 1)
                e.wait_ge(mean_ps, im + 1)
                e.tensor_scalar(cen[:], enh[:], small[:, 2 * TS:2 * TS + 1], None, ALU.subtract).then_inc(cen_done, 1)
                e.wait_ge(var_ps, im + 1)
                e.tensor_scalar(stat[:, 2:3], small[:, 2 * TS + 1:2 * TS + 2], 1e-5, None, ALU.add)\
                    .then_inc(var_done, 1)
                e.wait_ge(rstd_done, im + 1)
                e.wait_ge(stored, im * 32 + 1)
                e.tensor_scalar(out[:], cen[:], stat[:, 3:4], None, ALU.mult).then_inc(out_done, 1)

        @block.tensor
        def _(e):
            e.wait_ge(w_loaded, NLOAD)
            e.wait_ge(const_done, 6)
            with e.Fori(0, NI) as im:
                e.wait_ge(x_loaded, im * 32 + 32)
                alone(e)
                for g in range(NG):
                    r, c = at(g)
                    if g >= 2:
                        e.wait_ge(h_done, im * NG + g - 1)
                        alone(e)
                    e.matmul(ring[0:HID, g % 2], w1[r], x[r, c], start=True, stop=True).then_inc(h_ps, 1)
                e.wait_ge(h_done, im * NG + NG)
                alone(e)
                for t in range(TS):
                    ins = e.matmul(small[:, t:t + 1], hid[:, t * 128:t * 128 + 128], w2[:], start=True, stop=True)
                ins.then_inc(ks_ps, 1)
                for g in range(4):
                    if g >= 2:
                        e.wait_ge(xt_done, im * 4 + g - 1)
                        alone(e)
                    for t in range(4 * g, 4 * g + 4):
                        ins = e.transpose(ring[:, g % 2, (t % 4) * 128:(t % 4) * 128 + 128],
                                          x[:, t * 128:t * 128 + 128], ident[:])
                    ins.then_inc(xt_ps, 1)

                def sums(g):
                    e.wait_ge(e81_done, im * NG + g + 1)
                    alone(e)
                    for t in range(4 * g, 4 * g + 4):
                        ins = e.matmul(small[:, TS + t:TS + t + 1], e81[:, g % 2, (t % 4) * 128:(t % 4) * 128 + 128],
                                       ones[:], start=True, stop=True)
                    ins.then_inc(z_ps, 1)

                e.wait_ge(sc_done, im + 1)
                e.wait_ge(xt_done, im * 4 + 4)
                for g in range(NG):
                    if g >= 2:
                        sums(g - 2)
                    for t in range(4 * g, 4 * g + 4):
                        ins = e.matmul(ring[:, g % 2, (t % 4) * 128:(t % 4) * 128 + 128],
                                       sc[:, t:t + 1].broadcast_to([128, 128]), ident[:], start=True, stop=True)
                    ins.then_inc(sbc_ps, 1)
                sums(NG - 2)
                sums(NG - 1)
                e.wait_ge(rzc_done, im + 1)
                alone(e)

                def spread(g):
                    r, _ = at(g)
                    if g >= 2:
                        e.wait_ge(rz_done, im * NG + g - 1)
                        alone(e)
                    for t in range(4 * g, 4 * g + 4):
                        ins = e.matmul(rz_ps[r, g % 2, (t % 4) * 128:(t % 4) * 128 + 128],
                                       rzc[:, t:t + 1].broadcast_to([128, C]), ident[:], start=True, stop=True)
                    ins.then_inc(rz_ps_done, 1)

                for t in range(TS):
                    g = t // 4
                    r, _ = at(g)
                    if t % 4 == 0:
                        spread(g)
                        if g >= 2:
                            e.wait_ge(low_done, im * NG + g - 1)
                    e.wait_ge(f_done, im * TS + min(t + 3, TS))
                    alone(e)
                    reach = [q for q in range(t - 2, t + 3) if 0 <= q < TS]
                    for q in reach:
                        ins = e.matmul(acc[r, g % 2, (t % 4) * 128:(t % 4) * 128 + 128],
                                       xt[:, q % HT, 64 * (q // HT):64 * (q // HT) + 64],
                                       f[:, q % NB, (t - q + 2) * 128:(t - q + 2) * 128 + 128],
                                       start=q == reach[0], stop=q == reach[-1])
                    ins.then_inc(acc_done, 1)
                e.wait_ge(sum_done, im + 1)
                alone(e)
                e.matmul(small[:, 2 * TS:2 * TS + 1], fold[:], stat[:, 0:1], start=True, stop=True).then_inc(mean_ps, 1)
                e.wait_ge(ssq_done, im + 1)
                alone(e)
                e.matmul(small[:, 2 * TS + 1:2 * TS + 2], fold[:], stat[:, 1:2], start=True, stop=True)\
                    .then_inc(var_ps, 1)


def _copy_rows(nc, keep, name, rows_from, rows_to):
    done = keep.enter_context(nc.semaphore(name))
    with nc.Block() as block:
        @block.sync
        def _(e):
            e.dma_start(rows_to, rows_from).then_inc(done, 16)
            e.wait_ge(done, 16)


def conv_attention_swin_blur(nc, x, wt, out):
    S = SHIFT
    scratch = lambda n, shape: nc.dram_tensor(n, shape, F32, kind="Internal").ap()
    x1 = scratch("after_attention0", (NI, C, NT))
    x2 = scratch("after_attention1", (NI, C, HH, WW))
    x3 = scratch("after_swin", (NI, C, HH + S, WW))
    x4 = scratch("after_shifted_swin", (NI, C, HH + S, WW))
    pixels = lambda a: a.rearrange("i c h w -> i c (h w)")
    with ExitStack() as keep:
        _attention0(nc, keep, pixels(x), wt, x1)
        _attention1(nc, keep, x1, wt, pixels(x2))
        _swin(nc, keep, "w0", x2, {**wt, **{n: wt[n + "_0"] for n in SWIN_WEIGHTS}}, x3, False)
        _copy_rows(nc, keep, "x3_rows", x3[:, :, 0:S], x3[:, :, HH:HH + S])
        _swin(nc, keep, "w1", x3, {**wt, **{n: wt[n + "_1"] for n in SWIN_WEIGHTS}}, x4, True)
        _copy_rows(nc, keep, "x4_rows", x4[:, :, HH:HH + S], x4[:, :, 0:S])
        _adaptive_blur(nc, keep, x4[:, :, 0:HH].rearrange("i c h w -> i c (h w)"), wt, pixels(out))


SWIN_WEIGHTS = ("cols", "wqk2", "wv2", "vb2", "wp2", "w12", "w22", "rel")


def _layouts(inputs):
    import numpy as np
    f32 = np.float32
    with_bias = lambda m, b: np.concatenate([m.T, b[None], np.zeros((128 - C - 1, len(b)), f32)], 0)
    twice = lambda m: np.concatenate([m, m])

    def blocks(m):
        z = np.zeros_like(m)
        return np.block([[m, z], [z, m]])

    def four(m, b):
        a = np.zeros((128, 4, 32), f32)
        a[:, :, 0:8] = with_bias(m, b)[:, None]
        return a.reshape(128, 128)

    a = {}
    g = lambda n: np.asarray(inputs["L0_conv_" + n])
    a["wqk"] = np.stack([np.tile(with_bias(g("w" + n), g("b" + n)), (1, 3)) for n in "12"], 1)
    a["wv"] = with_bias(g("w3"), g("b3"))
    a["al"] = np.tile(np.concatenate([g("a1"), g("a2"), g("a3")])[None], (128, 1))
    g = lambda n: np.asarray(inputs["L1_conv_" + n])
    a["wqk1"] = np.stack([four(g("Wq"), g("bq")), four(g("Wk"), g("bk"))], 1)
    a["wv1"] = with_bias(g("Wv"), g("bv"))

    g = lambda n: np.asarray(inputs["L2_conv_" + n])
    at = np.stack(np.meshgrid(np.arange(8), np.arange(8), indexing="ij")).reshape(2, -1)
    dy, dx = at[:, :, None] - at[:, None, :] + 7
    for b in range(2):
        qw, qb = g("qkv_w")[b], g("qkv_b")[b]
        norms = [g("pe_g"), g("pe_b"), g("norm1_g")[b], g("norm1_b")[b], g("norm2_g")[b], g("norm2_b")[b]]
        a[f"cols_{b}"] = np.stack([twice(v) for v in norms + [qb[0:C], qb[C:2 * C], g("proj_b")[b]]]
                                  + [g("fc1_b")[b], twice(g("fc2_b")[b])], 1)
        a[f"wqk2_{b}"] = np.stack([blocks(qw[:, 0:C]), blocks(qw[:, C:2 * C])], 1)
        a[f"wv2_{b}"] = twice(qw[:, 2 * C:])
        a[f"vb2_{b}"] = np.tile(qb[2 * C:], (128, 1))
        a[f"wp2_{b}"] = blocks(g("proj_w")[b]).reshape(128, 2, C)
        a[f"w12_{b}"] = twice(g("fc1_w")[b])
        a[f"w22_{b}"] = g("fc2_w")[b]
        a[f"rel_{b}"] = np.tile(g("rpb")[b][dy * 15 + dx].transpose(0, 2, 1), (2, 1, 1))
    region = np.zeros((HH, WW))
    edges = (slice(0, -8), slice(-8, -4), slice(-4, None))
    for i, rows in enumerate(edges):
        for j, columns in enumerate(edges):
            region[rows, columns] = 3 * i + j
    region = region.reshape(8, 8, 8, 8).transpose(0, 2, 1, 3).reshape(8, 8, 64)
    mask = np.where(region[:, :, None] != region[..., None], f32(-100), f32(0))
    a["mask"] = mask.reshape(2, 4, 8, 64, 64)[:, :, [0, 7]].transpose(0, 3, 1, 2, 4).reshape(128, 4, 2, 64)
    a["mean_w"] = blocks(np.full((64, 64), 1 / 64, f32))
    a["half_w"] = a["mean_w"][:, [0, 64]]
    a["hmask"] = twice((np.arange(C)[:, None] // 8 == np.arange(8)).astype(f32))
    a["ident"] = np.eye(128, dtype=f32)

    g = lambda n: np.asarray(inputs["L3_conv_" + n])
    q, p = np.arange(128)[:, None], np.arange(128)[None]
    dist = np.full((128, 5, 128), 1e30, f32)
    for d in range(5):
        u, v = q // 64 - p // 64 - 2 * (d - 2) + 4, q % 64 - p % 64 + 4
        near = (u >= 0) & (u < 9) & (v >= 0) & (v < 9)
        dist[:, d][near] = g("gauss_kernel")[u[near], v[near]]
    a["b_dist"] = dist
    a["b_taps"] = g("gauss_kernel").reshape(81, 1)
    a["b_w1"], a["b_b1"], a["b_w2"] = twice(g("w1")), g("b1")[:, None], g("w2")
    a["b_b2"] = np.tile(g("b2")[None], (128, 1))
    a["b_fold"] = np.tile(np.eye(C, dtype=f32), (2, 2)) / f32(NT)
    return {n: np.ascontiguousarray(v, f32) for n, v in a.items()}


def kernel(**inputs):
    import numpy as np
    import concourse.bacc as bacc
    from concourse.bass_utils import run_bass_kernel_spmd

    nc = bacc.Bacc("TRN2", target_bir_lowering=False, num_devices=1)
    arrays = {"x": np.ascontiguousarray(inputs["x"]), **_layouts(inputs)}
    aps = {n: nc.dram_tensor(n, a.shape, mybir.dt.from_np(a.dtype), kind="ExternalInput").ap()
           for n, a in arrays.items()}
    out = nc.dram_tensor("out", (NI, C, HH, WW), F32, kind="ExternalOutput").ap()
    conv_attention_swin_blur(nc, aps.pop("x"), aps, out)
    r = run_bass_kernel_spmd(nc, [arrays], core_ids=[0])
    return r.results[0]["out"]
```
